# Optimizing a Trainium2 kernel written in Bass

```python
import numpy as np
import jax
import jax.numpy as jnp

def _softmax(x, axis=-1):
    return jax.nn.softmax(x, axis=axis)

def _gelu(x):
    return jax.nn.gelu(x, approximate=True)

def _silu(x):
    return jax.nn.silu(x)

def _sigmoid(x):
    return jax.nn.sigmoid(x)

def _layernorm(x, axis=-1, eps=1e-05):
    m = jnp.mean(x, axis=axis, keepdims=True)
    v = jnp.var(x, axis=axis, keepdims=True)
    return (x - m) / jnp.sqrt(v + eps)

def _scatter_add(tgt, idx, src, axis=0):
    return tgt.at[idx].add(src)

def _segment_sum(src, seg, n):
    return jax.ops.segment_sum(src, seg, n)
kernel_name = 'mk_gnn_ffn_d2_gnn_r8_8a050a'

def setup_inputs(seed: int=0):
    np.random.seed(seed)
    _w = jnp.asarray

    def _rec_inputs():
        import jax
        import jax.numpy as jnp
        _gk = jax.random.key(seed)
        x = -0.000364 + 1 * jax.random.normal(jax.random.fold_in(_gk, 1), (1250, 768), jnp.float32)
        src = jax.random.randint(jax.random.fold_in(_gk, 2), (40000,), 0, 1250, jnp.int32)
        dst = jax.random.randint(jax.random.fold_in(_gk, 3), (40000,), 0, 1250, jnp.int32)
        _o = jnp.argsort(dst, stable=True)
        src = src[_o]
        dst = dst[_o]
        edge_type_8 = jax.random.randint(jax.random.fold_in(_gk, 12), (40000,), 0, 8, jnp.int32)
        return (x, src, dst, edge_type_8)
    x, src, dst, edge_type_8 = _rec_inputs()

    def _L0_gnn_setup():
        import jax, jax.numpy as jnp
        import numpy as np
        N, IN, OUT, R, E = (2500, 768, 768, 8, 40000)

        def _rgcn_conv(x, src, dst, etype, W, root, b):
            num_nodes = x.shape[0]
            num_rel = W.shape[0]
            x_src = x[src]
            seg = dst * num_rel + etype
            sums = jax.ops.segment_sum(x_src, seg, num_segments=num_nodes * num_rel)
            cnt = jax.ops.segment_sum(jnp.ones((src.shape[0],), dtype=x.dtype), seg, num_segments=num_nodes * num_rel)
            mean = sums / jnp.maximum(cnt, 1.0)[:, None]
            mean = mean.reshape(num_nodes, num_rel, -1)
            out = jnp.einsum('nri,rio->no', mean, W)
            return out + x @ root + b
        key = jax.random.key(seed)
        ks = jax.random.split(key, 9)
        x = jax.random.normal(ks[0], (N, IN), dtype=jnp.float32)
        edge_index = jax.random.randint(ks[1], (2, E), 0, N, dtype=jnp.int64)
        edge_type = jax.random.randint(ks[2], (E,), 0, R, dtype=jnp.int64)
        s1 = 1.0 / np.sqrt(IN)
        s2 = 1.0 / np.sqrt(OUT)
        W1 = jax.random.normal(ks[3], (R, IN, OUT), dtype=jnp.float32) * s1
        root1 = jax.random.normal(ks[4], (IN, OUT), dtype=jnp.float32) * s1
        b1 = jnp.zeros((OUT,), dtype=jnp.float32)
        W2 = jax.random.normal(ks[5], (R, OUT, OUT), dtype=jnp.float32) * s2
        root2 = jax.random.normal(ks[6], (OUT, OUT), dtype=jnp.float32) * s2
        b2 = jnp.zeros((OUT,), dtype=jnp.float32)
        return {'x': x, 'edge_index': edge_index, 'edge_type': edge_type, 'W1': W1, 'root1': root1, 'b1': b1, 'W2': W2, 'root2': root2, 'b2': b2}
    _L0_gnn_all = _L0_gnn_setup()
    _L0_gnn_in = {k: v for k, v in _L0_gnn_all.items() if k in ('W1', 'root1', 'b1', 'W2', 'root2', 'b2')}
    del _L0_gnn_all

    def _L0_ffn_setup():
        import jax, jax.numpy as jnp
        import numpy as np
        B, T, E = (2, 1024, 768)
        H = 384
        N_EXP = 4
        key = jax.random.key(seed)
        ks = jax.random.split(key, 8)
        s_e = 1.0 / np.sqrt(E)
        s_h = 1.0 / np.sqrt(H)
        return {'x': jax.random.normal(ks[0], (B, T, E), dtype=jnp.float32), 'Wg': jax.random.uniform(ks[1], (E, N_EXP), minval=-s_e, maxval=s_e, dtype=jnp.float32), 'bg': jax.random.uniform(ks[2], (N_EXP,), minval=-s_e, maxval=s_e, dtype=jnp.float32), 'W1': jax.random.uniform(ks[3], (N_EXP, E, H), minval=-s_e, maxval=s_e, dtype=jnp.float32), 'b1': jax.random.uniform(ks[4], (N_EXP, H), minval=-s_e, maxval=s_e, dtype=jnp.float32), 'W2': jax.random.uniform(ks[5], (N_EXP, H, E), minval=-s_h, maxval=s_h, dtype=jnp.float32), 'b2': jax.random.uniform(ks[6], (N_EXP, E), minval=-s_h, maxval=s_h, dtype=jnp.float32)}
    _L0_ffn_all = _L0_ffn_setup()
    _L0_ffn_in = {k: v for k, v in _L0_ffn_all.items() if k in ('Wg', 'bg', 'W1', 'b1', 'W2', 'b2')}
    del _L0_ffn_all

    def _L1_gnn_setup():
        import jax, jax.numpy as jnp
        import numpy as np
        N_NODES = 2500
        N_EDGES = 20000
        IN_DIM = 768
        HID = 256
        HEADS = 4
        OUT_DIM = 768
        LN_EPS = 1e-05

        def _add_self_loops(edge_index, n):
            loop = jnp.arange(n, dtype=edge_index.dtype)
            return jnp.concatenate([edge_index, jnp.stack([loop, loop])], axis=1)

        def gat_conv(x, edge_index, W, a_src, a_dst, bias, heads, out_ch, concat):
            n = x.shape[0]
            ei = _add_self_loops(edge_index, n)
            src, dst = (ei[0], ei[1])
            xl = (x @ W).reshape(n, heads, out_ch)
            alpha_src = jnp.einsum('nhc,hc->nh', xl, a_src)
            alpha_dst = jnp.einsum('nhc,hc->nh', xl, a_dst)
            e = jax.nn.leaky_relu(alpha_src[src] + alpha_dst[dst], 0.2)
            m = jax.ops.segment_max(e, dst, num_segments=n)
            e = jnp.exp(e - m[dst])
            s = jax.ops.segment_sum(e, dst, num_segments=n)
            alpha = e / (s[dst] + 1e-16)
            msg = xl[src] * alpha[:, :, None]
            out = jax.ops.segment_sum(msg, dst, num_segments=n)
            out = out.reshape(n, heads * out_ch) if concat else out.mean(axis=1)
            return out + bias

        def layer_norm(x, g, b):
            mu = jnp.mean(x, axis=-1, keepdims=True)
            var = jnp.var(x, axis=-1, keepdims=True)
            return (x - mu) * jax.lax.rsqrt(var + LN_EPS) * g + b
        key = jax.random.key(seed)
        ks = jax.random.split(key, 16)
        s = 0.02
        HC = HID * HEADS
        return {'x': jax.random.normal(ks[0], (N_NODES, IN_DIM), jnp.float32), 'edge_index': jax.random.randint(ks[1], (2, N_EDGES), 0, N_NODES, jnp.int64 if jax.config.jax_enable_x64 else jnp.int32), 'W1': jax.random.normal(ks[2], (IN_DIM, HC), jnp.float32) * s, 'a_src1': jax.random.normal(ks[3], (HEADS, HID), jnp.float32) * s, 'a_dst1': jax.random.normal(ks[4], (HEADS, HID), jnp.float32) * s, 'b1': jnp.zeros((HC,), jnp.float32), 'g1': jnp.ones((HC,), jnp.float32), 'be1': jnp.zeros((HC,), jnp.float32), 'Wr1': jax.random.normal(ks[5], (IN_DIM, HC), jnp.float32) * s, 'br1': jnp.zeros((HC,), jnp.float32), 'W2': jax.random.normal(ks[6], (HC, OUT_DIM), jnp.float32) * s, 'a_src2': jax.random.normal(ks[7], (1, OUT_DIM), jnp.float32) * s, 'a_dst2': jax.random.normal(ks[8], (1, OUT_DIM), jnp.float32) * s, 'b2': jnp.zeros((OUT_DIM,), jnp.float32), 'g2': jnp.ones((OUT_DIM,), jnp.float32), 'be2': jnp.zeros((OUT_DIM,), jnp.float32), 'Wr2': jax.random.normal(ks[9], (HC, OUT_DIM), jnp.float32) * s, 'br2': jnp.zeros((OUT_DIM,), jnp.float32)}
    _L1_gnn_all = _L1_gnn_setup()
    _L1_gnn_in = {k: v for k, v in _L1_gnn_all.items() if k in ('W1', 'a_src1', 'a_dst1', 'b1', 'g1', 'be1', 'Wr1', 'br1', 'W2', 'a_src2', 'a_dst2', 'b2', 'g2', 'be2', 'Wr2', 'br2')}
    del _L1_gnn_all

    def _L1_ffn_setup():
        import jax, jax.numpy as jnp
        import numpy as np
        B_SZ, S, D = (8, 512, 768)
        H = 12
        N_EXP = 8
        RANK = 16
        ALPHA = 32
        TOP_K = 2
        key = jax.random.key(seed)
        ks = jax.random.split(key, 9)
        x = jax.random.normal(ks[0], (B_SZ, S, D), jnp.float32)
        W_qkv = jax.random.normal(ks[1], (3 * D, D), jnp.float32) * 0.02
        b_qkv = jnp.zeros((3 * D,), jnp.float32)
        W_gate = jax.random.normal(ks[2], (N_EXP, D), jnp.float32) * 0.02
        b_gate = jnp.zeros((N_EXP,), jnp.float32)
        A = jax.random.normal(ks[3], (N_EXP, RANK, D), jnp.float32) * 0.02
        B_lora = jax.random.normal(ks[4], (N_EXP, 3 * D, RANK), jnp.float32) * 0.02
        W_proj = jax.random.normal(ks[5], (D, D), jnp.float32) * 0.02
        b_proj = jnp.zeros((D,), jnp.float32)
        return {'x': x, 'W_qkv': W_qkv, 'b_qkv': b_qkv, 'W_gate': W_gate, 'b_gate': b_gate, 'A': A, 'B_lora': B_lora, 'W_proj': W_proj, 'b_proj': b_proj}
    _L1_ffn_all = _L1_ffn_setup()
    _L1_ffn_in = {k: v for k, v in _L1_ffn_all.items() if k in ('W_qkv', 'b_qkv', 'W_gate', 'b_gate', 'A', 'B_lora', 'W_proj', 'b_proj')}
    del _L1_ffn_all
    return {'x': x, 'src': src, 'dst': dst, 'edge_type_8': edge_type_8, 'L0_gnn_W1': _L0_gnn_in['W1'], 'L0_gnn_root1': _L0_gnn_in['root1'], 'L0_gnn_b1': _L0_gnn_in['b1'], 'L0_gnn_W2': _L0_gnn_in['W2'], 'L0_gnn_root2': _L0_gnn_in['root2'], 'L0_gnn_b2': _L0_gnn_in['b2'], 'L0_ffn_Wg': _L0_ffn_in['Wg'], 'L0_ffn_bg': _L0_ffn_in['bg'], 'L0_ffn_W1': _L0_ffn_in['W1'], 'L0_ffn_b1': _L0_ffn_in['b1'], 'L0_ffn_W2': _L0_ffn_in['W2'], 'L0_ffn_b2': _L0_ffn_in['b2'], 'L1_gnn_W1': _L1_gnn_in['W1'], 'L1_gnn_a_src1': _L1_gnn_in['a_src1'], 'L1_gnn_a_dst1': _L1_gnn_in['a_dst1'], 'L1_gnn_b1': _L1_gnn_in['b1'], 'L1_gnn_g1': _L1_gnn_in['g1'], 'L1_gnn_be1': _L1_gnn_in['be1'], 'L1_gnn_Wr1': _L1_gnn_in['Wr1'], 'L1_gnn_br1': _L1_gnn_in['br1'], 'L1_gnn_W2': _L1_gnn_in['W2'], 'L1_gnn_a_src2': _L1_gnn_in['a_src2'], 'L1_gnn_a_dst2': _L1_gnn_in['a_dst2'], 'L1_gnn_b2': _L1_gnn_in['b2'], 'L1_gnn_g2': _L1_gnn_in['g2'], 'L1_gnn_be2': _L1_gnn_in['be2'], 'L1_gnn_Wr2': _L1_gnn_in['Wr2'], 'L1_gnn_br2': _L1_gnn_in['br2'], 'L1_ffn_W_qkv': _L1_ffn_in['W_qkv'], 'L1_ffn_b_qkv': _L1_ffn_in['b_qkv'], 'L1_ffn_W_gate': _L1_ffn_in['W_gate'], 'L1_ffn_b_gate': _L1_ffn_in['b_gate'], 'L1_ffn_A': _L1_ffn_in['A'], 'L1_ffn_B_lora': _L1_ffn_in['B_lora'], 'L1_ffn_W_proj': _L1_ffn_in['W_proj'], 'L1_ffn_b_proj': _L1_ffn_in['b_proj']}

def reference(x, src, dst, edge_type_8, L0_gnn_W1, L0_gnn_root1, L0_gnn_b1, L0_gnn_W2, L0_gnn_root2, L0_gnn_b2, L0_ffn_Wg, L0_ffn_bg, L0_ffn_W1, L0_ffn_b1, L0_ffn_W2, L0_ffn_b2, L1_gnn_W1, L1_gnn_a_src1, L1_gnn_a_dst1, L1_gnn_b1, L1_gnn_g1, L1_gnn_be1, L1_gnn_Wr1, L1_gnn_br1, L1_gnn_W2, L1_gnn_a_src2, L1_gnn_a_dst2, L1_gnn_b2, L1_gnn_g2, L1_gnn_be2, L1_gnn_Wr2, L1_gnn_br2, L1_ffn_W_qkv, L1_ffn_b_qkv, L1_ffn_W_gate, L1_ffn_b_gate, L1_ffn_A, L1_ffn_B_lora, L1_ffn_W_proj, L1_ffn_b_proj):
    import jax
    import jax.numpy as jnp

    def _L0_gnn_ref(x, edge_index, edge_type, W1, root1, b1, W2, root2, b2):
        import jax, jax.numpy as jnp
        import numpy as np
        N, IN, OUT, R, E = (2500, 768, 768, 8, 40000)

        def _rgcn_conv(x, src, dst, etype, W, root, b):
            num_nodes = x.shape[0]
            num_rel = W.shape[0]
            x_src = x[src]
            seg = dst * num_rel + etype
            sums = jax.ops.segment_sum(x_src, seg, num_segments=num_nodes * num_rel)
            cnt = jax.ops.segment_sum(jnp.ones((src.shape[0],), dtype=x.dtype), seg, num_segments=num_nodes * num_rel)
            mean = sums / jnp.maximum(cnt, 1.0)[:, None]
            mean = mean.reshape(num_nodes, num_rel, -1)
            out = jnp.einsum('nri,rio->no', mean, W)
            return out + x @ root + b
        src, dst = (edge_index[0], edge_index[1])
        h = _rgcn_conv(x, src, dst, edge_type, W1, root1, b1)
        h = jax.nn.relu(h)
        out = _rgcn_conv(h, src, dst, edge_type, W2, root2, b2)
        return out

    def _L0_ffn_ref(x, Wg, bg, W1, b1, W2, b2):
        import jax, jax.numpy as jnp
        import numpy as np
        B, T, E = (2, 1024, 768)
        H = 384
        N_EXP = 4
        gate_logits = jnp.einsum('bte,en->btn', x, Wg) + bg
        top = jnp.argmax(gate_logits, axis=-1)
        h = jax.nn.gelu(jnp.einsum('bte,neh->nbth', x, W1) + b1[:, None, None, :], approximate=False)
        y = jnp.einsum('nbth,nhe->nbte', h, W2) + b2[:, None, None, :]
        onehot = jax.nn.one_hot(top, N_EXP, dtype=x.dtype)
        out = jnp.einsum('nbte,btn->bte', y, onehot)
        return out

    def _L1_gnn_ref(x, edge_index, W1, a_src1, a_dst1, b1, g1, be1, Wr1, br1, W2, a_src2, a_dst2, b2, g2, be2, Wr2, br2):
        import jax, jax.numpy as jnp
        import numpy as np
        N_NODES = 2500
        N_EDGES = 20000
        IN_DIM = 768
        HID = 256
        HEADS = 4
        OUT_DIM = 768
        LN_EPS = 1e-05

        def _add_self_loops(edge_index, n):
            loop = jnp.arange(n, dtype=edge_index.dtype)
            return jnp.concatenate([edge_index, jnp.stack([loop, loop])], axis=1)

        def gat_conv(x, edge_index, W, a_src, a_dst, bias, heads, out_ch, concat):
            n = x.shape[0]
            ei = _add_self_loops(edge_index, n)
            src, dst = (ei[0], ei[1])
            xl = (x @ W).reshape(n, heads, out_ch)
            alpha_src = jnp.einsum('nhc,hc->nh', xl, a_src)
            alpha_dst = jnp.einsum('nhc,hc->nh', xl, a_dst)
            e = jax.nn.leaky_relu(alpha_src[src] + alpha_dst[dst], 0.2)
            m = jax.ops.segment_max(e, dst, num_segments=n)
            e = jnp.exp(e - m[dst])
            s = jax.ops.segment_sum(e, dst, num_segments=n)
            alpha = e / (s[dst] + 1e-16)
            msg = xl[src] * alpha[:, :, None]
            out = jax.ops.segment_sum(msg, dst, num_segments=n)
            out = out.reshape(n, heads * out_ch) if concat else out.mean(axis=1)
            return out + bias

        def layer_norm(x, g, b):
            mu = jnp.mean(x, axis=-1, keepdims=True)
            var = jnp.var(x, axis=-1, keepdims=True)
            return (x - mu) * jax.lax.rsqrt(var + LN_EPS) * g + b
        h0 = x
        h = gat_conv(x, edge_index, W1, a_src1, a_dst1, b1, HEADS, HID, True)
        h = layer_norm(h, g1, be1)
        h = jax.nn.relu(h)
        h = h + (h0 @ Wr1 + br1)
        h1 = h
        h = gat_conv(h, edge_index, W2, a_src2, a_dst2, b2, 1, OUT_DIM, False)
        h = layer_norm(h, g2, be2)
        h = h + (h1 @ Wr2 + br2)
        return h

    def _L1_ffn_ref(x, W_qkv, b_qkv, W_gate, b_gate, A, B_lora, W_proj, b_proj):
        import jax, jax.numpy as jnp
        import numpy as np
        B_SZ, S, D = (8, 512, 768)
        H = 12
        N_EXP = 8
        RANK = 16
        ALPHA = 32
        TOP_K = 2
        b, s, d = x.shape
        n_exp, rank = (A.shape[0], A.shape[1])
        scaling = ALPHA / rank
        head_dim = d // H
        scale = head_dim ** (-0.5)
        t = b * s
        x_flat = x.reshape(t, d)
        qkv_base = x @ W_qkv.T + b_qkv
        logits = x_flat @ W_gate.T + b_gate
        router_probs = jax.nn.softmax(logits, axis=-1)
        top_k_weights, top_k_indices = jax.lax.top_k(router_probs, TOP_K)
        a_down = jnp.einsum('td,nrd->tnr', x_flat, A)
        expert_out = jnp.einsum('tnr,nor->tno', a_down, B_lora) * scaling
        dispatch = jnp.zeros((t, n_exp), x.dtype).at[jnp.arange(t)[:, None], top_k_indices].add(top_k_weights)
        sparse_out = jnp.einsum('tno,tn->to', expert_out, dispatch)
        qkv = qkv_base + sparse_out.reshape(b, s, 3 * d)
        qkv = qkv.reshape(b, s, 3, H, head_dim).transpose(2, 0, 3, 1, 4)
        q, k, v = (qkv[0], qkv[1], qkv[2])
        attn = jax.nn.softmax(jnp.einsum('bhqd,bhkd->bhqk', q, k) * scale, axis=-1)
        out = jnp.einsum('bhqk,bhkd->bhqd', attn, v)
        out = out.transpose(0, 2, 1, 3).reshape(b, s, d)
        return out @ W_proj.T + b_proj
    edge_index = jnp.stack([src, dst])
    x = x + _L0_gnn_ref(_layernorm(x, axis=-1), edge_index, edge_type_8, L0_gnn_W1, L0_gnn_root1, L0_gnn_b1, L0_gnn_W2, L0_gnn_root2, L0_gnn_b2)
    x = x + _L0_ffn_ref(_layernorm(x, axis=-1)[None], L0_ffn_Wg, L0_ffn_bg, L0_ffn_W1, L0_ffn_b1, L0_ffn_W2, L0_ffn_b2)[0]
    x = x + _L1_gnn_ref(_layernorm(x, axis=-1), edge_index, L1_gnn_W1, L1_gnn_a_src1, L1_gnn_a_dst1, L1_gnn_b1, L1_gnn_g1, L1_gnn_be1, L1_gnn_Wr1, L1_gnn_br1, L1_gnn_W2, L1_gnn_a_src2, L1_gnn_a_dst2, L1_gnn_b2, L1_gnn_g2, L1_gnn_be2, L1_gnn_Wr2, L1_gnn_br2)
    x = x + _L1_ffn_ref(_layernorm(x, axis=-1)[None], L1_ffn_W_qkv, L1_ffn_b_qkv, L1_ffn_W_gate, L1_ffn_b_gate, L1_ffn_A, L1_ffn_B_lora, L1_ffn_W_proj, L1_ffn_b_proj)[0]
    return x

_drawn_inputs = setup_inputs


def setup_inputs(seed=0):
    import zlib

    import numpy as np

    out = dict(_drawn_inputs(seed))
    spreads = {'L0_gnn_b1': (0.0, 0.1),
     'L0_gnn_b2': (0.0, 0.1),
     'L1_gnn_b1': (0.0, 0.1),
     'L1_gnn_g1': (1.0, 0.2),
     'L1_gnn_be1': (0.0, 0.313),
     'L1_gnn_br1': (0.0, 0.1),
     'L1_gnn_b2': (0.0, 0.1),
     'L1_gnn_g2': (1.0, 0.2),
     'L1_gnn_be2': (0.0, 0.1),
     'L1_gnn_br2': (0.0, 0.283),
     'L1_ffn_b_qkv': (0.0, 0.506),
     'L1_ffn_b_gate': (0.0, 0.8),
     'L1_ffn_b_proj': (0.0, 0.273)}
    factors = {'L0_ffn_bg': 3.742,
     'L0_ffn_b1': 8.0,
     'L0_ffn_b2': 6.415,
     'L1_gnn_a_src1': 8.0,
     'L1_gnn_a_dst1': 8.0,
     'L1_gnn_a_src2': 8.0,
     'L1_gnn_a_dst2': 8.0,
     'L1_ffn_W_gate': 8.0,
     'L1_ffn_A': 8.0,
     'L1_ffn_B_lora': 8.0}
    for name, (base, spread) in spreads.items():
        noise = np.random.default_rng([zlib.crc32(name.encode()), seed]).standard_normal(out[name].shape)
        drawn = base * np.exp(spread * noise) if base else spread * noise
        out[name] = jnp.asarray(drawn.astype(out[name].dtype))
    for name, factor in factors.items():
        out[name] = (out[name] * factor).astype(out[name].dtype)
    return out
```

```python
from contextlib import ExitStack, contextmanager

import concourse.bass as bass
from concourse import mybir

ALU = mybir.AluOpType
ACT = mybir.ActivationFunctionType
AXX = mybir.AxisListType.X
F32, F32R, F16, I32 = mybir.dt.float32, mybir.dt.float32r, mybir.dt.float16, mybir.dt.int32

P = 128
N = 1250
NT = -(-N // P)
NP = NT * P
LAST = N - (NT - 1) * P
D = 768
KB = D // P
HD = D // 2
R = 8
E = 40000
CHUNKS = [(0, 4), (4, 4), (8, 2)]
EPS = 1e-5

NODES_PER_BLOCK = 16
BLOCKS = NP // NODES_PER_BLOCK
PLANES = R + 1
COLS = PLANES * NODES_PER_BLOCK
KEYS = R * NODES_PER_BLOCK
EC = 5
GROUP = EC * P
ER = 320
EP = P * ER
ALL_GROUPS = -(-E // GROUP)
KEY = 2048
BPG = P // NODES_PER_BLOCK
assert E % ER == 0 and E // ER < P and N < KEY and ALL_GROUPS * GROUP <= EP


class Phase:

    def __init__(self, nc, name):
        self.nc, self.name, self.ctx, self.sems = nc, name, ExitStack(), []

    def __enter__(self):
        return self

    def sb(self, name, shape, dt=F32):
        return self.ctx.enter_context(self.nc.sbuf_tensor(f"{self.name}_{name}", shape, dt))

    def ps(self, name, shape, dt=F32):
        return self.ctx.enter_context(self.nc.psum_tensor(f"{self.name}_{name}", shape, dt))

    def sem(self, name):
        s = self.ctx.enter_context(self.nc.semaphore(f"{self.name}_{name}"))
        self.sems.append(s)
        return s

    def __exit__(self, *exc):
        if exc[0] is None:
            with self.nc.Block() as block:
                @block.gpsimd
                def _(pool):
                    for s in self.sems:
                        pool.sem_clear(s)
        self.ctx.close()


class Steps:

    def __init__(self, engine, sem):
        self.engine, self.sem, self.n = engine, sem, 0

    def done(self, instruction):
        instruction.then_inc(self.sem, 1)
        self.n += 1
        return self.n

    def wait(self, base=0):
        self.engine.wait_ge(self.sem, base + self.n)


def edges_phase(nc, src, dst, etype, edge_dram, starts, flag):
    rows = E // ER
    with Phase(nc, "edges") as ph:
        raw = ph.sb("raw", [P, 3, ER], I32)
        nxt = ph.sb("next", [P, ER], I32)
        fl = ph.sb("float", [P, 3, ER])
        nfl = ph.sb("nextf", [P, ER])
        rec = ph.sb("rec", [P, ER, 4])
        below = ph.sb("below", [P, BLOCKS + 2])
        junk = ph.sb("junk", [P, 2, ER])
        ones = ph.sb("ones", [P, P])
        row = ph.sb("row", [1, BLOCKS + 2])
        width = ph.sb("width", [1, BLOCKS])
        few = ph.sb("few", [1, 8])
        total = ph.ps("total", [P, BLOCKS + 2])
        loaded, zeroed, dve, summed, stored = (ph.sem(x) for x in ("loaded", "zeroed", "dve", "summed", "stored"))
        ready = ph.sem("records")
        with nc.Block() as block:
            @block.sync
            def _(sp):
                for k, a in enumerate((src, dst, etype)):
                    sp.dma_start(raw[0:rows, k, :], a.rearrange("(p n) -> p n", n=ER)).then_inc(loaded, 16)
                sp.wait_ge(zeroed, 1)
                sp.dma_start(nxt[0:rows - 1, :],
                             dst[1:1 + (rows - 1) * ER].rearrange("(p n) -> p n", n=ER)).then_inc(loaded, 16)
                sp.dma_start(nxt[rows - 1:rows, 0:ER - 1],
                             dst[1 + (rows - 1) * ER:E].rearrange("(p n) -> p n", p=1)).then_inc(loaded, 16)
                sp.wait_ge(ready, 1)
                sp.dma_start(edge_dram.rearrange("(p n) -> p n", p=P),
                             rec[:, :, :].rearrange("p n c -> p (n c)")).then_inc(stored, 16)
                sp.wait_ge(stored, 16)

            @block.vector
            def _(dve_):
                v, s = dve_, Steps(dve_, dve)
                v.memset(nxt[:, :], NP).then_inc(zeroed, 1)
                s.done(v.memset(rec[:, :, :], -1.0))
                s.done(v.memset(ones[:, :], 1.0))
                s.done(v.memset(below[:, :], 0.0))
                v.wait_ge(loaded, 80)
                s.done(v.tensor_copy(fl[0:rows, :, :], raw[0:rows, :, :]))
                s.done(v.tensor_copy(nfl[0:rows, :], nxt[0:rows, :]))
                s.wait()
                s.done(v.tensor_copy(rec[0:rows, :, 0], fl[0:rows, 0, :]))
                s.done(v.tensor_copy(rec[0:rows, :, 2], fl[0:rows, 1, :]))
                v.scalar_tensor_tensor(out=rec[0:rows, :, 1], in0=fl[0:rows, 2, :], scalar=float(KEY),
                                       in1=fl[0:rows, 1, :], op0=ALU.mult, op1=ALU.add).then_inc(ready, 1)
                for b in range(BLOCKS + 1):
                    if b >= 2:
                        v.wait_ge(dve, s.n - 1)
                    s.done(v.tensor_scalar(junk[0:rows, b % 2, :], fl[0:rows, 1, :], float(b * NODES_PER_BLOCK),
                                           0.0, ALU.is_lt, ALU.add, accum_out=below[0:rows, b:b + 1]))
                s.wait()
                s.done(v.tensor_tensor(junk[0:rows, 0, :], nfl[0:rows, :], fl[0:rows, 1, :], ALU.is_lt))
                s.wait()
                s.done(v.tensor_reduce(below[0:rows, BLOCKS + 1:BLOCKS + 2], junk[0:rows, 0, :], AXX, ALU.add))
                v.wait_ge(summed, 1)
                s.done(v.tensor_copy(row[:, :], total[0:1, :]))
                s.wait()
                s.done(v.tensor_tensor(width[:, :], row[:, 1:BLOCKS + 1], row[:, 0:BLOCKS], ALU.subtract))
                s.wait()
                s.done(v.tensor_reduce(few[:, 0:1], width[:, :], AXX, ALU.max))
                s.wait()
                s.done(v.tensor_scalar(few[:, 1:2], few[:, 0:1], float(GROUP), None, ALU.is_gt))
                s.done(v.tensor_scalar(few[:, 2:3], row[:, BLOCKS + 1:BLOCKS + 2], 0.0, None, ALU.is_gt))
                s.wait()
                s.done(v.tensor_tensor(few[:, 3:4], few[:, 1:2], few[:, 2:3], ALU.max))
                s.wait()
                s.done(v.tensor_scalar(few[:, 4:5], few[:, 3:4], -1.0, 1.0, ALU.mult, ALU.add))
                s.done(v.tensor_copy(flag[:, :], few[:, 3:4]))
                s.wait()
                s.done(v.tensor_scalar(starts[:, :], row[:, 0:BLOCKS], few[:, 4:5], None, ALU.mult))

            @block.tensor
            def _(pe):
                pe.wait_ge(dve, BLOCKS + 10)
                pe.matmul(total[:, :], ones[0:rows, :], below[0:rows, :], start=True, stop=True).then_inc(summed, 1)


def plane(r, part):
    return part * R + r if r < R else 2 * R + part


def where_flag(engine, flag, run, wanted):
    found = engine.value_load(flag[0:1, 0:1], min_val=0, max_val=1)
    with engine.If(found > 0 if wanted else found < 1):
        run()
        engine.nop()


def hot_column_row(pool, out, ids, record):
    pool.tensor_scalar(out[:, 0:KEYS], ids[:, 0:KEYS], record[:, 1:2], None, ALU.is_equal)
    return pool.tensor_scalar(out[:, KEYS:COLS], ids[:, KEYS:COLS], record[:, 2:3], None, ALU.is_equal)


def count_products(pe, acc, source, column, ones, first):
    for m in range(NT):
        pe.matmul(acc[:, m // 3, (m % 3) * COLS:(m % 3 + 1) * COLS], source[:, m * P:(m + 1) * P], column,
                  start=first and m % 3 == 0, stop=True, skip_group_check=True)
    return pe.matmul(acc[:, 3, COLS:2 * COLS], ones[:, :], column, start=False, stop=True,
                     skip_group_check=True)


def count_banks(acc):
    for bank in range(4):
        m0, m1 = 3 * bank, min(3 * bank + 3, NT)
        yield m0, m1, acc[:, bank, 0:(m1 - m0) * COLS].rearrange("p (m c) -> p m c", c=COLS)


def make_ids(pool, s, source_ids, ids, ones, step):
    s.done(pool.iota(source_ids[:, :], pattern=[[1, NP]], base=0, channel_multiplier=0,
                     allow_small_or_imprecise_dtypes=True))
    s.done(pool.iota(ids[:, 0, 0:KEYS], pattern=[[KEY, R], [1, NODES_PER_BLOCK]], base=0,
                     channel_multiplier=0, allow_small_or_imprecise_dtypes=True))
    s.done(pool.iota(ids[:, 0, KEYS:COLS], pattern=[[1, NODES_PER_BLOCK]], base=0,
                     channel_multiplier=0, allow_small_or_imprecise_dtypes=True))
    s.done(pool.memset(ones[:, :], 1.0))
    s.done(pool.memset(step[:, :], float(NODES_PER_BLOCK)))
    s.wait()


def adjacency_phase(nc, edge_dram, starts, flag, c_dram, counts):
    with Phase(nc, "adj") as ph:
        NREC, NHOT = 4, 4
        ROUND = 2 * BPG
        rec = ph.sb("rec", [P, NREC, EC, 4])
        source_ids = ph.sb("source_ids", [P, NP], F16)
        ids = ph.sb("ids", [P, 2, COLS])
        hot_source = ph.sb("hot_source", [P, NHOT, NP], F16)
        hot_column = ph.sb("hot_column", [P, NHOT, COLS], F16)
        ones = ph.sb("ones", [P, P], F16)
        step = ph.sb("step", [P, 1])
        stage = [ph.sb(f"stage{k}", [P, NT, PLANES, P], F32R) for k in range(2)]
        count = ph.sb("count", [1, 2, PLANES, P])
        seed = ph.sb("seed", [1, 16])
        acc = [ph.ps(f"acc{k}", [P, 4, 512]) for k in range(2)]
        rec_loaded = [ph.sem(f"rec{k}_loaded") for k in range(NREC)]
        pool_done, ids_made, source_made, column_made, products_done = (ph.sem(x) for x in (
            "pool_done", "ids_made", "source_made", "column_made", "products_done"))
        block_taken = ph.sem("block_taken")
        stage_stored = [ph.sem(f"stage{k}_stored") for k in range(2)]
        rounds = BLOCKS // ROUND
        assert rounds * ROUND == BLOCKS and ROUND * EC % NHOT == 0 and ROUND % NREC == 0

        with nc.Block() as block:
            @block.sync
            def _(sp):
                def run():
                    with sp.Fori(0, rounds) as g:
                        for j in range(ROUND):
                            b = g * ROUND + j
                            sp.wait_ge(source_made, b * EC + 1)
                            sp.wait_ge(column_made, b * EC + 1)
                            sp.nop(nofuse=True)
                            start = sp.value_load(starts[0:1, bass.ds(b, 1)], min_val=0, max_val=E)
                            sp.dma_start(rec[:, j % NREC, :, :].rearrange("p a b -> p (a b)"),
                                         edge_dram[bass.ds(start * 4, GROUP * 4)].rearrange("(p n) -> p n", p=P))\
                                .then_inc(rec_loaded[j % NREC], 16)
                where_flag(sp, flag, run, False)

            @block.gpsimd
            def _(pool):
                def run():
                    make_ids(pool, Steps(pool, pool_done), source_ids, ids, ones, step)
                    pool.memset(seed[:, 0:1], 0.0).then_inc(ids_made, 2)
                    pool.memset(seed[:, 1:2], 0.0).then_inc(column_made, (NREC - 1) * EC + 1)
                    with pool.Fori(0, rounds) as g:
                        for j in range(ROUND):
                            b, k = g * ROUND + j, j % 2
                            pool.wait_ge(rec_loaded[j % NREC], g * (ROUND // NREC * 16) + (j // NREC + 1) * 16)
                            pool.wait_ge(ids_made, b + 2)
                            for c in range(EC):
                                pool.wait_ge(products_done, b * EC + c + 1)
                                pool.nop(nofuse=True)
                                pool.tensor_scalar(hot_column[:, (j * EC + c) % NHOT, KEYS:COLS], ids[:, k, KEYS:COLS],
                                                   rec[:, j % NREC, c, 2:3], None, ALU.is_equal)\
                                    .then_inc(column_made, 1)
                            pool.wait_ge(column_made, b * EC + (NREC - 1) * EC + 1)
                            pool.wait_ge(source_made, b * EC + (NREC - 1) * EC + 1)
                            pool.tensor_tensor(ids[:, 1 - k, :], ids[:, k, :], step[:, :].to_broadcast([P, COLS]),
                                               ALU.add).then_inc(ids_made, 1)
                where_flag(pool, flag, run, False)

            @block.vector
            def _(v):
                def run():
                    v.memset(seed[:, 3:4], 0.0).then_inc(source_made, (NREC - 1) * EC + 1)
                    v.wait_ge(pool_done, 5)
                    with v.Fori(0, rounds) as g:
                        for j in range(ROUND):
                            b = g * ROUND + j
                            v.wait_ge(ids_made, b + 2)
                            v.wait_ge(rec_loaded[j % NREC], g * (ROUND // NREC * 16) + (j // NREC + 1) * 16)
                            for c in range(EC):
                                v.wait_ge(products_done, b * EC + c + 1)
                                v.tensor_scalar(hot_column[:, (j * EC + c) % NHOT, 0:KEYS], ids[:, j % 2, 0:KEYS],
                                                rec[:, j % NREC, c, 1:2], None, ALU.is_equal)
                                v.tensor_scalar(hot_source[:, (j * EC + c) % NHOT, :], source_ids[:, :],
                                                rec[:, j % NREC, c, 0:1], None, ALU.is_equal)\
                                    .then_inc(source_made, 1)
                where_flag(v, flag, run, False)

            @block.tensor
            def _(pe):
                def run():
                    pe.wait_ge(pool_done, 5)
                    with pe.Fori(0, rounds) as g:
                        for j in range(ROUND):
                            b = g * ROUND + j
                            pe.wait_ge(block_taken, b + 1)
                            for c in range(EC):
                                slot = (j * EC + c) % NHOT
                                pe.wait_ge(source_made, b * EC + (NREC - 1) * EC + c + 2)
                                pe.wait_ge(column_made, b * EC + (NREC - 1) * EC + c + 2)
                                count_products(pe, acc[j % 2], hot_source[:, slot, :], hot_column[:, slot, :],
                                               ones, c == 0).then_inc(products_done, 1)
                where_flag(pe, flag, run, False)

            @block.scalar
            def _(act):
                def run():
                    act.activation(seed[:, 8:9], flag[:, :].bitcast(F32), ACT.Copy).then_inc(products_done, NHOT)
                    act.activation(seed[:, 9:10], flag[:, :].bitcast(F32), ACT.Copy).then_inc(block_taken, 2)
                    for h in range(2):
                        act.activation(seed[:, 10 + h:11 + h], flag[:, :].bitcast(F32), ACT.Copy)\
                            .then_inc(stage_stored[h], (PLANES + 1) * 16)
                    with act.Fori(0, rounds) as g:
                        for j in range(ROUND):
                            b, h = g * ROUND + j, j // BPG
                            nodes = bass.ts(j % BPG, NODES_PER_BLOCK)
                            act.wait_ge(products_done, b * EC + NHOT + EC)
                            if j % BPG == 0:
                                act.wait_ge(stage_stored[h], (g + 1) * ((PLANES + 1) * 16))
                            for m0, m1, lot in count_banks(acc[j % 2]):
                                act.activation(stage[h][:, m0:m1, :, nodes],
                                               lot.rearrange("p m (r n) -> p m r n", r=PLANES), ACT.Copy)
                            act.activation(count[:, h, :, nodes],
                                           acc[j % 2][0:1, 3, COLS:2 * COLS].rearrange("p (r n) -> p r n", r=PLANES),
                                           ACT.Copy).then_inc(block_taken, 1)
                            if j % BPG == BPG - 1:
                                act.wait_ge(block_taken, b + 3)
                                to = bass.ds((g * 2 + h) * P, P)
                                for r in range(PLANES):
                                    act.dma_start(c_dram[plane(r, 0)].rearrange("(m p) d -> p m d", p=P)[:, :, to],
                                                  stage[h][:, :, r, :].bitcast(F32)).then_inc(stage_stored[h], 16)
                                act.dma_start(counts[:, to].rearrange("(a r) d -> a r d", a=1),
                                              count[:, h, :, :]).then_inc(stage_stored[h], 16)
                    for h in range(2):
                        act.wait_ge(stage_stored[h], (rounds + 1) * ((PLANES + 1) * 16))
                where_flag(act, flag, run, False)


def whole_adjacency_phase(nc, edge_dram, flag, c_dram, counts):
    with Phase(nc, "whole") as ph:
        rec = ph.sb("rec", [P, EC, 4])
        source_ids = ph.sb("source_ids", [P, NP], F16)
        ids = ph.sb("ids", [P, 1, COLS])
        source = ph.sb("source", [P, EC, NP], F16)
        column = ph.sb("column", [P, EC, COLS], F16)
        ones = ph.sb("ones", [P, P], F16)
        step = ph.sb("step", [P, 1])
        zeros = ph.sb("zeros", [P, P], F16)
        hi = ph.sb("hi", [P, NT, COLS], F32R)
        lo = ph.sb("lo", [P, NT, COLS], F32R)
        count = ph.sb("count", [1, COLS])
        seed = ph.sb("seed", [1, 16])
        acc = ph.ps("acc", [P, 4, 512])
        pool_done, loaded, source_made, column_made, group_done, begun = (ph.sem(x) for x in (
            "pool_done", "loaded", "source_made", "column_made", "group_done", "begun"))
        hi_made, lo_made, stored = (ph.sem(x) for x in ("hi_made", "lo_made", "stored"))
        STORES = 2 * PLANES + 1
        with nc.Block() as block:
            @block.sync
            def _(sp):
                def run():
                    with sp.Fori(0, BLOCKS) as b:
                        with sp.Fori(0, ALL_GROUPS) as q:
                            sp.wait_ge(group_done, b * ALL_GROUPS + q + 1)
                            sp.dma_start(rec[:, :, :].rearrange("p a b -> p (a b)"),
                                         edge_dram[bass.ds(q * (GROUP * 4), GROUP * 4)]
                                         .rearrange("(p n) -> p n", p=P)).then_inc(loaded, 16)
                        sp.wait_ge(hi_made, b + 1)
                        sp.wait_ge(lo_made, b + 1)
                        to = bass.ds(b * NODES_PER_BLOCK, NODES_PER_BLOCK)
                        for r in range(PLANES):
                            for k, part in enumerate((hi, lo)):
                                sp.dma_start(c_dram[plane(r, k)].rearrange("(m p) d -> p m d", p=P)[:, :, to],
                                             part[:, :, bass.ts(r, NODES_PER_BLOCK)].bitcast(F32)).then_inc(stored, 16)
                        sp.dma_start(counts[:, to].rearrange("(a r) d -> a r d", a=1),
                                     count[:, :].rearrange("a (r d) -> a r d", r=PLANES)).then_inc(stored, 16)
                    sp.wait_ge(stored, BLOCKS * STORES * 16)
                where_flag(sp, flag, run, True)

            @block.gpsimd
            def _(pool):
                def run():
                    make_ids(pool, Steps(pool, pool_done), source_ids, ids, ones, step)
                    pool.memset(zeros[:, :], 0.0).then_inc(group_done, 1)
                    with pool.Fori(0, BLOCKS) as b:
                        with pool.Fori(0, ALL_GROUPS) as q:
                            pool.wait_ge(loaded, (b * ALL_GROUPS + q + 1) * 16)
                            pool.nop(nofuse=True)
                            for c in range(EC):
                                hot_column_row(pool, column[:, c, :], ids[:, 0, :], rec[:, c, :])\
                                    .then_inc(column_made, 1)
                        pool.wait_ge(column_made, (b + 1) * (ALL_GROUPS * EC) + b)
                        pool.tensor_tensor(ids[:, 0, :], ids[:, 0, :], step[:, :].to_broadcast([P, COLS]),
                                           ALU.add).then_inc(column_made, 1)
                        pool.wait_ge(column_made, (b + 1) * (ALL_GROUPS * EC + 1))
                where_flag(pool, flag, run, True)

            @block.vector
            def _(v):
                def run():
                    v.wait_ge(pool_done, 5)
                    with v.Fori(0, BLOCKS) as b:
                        with v.Fori(0, ALL_GROUPS) as q:
                            v.wait_ge(loaded, (b * ALL_GROUPS + q + 1) * 16)
                            for c in range(EC):
                                v.tensor_scalar(source[:, c, :], source_ids[:, :], rec[:, c, 0:1], None,
                                                ALU.is_equal).then_inc(source_made, 1)
                        v.wait_ge(hi_made, b + 1)
                        for m0, m1, lot in count_banks(acc):
                            last = v.tensor_tensor(lo[:, m0:m1, :], lot, hi[:, m0:m1, :].bitcast(F32), ALU.subtract)
                        last.then_inc(lo_made, 1)
                where_flag(v, flag, run, True)

            @block.tensor
            def _(pe):
                def run():
                    pe.wait_ge(pool_done, 5)
                    pe.wait_ge(group_done, 1)
                    with pe.Fori(0, BLOCKS) as b:
                        pe.wait_ge(begun, b + 1)
                        for bank in range(4):
                            pe.matmul(acc[:, bank, 0:P], zeros[:, :], zeros[:, :], start=True, stop=True,
                                      skip_group_check=True)
                        with pe.Fori(0, ALL_GROUPS) as q:
                            pe.wait_ge(source_made, (b * ALL_GROUPS + q + 1) * EC)
                            pe.wait_ge(column_made, (b * ALL_GROUPS + q + 1) * EC + b)
                            for c in range(EC):
                                last = count_products(pe, acc, source[:, c, :], column[:, c, :], ones, False)
                            last.then_inc(group_done, 1)
                where_flag(pe, flag, run, True)

            @block.scalar
            def _(act):
                def run():
                    act.activation(seed[:, 8:9], flag[:, :].bitcast(F32), ACT.Copy).then_inc(begun, 1)
                    with act.Fori(0, BLOCKS) as b:
                        act.wait_ge(group_done, (b + 1) * ALL_GROUPS + 1)
                        for m0, m1, lot in count_banks(acc):
                            act.activation(hi[:, m0:m1, :], lot, ACT.Copy)
                        act.activation(count[:, :], acc[0:1, 3, COLS:2 * COLS], ACT.Copy).then_inc(hi_made, 1)
                        act.wait_ge(lo_made, b + 1)
                        act.wait_ge(stored, (b + 1) * (STORES * 16))
                        act.activation(seed[:, 9:10], flag[:, :].bitcast(F32), ACT.Copy).then_inc(begun, 1)
                where_flag(act, flag, run, True)


def inverses_phase(nc, counts, inv_dram):
    with Phase(nc, "inv") as ph:
        count = ph.sb("count", [R * NT, P])
        least = ph.sb("least", [R * NT, P])
        inverse = ph.sb("inverse", [R * NT, P])
        loaded, made, stored = ph.sem("loaded"), ph.sem("made"), ph.sem("stored")
        with nc.Block() as block:
            @block.sync
            def _(sp):
                sp.dma_start(count[:, :], counts[0:R, :].rearrange("r (t d) -> (r t) d", d=P)).then_inc(loaded, 16)
                sp.wait_ge(made, 2)
                sp.dma_start(inv_dram.rearrange("r (t d) -> (r t) d", d=P), inverse[:, :]).then_inc(stored, 16)
                sp.wait_ge(stored, 16)

            @block.vector
            def _(v):
                v.wait_ge(loaded, 16)
                v.tensor_scalar(least[:, :], count[:, :], 1.0, None, ALU.max).then_inc(made, 1)
                v.wait_ge(made, 1)
                v.reciprocal(inverse[:, :], least[:, :]).then_inc(made, 1)


def norm_phase(nc, name, x, ident, tokens=None, features=None, keep=None):
    with Phase(nc, name) as ph:
        kept = ph.sem("kept")
        stats = ph.sb("stats", [P, NT, 2, 6])
        moments = ph.sb("moments", [P, NT, 2])
        eps = ph.sb("eps", [P, 1])
        dev = ph.sb("dev", [P, NT])
        inv = ph.sb("inv", [P, NT])
        xn = ph.sb("xn", [P, 2, D])
        turned = [ph.ps(f"turned{k}", [P, 4, P]) for k in range(4)] if features else None
        v_s, dev_made, normed, turned_s, hi_made, lo_made = (ph.sem(x) for x in (
            "vector", "dev_made", "normed", "turned", "hi_made", "lo_made"))
        with nc.Block() as block:
            if keep is not None:
                @block.sync
                def _(sp):
                    sp.dma_start(keep.rearrange("(t p) d -> p t d", p=P), x[:, :, :]).then_inc(kept, 16)
                    sp.wait_ge(kept, 16)

            @block.vector
            def _(v):
                s = Steps(v, v_s)
                s.done(v.memset(eps[:, :], EPS))
                for t in range(NT):
                    for h in range(2):
                        s.done(v.bn_stats(stats[:, t, h, :], x[:, t, h * HD:(h + 1) * HD]))
                s.wait()
                for t in range(NT):
                    s.done(v.bn_aggr(moments[:, t, :], stats[:, t, :, :].rearrange("p a b -> p (a b)")))
                v.wait_ge(dev_made, 1)
                s.done(v.reciprocal(inv[:, :], dev[:, :]))
                s.wait()
                for t in range(NT + 1):
                    if t < NT:
                        if t >= 2:
                            if tokens:
                                v.wait_ge(lo_made, t - 1)
                            else:
                                v.wait_ge(turned_s, 2 * t - 2)
                        v.tensor_scalar(xn[:, t % 2, :], x[:, t, :], moments[:, t, 0:1], inv[:, t:t + 1],
                                        ALU.subtract, ALU.mult).then_inc(normed, 1)
                    if t == 0:
                        continue
                    u = t - 1
                    if tokens:
                        v.wait_ge(hi_made, t)
                        v.tensor_tensor(tokens[1][:, u, :], xn[:, u % 2, :], tokens[0][:, u, :].bitcast(F32),
                                        ALU.subtract).then_inc(lo_made, 1)
                    else:
                        for h in range(2):
                            v.wait_ge(hi_made, 2 * u + h + 1)
                            at = (slice(None), slice(3 * h, 3 * h + 3), slice(u * P, u * P + P))
                            v.tensor_tensor(features[1][at], turned[(2 * u + h) % 4][:, 0:3, :],
                                            features[0][at].bitcast(F32), ALU.subtract).then_inc(lo_made, 1)

            @block.scalar
            def _(act):
                act.wait_ge(v_s, 1 + 3 * NT)
                act.activation(dev[:, :], moments[:, :, 1], ACT.Sqrt, bias=eps[:, 0:1]).then_inc(dev_made, 1)
                for t in range(NT):
                    if tokens:
                        act.wait_ge(normed, t + 1)
                        act.activation(tokens[0][:, t, :], xn[:, t % 2, :], ACT.Copy).then_inc(hi_made, 1)
                    else:
                        for h in range(2):
                            act.wait_ge(turned_s, 2 * t + h + 1)
                            act.activation(features[0][:, 3 * h:3 * h + 3, t * P:t * P + P],
                                           turned[(2 * t + h) % 4][:, 0:3, :], ACT.Copy).then_inc(hi_made, 1)

            if features:
                @block.tensor
                def _(pe):
                    for t in range(NT):
                        pe.wait_ge(normed, t + 1)
                        for h in range(2):
                            if t >= 2:
                                pe.wait_ge(lo_made, 2 * t + h - 3)
                            for k in range(3):
                                last = pe.transpose(turned[(2 * t + h) % 4][:, k, :],
                                                    xn[:, t % 2, (3 * h + k) * P:(3 * h + k + 1) * P], ident[:, :])
                            last.then_inc(turned_s, 1)


def rgcn_phase(nc, name, x_hi, x_lo, out, w, root, c_dram, inv_dram, ident_r, flag, pool_loads):
    with Phase(nc, name) as ph:
        NC, NW, CS = len(CHUNKS), 2, 5
        CW = CHUNKS[0][1] * P
        m_hi = [ph.sb(f"m_hi{k}", [P, KB, CW], F32R) for k in range(2)]
        m_lo = [ph.sb(f"m_lo{k}", [P, KB, CW], F32R) for k in range(2)]
        w_hi, w_lo = ph.sb("w_hi", [P, KB, D], F32R), ph.sb("w_lo", [P, KB, D], F32R)
        w_raw = ph.sb("w_raw", [P, NW, D])
        counts = ph.sb("counts", [P, CS, CW], F32R)
        inv = ph.sb("inv", [P, 2, CW])
        mean = ph.sb("mean", [P, 2, CW])
        seed = ph.sb("seed", [1, 4])
        sums = [ph.ps(f"sums{k}", [P, 512]) for k in range(KB)]
        prod = [ph.ps(f"prod{k}", [P, 512]) for k in range(2)]
        counts_in = [ph.sem(f"counts{k}_in") for k in range(CS)]
        w_in, inv_in = pool_loads[0:NW], pool_loads[NW:NW + 2]
        counts_used, summed, scaled, m_hi_made, m_lo_made = (ph.sem(x) for x in (
            "counts_used", "summed", "scaled", "m_hi_made", "m_lo_made"))
        w_hi_made, w_lo_made, multiplied, added, begun = (ph.sem(x) for x in (
            "w_hi_made", "w_lo_made", "multiplied", "added", "begun"))
        SUMS, PRODS, TILES = NC * KB, 2 * NT, NC * (NT - 1)

        def half(h):
            return slice(h * HD, (h + 1) * HD)

        def relations(engine, body):
            passes = engine.value_load(flag[0:1, 0:1], min_val=0, max_val=1) + 1
            with engine.Fori(0, passes) as again:
                with engine.Fori(0, R // 2) as g:
                    for u in range(2):
                        body(g * 2 + u, again * R + g * 2 + u, u)
            return passes * R

        with nc.Block() as block:
            @block.sync
            def _(sp):
                def body(r, m, u):
                    for c, (t0, nt) in enumerate(CHUNKS):
                        for s in range(NT):
                            if s == NT - 1 - CS:
                                sp.wait_ge(summed, (m + 1) * SUMS + c * KB)
                            else:
                                sp.wait_ge(counts_used, m * TILES + c * (NT - 1) + s + (2 if s < CS else 1))
                            sp.dma_start(counts[:, s % CS, 0:nt * P].bitcast(F32),
                                         c_dram[bass.ds(m, 1), s * P:(s + 1) * P, t0 * P:(t0 + nt) * P]
                                         .rearrange("a p d -> (a p) d")).then_inc(counts_in[s % CS], 16)
                relations(sp, body)

            @block.gpsimd
            def _(pool):
                def weight_blocks(source, n):
                    for kb in range(KB):
                        pool.wait_ge(w_lo_made, n * KB + kb + 1)
                        pool.wait_ge(begun, 1)
                        pool.dma_start(w_raw[:, kb % NW, :], source(slice(kb * P, (kb + 1) * P)))\
                            .then_inc(w_in[kb % NW], 16)

                def inverse_row(r, m, c, row):
                    t0, nt = CHUNKS[c]
                    pool.wait_ge(scaled, m * SUMS + c * KB + 2 * KB)
                    pool.wait_ge(begun, 1)
                    pool.dma_start(inv[:, row, 0:nt * P],
                                   inv_dram[bass.ds(r, 1), t0 * P:(t0 + nt) * P]
                                   .rearrange("a d -> (a d)").partition_broadcast(P)).then_inc(inv_in[row], 16)

                def body(r, m, u):
                    inverse_row(r, m, 0, u)
                    inverse_row(r, m, 1, 1 - u)
                    weight_blocks(lambda at: w[bass.ds(r, 1), at, :].rearrange("a p d -> (a p) d"), m + 1)
                    inverse_row(r, m, 2, u)
                pool.memset(seed[:, 0:1], 0.0).then_inc(w_lo_made, NW)
                pool.memset(seed[:, 1:2], 0.0).then_inc(counts_used, CS)
                pool.memset(seed[:, 2:3], 0.0).then_inc(begun, 1)
                weight_blocks(lambda at: root[at, :], 0)
                relations(pool, body)

            @block.tensor
            def _(pe):
                def products_of(n, c, k):
                    t0, nt = CHUNKS[c]
                    pe.wait_ge(m_lo_made, n * SUMS + (c + 1) * KB)
                    if c == 0:
                        pe.wait_ge(w_lo_made, n * KB + KB + NW)
                    for t in range(nt):
                        at = slice(t * P, (t + 1) * P)
                        for h in range(2):
                            pe.wait_ge(added, n * PRODS + (t0 + t) * 2 + h + 1)
                            for f in range(KB):
                                for a, b in ((m_hi, w_hi), (m_hi, w_lo), (m_lo, w_hi)):
                                    last = pe.matmul(prod[h][:, 0:HD], a[k][:, f, at], b[:, f, half(h)],
                                                     start=f == 0 and b is w_hi and a is m_hi,
                                                     stop=f == KB - 1 and a is m_lo)
                            last.then_inc(multiplied, 1)

                for c, (t0, nt) in enumerate(CHUNKS):
                    if c:
                        pe.wait_ge(scaled, c * KB)
                    for f in range(KB):
                        for t in range(nt):
                            for part in (x_hi, x_lo):
                                last = pe.matmul(sums[f][:, t * P:(t + 1) * P],
                                                 part[:, t0 + t, f * P:(f + 1) * P], ident_r[:, :],
                                                 start=part is x_hi and t == 0, stop=True, skip_group_check=True)
                        last.then_inc(summed, 1)
                    if c:
                        products_of(0, c - 1, (c - 1) % 2)

                def body(r, m, u):
                    for c, (t0, nt) in enumerate(CHUNKS):
                        pe.wait_ge(scaled, m * SUMS + SUMS + c * KB)
                        for s in range(NT):
                            pe.wait_ge(counts_in[s % CS], (m * NC + c) * (NT // CS * 16) + (s // CS + 1) * 16)
                            for f in range(KB):
                                for part in (x_hi, x_lo):
                                    last = pe.matmul(sums[f][:, 0:nt * P], part[:, s, f * P:(f + 1) * P],
                                                     counts[:, s % CS, 0:nt * P], start=s == 0 and part is x_hi,
                                                     stop=s == NT - 1 and part is x_lo)
                                if s == NT - 1:
                                    last.then_inc(summed, 1)
                            if s < NT - 1:
                                last.then_inc(counts_used, 1)
                        products_of(m + 1 if c else m, (c - 1) % NC, (u + c) % 2)
                planes = relations(pe, body)
                products_of(planes, NC - 1, (R + NC - 1) % 2)

            @block.scalar
            def _(act):
                def weight(n):
                    for kb in range(KB):
                        act.wait_ge(w_in[kb % NW], n * (KB // NW * 16) + (kb // NW + 1) * 16)
                        act.activation(w_hi[:, kb, :], w_raw[:, kb % NW, :], ACT.Copy).then_inc(w_hi_made, 1)

                def first_parts(n, c, k):
                    width = CHUNKS[c][1] * P
                    for f in range(KB):
                        act.wait_ge(scaled, n * SUMS + c * KB + f + 1)
                        act.activation(m_hi[k][:, f, 0:width], mean[:, f % 2, 0:width], ACT.Copy)\
                            .then_inc(m_hi_made, 1)
                for c in range(NC):
                    first_parts(0, c, c % 2)
                    if c == 0:
                        weight(0)

                def body(r, m, u):
                    for c in range(NC):
                        first_parts(m + 1, c, (u + 1 + c) % 2)
                        if c == 0:
                            act.wait_ge(multiplied, (m + 1) * PRODS)
                            weight(m + 1)
                relations(act, body)

            @block.vector
            def _(v):
                def second_parts(n, c, k, f):
                    width = CHUNKS[c][1] * P
                    v.wait_ge(m_hi_made, n * SUMS + c * KB + f + 1)
                    v.tensor_tensor(m_lo[k][:, f, 0:width], mean[:, f % 2, 0:width],
                                    m_hi[k][:, f, 0:width].bitcast(F32), ALU.subtract).then_inc(m_lo_made, 1)

                def means(n, c, k, fs, inv_row):
                    width = CHUNKS[c][1] * P
                    for f in fs:
                        at = n * SUMS + c * KB + f
                        v.wait_ge(summed, at + 1)
                        if not isinstance(at, int) or at >= 2:
                            v.wait_ge(m_lo_made, at - 1)
                        if inv_row is None:
                            last = v.tensor_copy(mean[:, f % 2, 0:width], sums[f][:, 0:width])
                        else:
                            last = v.tensor_tensor(mean[:, f % 2, 0:width], sums[f][:, 0:width],
                                                   inv[:, inv_row, 0:width], ALU.mult)
                        last.then_inc(scaled, 1)
                        if f > fs[0]:
                            second_parts(n, c, k, f - 1)
                    second_parts(n, c, k, fs[-1])

                def add(n, c, i, over):
                    t, h = CHUNKS[c][0] + i // 2, i % 2
                    v.wait_ge(multiplied, n * PRODS + t * 2 + h + 1)
                    if over:
                        last = v.tensor_copy(out[:, t, half(h)], prod[h][:, 0:HD])
                    else:
                        last = v.tensor_tensor(out[:, t, half(h)], prod[h][:, 0:HD], out[:, t, half(h)], ALU.add)
                    last.then_inc(added, 1)

                def weight(n):
                    for kb in range(KB):
                        v.wait_ge(w_hi_made, n * KB + kb + 1)
                        v.tensor_tensor(w_lo[:, kb, :], w_raw[:, kb % NW, :], w_hi[:, kb, :].bitcast(F32),
                                        ALU.subtract).then_inc(w_lo_made, 1)

                v.memset(out[:, CHUNKS[-1][0]:NT, :], 0.0).then_inc(added, 2)
                for c in range(NC):
                    means(0, c, c % 2, (0, 1, 2), None)
                    if c:
                        add(0, c - 1, 0, True)
                    means(0, c, c % 2, (3, 4, 5), None)
                    for i in range(1, 2 * CHUNKS[c - 1][1] if c else 0):
                        add(0, c - 1, i, True)
                    if c == 0:
                        weight(0)

                def body(r, m, u):
                    for c in range(NC):
                        row = (u + c) % 2
                        v.wait_ge(inv_in[row], m_half(m, u) + ((3 * u + c) // 2 + 1) * 16)
                        before = (m + 1 if c else m, (c - 1) % NC)
                        means(m + 1, c, (u + 1 + c) % 2, (0, 1, 2), row)
                        add(*before, 0, False)
                        means(m + 1, c, (u + 1 + c) % 2, (3, 4, 5), row)
                        for i in range(1, 2 * CHUNKS[before[1]][1]):
                            add(*before, i, False)
                        if c == 0:
                            weight(m + 1)

                def m_half(m, u):
                    return (m - u) * (NC * 16 // 2)
                planes = relations(v, body)
                for i in range(2 * CHUNKS[-1][1]):
                    add(planes, NC - 1, i, False)


H_FFN, N_EXP0 = 384, 4
HB = H_FFN // P


def load_rows(nc, x, rows, row=None, add=None):
    with Phase(nc, "load" + ("add" if row is not None else "")) as ph:
        loaded, done = ph.sem("loaded"), ph.sem("done")
        dest = rows if row is None else ph.sb("x", [P, NT, D])
        bias = ph.sb("bias", [P, D]) if row is not None else None
        with nc.Block() as block:
            @block.sync
            def _(sp):
                sp.wait_ge(done, 1)
                sp.dma_start(dest[:, 0:NT - 1, :], x[0:(NT - 1) * P, :].rearrange("(t p) d -> p t d", p=P))\
                    .then_inc(loaded, 16)
                sp.dma_start(dest[0:LAST, NT - 1, :], x[(NT - 1) * P:N, :]).then_inc(loaded, 16)
                if row is not None:
                    sp.dma_start(bias[:, :], row.partition_broadcast(P)).then_inc(loaded, 16)
                sp.wait_ge(loaded, 48 if row is not None else 32)

            @block.vector
            def _(v):
                v.memset(dest[:, NT - 1, :], 0.0).then_inc(done, 1)
                if row is None:
                    return
                v.wait_ge(loaded, 48)
                for t in range(NT):
                    v.tensor_tensor(rows[:, t, :], rows[:, t, :], dest[:, t, :], ALU.add).then_inc(done, 1)
                for t in range(NT):
                    v.wait_ge(done, t + 2)
                    v.tensor_tensor(rows[:, t, :], rows[:, t, :], bias[:, :], ALU.add).then_inc(done, 1)


def relu_phase(nc, name, rows, row, hi, lo):
    with Phase(nc, name) as ph:
        bias = ph.sb("bias", [P, D])
        loaded, summed, cut, hi_made, lo_made = (ph.sem(x) for x in ("loaded", "summed", "cut", "hi_made", "lo_made"))
        with nc.Block() as block:
            @block.sync
            def _(sp):
                sp.dma_start(bias[:, :], row.partition_broadcast(P)).then_inc(loaded, 16)

            @block.vector
            def _(v):
                v.wait_ge(loaded, 16)
                for t in range(NT + 2):
                    if t < NT:
                        v.tensor_tensor(rows[:, t, :], rows[:, t, :], bias[:, :], ALU.add).then_inc(summed, 1)
                    if 0 < t <= NT:
                        v.wait_ge(summed, t)
                        v.tensor_scalar(rows[:, t - 1, :], rows[:, t - 1, :], 0.0, None, ALU.max).then_inc(cut, 1)
                    if t > 1:
                        v.wait_ge(hi_made, t - 1)
                        v.wait_ge(cut, t - 1)
                        v.tensor_tensor(lo[:, t - 2, :], rows[:, t - 2, :], hi[:, t - 2, :].bitcast(F32),
                                        ALU.subtract).then_inc(lo_made, 1)

            @block.scalar
            def _(act):
                for t in range(NT):
                    act.wait_ge(cut, t + 1)
                    act.activation(hi[:, t, :], rows[:, t, :], ACT.Copy).then_inc(hi_made, 1)


def experts_phase(nc, f_hi, f_lo, rows, wg, bg, w1, b1, w2, b2):
    with Phase(nc, "experts") as ph:
        NC, CW = len(CHUNKS), CHUNKS[0][1] * P
        NE = N_EXP0
        g_raw = ph.sb("g_raw", [P, KB, NE])
        g_hi, g_lo = ph.sb("g_hi", [P, KB, NE], F32R), ph.sb("g_lo", [P, KB, NE], F32R)
        g_bias = ph.sb("g_bias", [P, NE])
        logits, largest = ph.sb("logits", [P, NT, NE]), ph.sb("largest", [P, NT])
        equal, chosen = ph.sb("equal", [P, NT, NE]), ph.sb("chosen", [P, NT, NE])
        free = ph.sb("free", [P, NE, NT])
        raw1, raw2 = ph.sb("raw1", [P, KB, H_FFN]), ph.sb("raw2", [P, HB, D])
        w1_hi, w1_lo = ph.sb("w1_hi", [P, KB, H_FFN], F32R), ph.sb("w1_lo", [P, KB, H_FFN], F32R)
        w2_hi, w2_lo = ph.sb("w2_hi", [P, HB, D], F32R), ph.sb("w2_lo", [P, HB, D], F32R)
        b1_col = ph.sb("b1_col", [P, NE, HB])
        b2_row = ph.sb("b2_row", [P, NE, D])
        act_out = ph.sb("act_out", [P, 2, CW])
        h_hi, h_lo = ph.sb("h_hi", [P, 2, HB, CW], F32R), ph.sb("h_lo", [P, 2, HB, CW], F32R)
        hid = [ph.ps(f"hid{k}", [P, 512]) for k in range(HB)]
        prod = [ph.ps(f"prod{k}", [P, 512]) for k in range(4)]
        gate = ph.ps("gate", [P, NT, NE])
        loaded, raw1_in, raw2_in = ph.sem("loaded"), ph.sem("raw1_in"), ph.sem("raw2_in")
        v_s, gate_split, gated, w1_hi_s, w1_lo_s, w2_hi_s, w2_lo_s = (ph.sem(x) for x in (
            "vector", "gate_split", "gated", "w1_hi_made", "w1_lo_made", "w2_hi_made", "w2_lo_made"))
        hid_made, gelu_made, h_hi_s, h_lo_s, multiplied, added, biased, gate_hi = (ph.sem(x) for x in (
            "hid_made", "gelu_made", "h_hi_made", "h_lo_made", "multiplied", "added", "biased", "gate_hi"))
        PARTS = ((0, 0), (0, 1), (1, 0))

        with nc.Block() as block:
            @block.sync
            def _(sp):
                sp.dma_start(g_raw[:, :, :], wg.rearrange("(k p) n -> p k n", p=P)).then_inc(loaded, 16)
                sp.dma_start(g_bias[:, :], bg.partition_broadcast(P)).then_inc(loaded, 16)
                sp.dma_start(b1_col[:, :, :], b1.rearrange("e (k p) -> p e k", p=P),
                             allow_slow_non_contiguous=True).then_inc(loaded, 16)
                sp.dma_start(b2_row[:, :, :], b2.partition_broadcast(P)).then_inc(loaded, 16)
                for e in range(NE):
                    if e:
                        sp.wait_ge(w1_lo_s, e)
                    sp.dma_start(raw1[:, :, :], w1[e].rearrange("(k p) n -> p k n", p=P)).then_inc(raw1_in, 16)
                    if e:
                        sp.wait_ge(w2_lo_s, e)
                    sp.dma_start(raw2[:, :, :], w2[e].rearrange("(k p) n -> p k n", p=P)).then_inc(raw2_in, 16)

            @block.tensor
            def _(pe):
                pe.wait_ge(gate_split, 1)
                f, g = (f_hi, f_lo), (g_hi, g_lo)
                for t in range(NT):
                    for kb in range(KB):
                        for a, b in PARTS:
                            last = pe.matmul(gate[:, t, :], f[a][:, kb, t * P:(t + 1) * P], g[b][:, kb, :],
                                             start=t == 0 and kb == 0 and (a, b) == (0, 0), stop=True,
                                             skip_group_check=True)
                last.then_inc(gated, 1)
                h, w1p, w2p = (h_hi, h_lo), (w1_hi, w1_lo), (w2_hi, w2_lo)

                def hidden(e, c):
                    t0, nt = CHUNKS[c]
                    if c == 0:
                        pe.wait_ge(w1_lo_s, e + 1)
                    for m in range(HB):
                        if (e, c) != (0, 0):
                            pe.wait_ge(gelu_made, (e * NC + c - 1) * HB + m + 1)
                        for kb in range(KB):
                            for a, b in PARTS:
                                last = pe.matmul(hid[m][:, 0:nt * P], w1p[a][:, kb, m * P:(m + 1) * P],
                                                 f[b][:, kb, t0 * P:(t0 + nt) * P],
                                                 start=kb == 0 and (a, b) == (0, 0), stop=kb == KB - 1 and a == 1)
                        last.then_inc(hid_made, 1)

                def products(e, c):
                    t0, nt = CHUNKS[c]
                    k = (e * NC + c) % 2
                    pe.wait_ge(h_lo_s, (e * NC + c + 1) * HB)
                    if c == 0:
                        pe.wait_ge(w2_lo_s, e + 1)
                    for t in range(nt):
                        for half in range(2):
                            n = (e * NT + t0 + t) * 2 + half
                            if n >= 4:
                                pe.wait_ge(added, n - 3)
                            for m in range(HB):
                                for a, b in PARTS:
                                    last = pe.matmul(prod[n % 4][:, 0:HD], h[a][:, k, m, t * P:(t + 1) * P],
                                                     w2p[b][:, m, half * HD:(half + 1) * HD],
                                                     start=m == 0 and (a, b) == (0, 0), stop=m == HB - 1 and a == 1)
                            last.then_inc(multiplied, 1)
                order = [(e, c) for e in range(NE) for c in range(NC)]
                for i, (e, c) in enumerate(order):
                    hidden(e, c)
                    if i:
                        products(*order[i - 1])
                products(*order[-1])

            @block.scalar
            def _(act):
                act.wait_ge(loaded, 64)
                act.activation(g_hi[:, :, :], g_raw[:, :, :], ACT.Copy).then_inc(gate_hi, 1)

                def weight(e):
                    act.wait_ge(raw1_in, 16 * (e + 1))
                    if e:
                        act.wait_ge(hid_made, e * NC * HB)
                    act.activation(w1_hi[:, :, :], raw1[:, :, :], ACT.Copy).then_inc(w1_hi_s, 1)
                weight(0)
                for e in range(NE):
                    for c, (t0, nt) in enumerate(CHUNKS):
                        i = e * NC + c
                        for m in range(HB):
                            at = i * HB + m
                            act.wait_ge(hid_made, at + 1)
                            if at >= 2:
                                act.wait_ge(h_lo_s, at - 1)
                            act.activation(act_out[:, at % 2, 0:nt * P], hid[m][:, 0:nt * P], ACT.Gelu,
                                           bias=b1_col[:, e, m:m + 1]).then_inc(gelu_made, 1)
                            act.wait_ge(gelu_made, at + 1)
                            if m == 0 and i >= 2:
                                act.wait_ge(multiplied, 2 * (e * NT + t0) - 2 * (CHUNKS[c - 1][1] if c or e else 0))
                            act.activation(h_hi[:, i % 2, m, 0:nt * P], act_out[:, at % 2, 0:nt * P], ACT.Copy)\
                                .then_inc(h_hi_s, 1)
                        if c == 0:
                            act.wait_ge(raw2_in, 16 * (e + 1))
                            if e:
                                act.wait_ge(multiplied, e * NT * 2)
                            act.activation(w2_hi[:, :, :], raw2[:, :, :], ACT.Copy).then_inc(w2_hi_s, 1)
                    if e + 1 < NE:
                        weight(e + 1)

            @block.vector
            def _(v):
                s = Steps(v, v_s)
                v.wait_ge(gate_hi, 1)
                v.tensor_tensor(g_lo[:, :, :], g_raw[:, :, :], g_hi[:, :, :].bitcast(F32), ALU.subtract)\
                    .then_inc(gate_split, 1)

                def weight1(e):
                    v.wait_ge(w1_hi_s, e + 1)
                    v.tensor_tensor(w1_lo[:, :, :], raw1[:, :, :], w1_hi[:, :, :].bitcast(F32), ALU.subtract)\
                        .then_inc(w1_lo_s, 1)
                weight1(0)
                v.wait_ge(gated, 1)
                s.done(v.tensor_tensor(logits[:, :, :], gate[:, :, :],
                                       g_bias[:, :].unsqueeze(1).to_broadcast([P, NT, NE]), ALU.add))
                s.wait()
                s.done(v.tensor_reduce(largest[:, :], logits[:, :, :], AXX, ALU.max))
                s.wait()
                s.done(v.tensor_tensor(equal[:, :, :], logits[:, :, :],
                                       largest[:, :].unsqueeze(2).to_broadcast([P, NT, NE]), ALU.is_equal))
                s.done(v.memset(free[:, 0, :], 1.0))
                for e in range(NE):
                    s.wait()
                    s.done(v.tensor_tensor(chosen[:, :, e], equal[:, :, e], free[:, e, :], ALU.mult))
                    if e + 1 < NE:
                        s.wait()
                        s.done(v.tensor_tensor(free[:, e + 1, :], free[:, e, :], chosen[:, :, e], ALU.subtract))
                s.wait()

                def add(e, t0, i):
                    t, half = t0 + i // 2, i % 2
                    n = (e * NT + t) * 2 + half
                    v.wait_ge(multiplied, n + 1)
                    if not half:
                        if e:
                            v.wait_ge(added, ((e - 1) * NT + t) * 2 + 2)
                        v.scalar_tensor_tensor(out=rows[:, t, :], in0=b2_row[:, e, :], scalar=chosen[:, t, e:e + 1],
                                               in1=rows[:, t, :], op0=ALU.mult, op1=ALU.add).then_inc(biased, 1)
                        v.wait_ge(biased, e * NT + t + 1)
                    at = (slice(None), t, slice(half * HD, (half + 1) * HD))
                    v.scalar_tensor_tensor(out=rows[at], in0=prod[n % 4][:, 0:HD], scalar=chosen[:, t, e:e + 1],
                                           in1=rows[at], op0=ALU.mult, op1=ALU.add).then_inc(added, 1)

                order = [(e, c) for e in range(NE) for c in range(NC)]
                for i, (e, c) in enumerate(order):
                    nt = CHUNKS[c][1]
                    for m in range(HB):
                        at = i * HB + m
                        v.wait_ge(h_hi_s, at + 1)
                        v.tensor_tensor(h_lo[:, i % 2, m, 0:nt * P], act_out[:, at % 2, 0:nt * P],
                                        h_hi[:, i % 2, m, 0:nt * P].bitcast(F32), ALU.subtract).then_inc(h_lo_s, 1)
                    if i:
                        pe_, pc = order[i - 1]
                        for n in range(2 * CHUNKS[pc][1]):
                            add(pe_, CHUNKS[pc][0], n)
                    if c == 0:
                        v.wait_ge(w2_hi_s, e + 1)
                        v.tensor_tensor(w2_lo[:, :, :], raw2[:, :, :], w2_hi[:, :, :].bitcast(F32), ALU.subtract)\
                            .then_inc(w2_lo_s, 1)
                    if c == NC - 1 and e + 1 < NE:
                        weight1(e + 1)
                for n in range(2 * CHUNKS[-1][1]):
                    add(NE - 1, CHUNKS[-1][0], n)


SUM_AT = 256
NEVER = -1e38


def loops_phase(nc, c_dram, ident, ctot_dram, no_edge_dram):
    with Phase(nc, "loops") as ph:
        total = ph.sb("total", [P, 2, NP])
        with_loop = ph.sb("with_loop", [P, 2, NP])
        none = ph.sb("none", [P, 2, NP])
        turned_sb = ph.sb("turned_sb", [P, 2, NP])
        turned = [ph.ps(f"turned{k}", [P, 3, 512]) for k in range(2)]
        loaded = [ph.sem(f"loaded{k}") for k in range(2)]
        counts_out = [ph.sem(f"counts_out{k}") for k in range(2)]
        none_out = [ph.sem(f"none_out{k}") for k in range(2)]
        copied, looped, none_made, turned_s, taken = (ph.sem(x) for x in (
            "copied", "looped", "none_made", "turned", "taken"))
        def store(sp, t):
            sp.wait_ge(looped, t + 1)
            sp.dma_start(ctot_dram[t * P:(t + 1) * P, :], with_loop[:, t % 2, :]).then_inc(counts_out[t % 2], 16)
            sp.wait_ge(taken, t + 1)
            sp.dma_start(no_edge_dram[:, t * P:(t + 1) * P].rearrange("(j p) s -> p j s", p=P),
                         turned_sb[:, t % 2, :].rearrange("p (j s) -> p j s", s=P)).then_inc(none_out[t % 2], 16)

        with nc.Block() as block:
            @block.sync
            def _(sp):
                for t in range(NT):
                    if t >= 2:
                        sp.wait_ge(looped, t - 1)
                    sp.dma_start(total[:, t % 2, :], c_dram[plane(R, 0), t * P:(t + 1) * P, :])\
                        .then_inc(loaded[t % 2], 16)
                    if t:
                        store(sp, t - 1)
                store(sp, NT - 1)
                for k in range(2):
                    sp.wait_ge(counts_out[k], NT // 2 * 16)
                    sp.wait_ge(none_out[k], NT // 2 * 16)

            @block.vector
            def _(v):
                for t in range(NT):
                    v.wait_ge(loaded[t % 2], (t // 2 + 1) * 16)
                    if t >= 2:
                        v.wait_ge(counts_out[t % 2], t // 2 * 16)
                        v.wait_ge(turned_s, t - 1)
                    v.tensor_copy(with_loop[:, t % 2, :], total[:, t % 2, :]).then_inc(copied, 1)
                    v.wait_ge(copied, t + 1)
                    v.tensor_tensor(with_loop[:, t % 2, t * P:(t + 1) * P], with_loop[:, t % 2, t * P:(t + 1) * P],
                                    ident[:, :], ALU.add).then_inc(looped, 1)
                    v.wait_ge(looped, t + 1)
                    v.tensor_scalar(none[:, t % 2, :], with_loop[:, t % 2, :], 0.0, NEVER, ALU.is_equal,
                                    ALU.mult).then_inc(none_made, 1)

            @block.tensor
            def _(pe):
                for t in range(NT):
                    pe.wait_ge(none_made, t + 1)
                    if t >= 2:
                        pe.wait_ge(taken, t - 1)
                    for j in range(NT):
                        last = pe.transpose(turned[t % 2][:, j // 4, (j % 4) * P:(j % 4 + 1) * P],
                                            none[:, t % 2, j * P:(j + 1) * P], ident[:, :])
                    last.then_inc(turned_s, 1)

            @block.scalar
            def _(act):
                for t in range(NT):
                    act.wait_ge(turned_s, t + 1)
                    if t >= 2:
                        act.wait_ge(none_out[t % 2], t // 2 * 16)
                    act.activation(turned_sb[:, t % 2, :],
                                   turned[t % 2].rearrange("p b c -> p (b c)")[:, 0:NP], ACT.Copy).then_inc(taken, 1)


def add_low_phase(nc, flag, c_dram, ctot_dram):
    with Phase(nc, "low") as ph:
        high, low = ph.sb("high", [P, NP]), ph.sb("low", [P, NP])
        loaded, summed, stored = ph.sem("loaded"), ph.sem("summed"), ph.sem("stored")
        with nc.Block() as block:
            @block.sync
            def _(sp):
                def run():
                    for t in range(NT):
                        if t:
                            sp.wait_ge(stored, t * 16)
                        sp.dma_start(high[:, :], ctot_dram[t * P:(t + 1) * P, :]).then_inc(loaded, 16)
                        sp.dma_start(low[:, :], c_dram[plane(R, 1), t * P:(t + 1) * P, :]).then_inc(loaded, 16)
                        sp.wait_ge(summed, t + 1)
                        sp.dma_start(ctot_dram[t * P:(t + 1) * P, :], high[:, :]).then_inc(stored, 16)
                    sp.wait_ge(stored, NT * 16)
                where_flag(sp, flag, run, True)

            @block.vector
            def _(v):
                def run():
                    for t in range(NT):
                        v.wait_ge(loaded, (t + 1) * 32)
                        v.tensor_tensor(high[:, :], high[:, :], low[:, :], ALU.add).then_inc(summed, 1)
                where_flag(v, flag, run, True)


def turn_phase(nc, name, rows, blocks, ident, f_hi, f_lo, at=0):
    with Phase(nc, name) as ph:
        turned = [ph.ps(f"turned{k}", [P, 4, P]) for k in range(4)]
        turned_s, hi_made, lo_made = (ph.sem(x) for x in ("turned", "hi_made", "lo_made"))
        steps = [(t, f, min(4, blocks - f)) for t in range(NT) for f in range(0, blocks, 4)]

        def where(t, f, n):
            return slice(None), slice(at + f, at + f + n), slice(t * P, (t + 1) * P)
        with nc.Block() as block:
            @block.tensor
            def _(pe):
                for i, (t, f, n) in enumerate(steps):
                    if i >= 4:
                        pe.wait_ge(lo_made, i - 3)
                    for k in range(n):
                        last = pe.transpose(turned[i % 4][:, k, :], rows[:, t, (f + k) * P:(f + k + 1) * P],
                                            ident[:, :])
                    last.then_inc(turned_s, 1)

            @block.scalar
            def _(act):
                for i, (t, f, n) in enumerate(steps):
                    act.wait_ge(turned_s, i + 1)
                    act.activation(f_hi[where(t, f, n)], turned[i % 4][:, 0:n, :], ACT.Copy).then_inc(hi_made, 1)

            @block.vector
            def _(v):
                for i, (t, f, n) in enumerate(steps):
                    v.wait_ge(hi_made, i + 1)
                    v.tensor_tensor(f_lo[where(t, f, n)], turned[i % 4][:, 0:n, :],
                                    f_hi[where(t, f, n)].bitcast(F32), ALU.subtract).then_inc(lo_made, 1)


def project_phase(nc, name, f_hi, f_lo, kbs, jobs, beside=None):
    with Phase(nc, name) as ph:
        side = beside(ph) if beside else None
        width = max(w for _, w, _, _ in jobs)
        raw = ph.sb("raw", [P, kbs, width])
        w_hi = [ph.sb(f"w_hi{k}", [P, kbs, width], F32R) for k in range(2)]
        w_lo = [ph.sb(f"w_lo{k}", [P, kbs, width], F32R) for k in range(2)]
        stage = ph.sb("stage", [P, 2, width])
        prod = [ph.ps(f"prod{k}", [P, 512]) for k in range(4)]
        raw_in, w_hi_s, w_lo_s, multiplied, hi_out, taken = (ph.sem(x) for x in (
            "raw_in", "w_hi_made", "w_lo_made", "multiplied", "hi_out", "taken"))
        stored = [ph.sem(f"stored{k}") for k in range(2)]

        def weights(j):
            return jobs[j][0] if isinstance(jobs[j][0], list) else [(jobs[j][0], 0, kbs)]

        def pieces(i):
            n = len(jobs) * NT
            return range(i * side.pieces // n, (i + 1) * side.pieces // n) if side else ()
        DRAM_JOBS = [j for j, job in enumerate(jobs) if job[2] == "dram"]

        def stores_before(j, t, k):
            return sum(1 for i in DRAM_JOBS for u in range(NT) if (i, u) < (j, t) and u % 2 == k)
        with nc.Block() as block:
            @block.sync
            def _(sp):
                def load(j):
                    if j:
                        sp.wait_ge(w_lo_s, j)
                    for view, k0, k1 in weights(j):
                        sp.dma_start(raw[:, k0:k1, 0:jobs[j][1]], view).then_inc(raw_in, 16)
                load(0)
                if side:
                    side.sync_begin(sp)
                for j, (_, w, sink, dest) in enumerate(jobs):
                    if j + 1 < len(jobs):
                        load(j + 1)
                    for t in range(NT):
                        if sink == "dram":
                            sp.wait_ge(taken, j * NT + t + 1)
                            sp.dma_start(dest(t), stage[:, t % 2, 0:w]).then_inc(stored[t % 2], 16)
                        for i in pieces(j * NT + t):
                            side.sync_piece(sp, i)
                if side:
                    side.sync_end(sp)
                for k in range(2):
                    if DRAM_JOBS:
                        sp.wait_ge(stored[k], 16 * stores_before(len(jobs), 0, k))

            @block.tensor
            def _(pe):
                f, w_parts = (f_hi, f_lo), (w_hi, w_lo)
                for j, (_, w, _, _) in enumerate(jobs):
                    pe.wait_ge(w_lo_s, j + 1)
                    for t in range(NT):
                        i = j * NT + t
                        if i >= 4:
                            pe.wait_ge(taken, i - 3)
                        for kb in range(kbs):
                            for a, b in ((0, 0), (0, 1), (1, 0)):
                                last = pe.matmul(prod[i % 4][:, 0:w], f[a][:, kb, t * P:(t + 1) * P],
                                                 w_parts[b][j % 2][:, kb, 0:w], start=kb == 0 and (a, b) == (0, 0),
                                                 stop=kb == kbs - 1 and a == 1)
                        last.then_inc(multiplied, 1)
                if side:
                    side.tensor_end(pe)

            @block.scalar
            def _(act):
                def weight(j):
                    act.wait_ge(raw_in, 16 * sum(len(weights(i)) for i in range(j + 1)))
                    if j >= 2:
                        act.wait_ge(multiplied, (j - 1) * NT)
                    w = jobs[j][1]
                    act.activation(w_hi[j % 2][:, :, 0:w], raw[:, :, 0:w], ACT.Copy).then_inc(w_hi_s, 1)
                weight(0)
                for j, (_, w, sink, dest) in enumerate(jobs):
                    for t in range(NT):
                        if t == 1 and j + 1 < len(jobs):
                            weight(j + 1)
                        i = j * NT + t
                        if sink == "parts":
                            act.wait_ge(multiplied, i + 1)
                            act.activation(dest(t)[0], prod[i % 4][:, 0:w], ACT.Copy).then_inc(hi_out, 1)
                        elif sink == "dram":
                            act.wait_ge(multiplied, i + 1)
                            if stores_before(j, t, t % 2):
                                act.wait_ge(stored[t % 2], 16 * stores_before(j, t, t % 2))
                            act.activation(stage[:, t % 2, 0:w], prod[i % 4][:, 0:w], ACT.Copy).then_inc(taken, 1)

            @block.vector
            def _(v):
                def weight(j):
                    w = jobs[j][1]
                    v.wait_ge(w_hi_s, j + 1)
                    v.tensor_tensor(w_lo[j % 2][:, :, 0:w], raw[:, :, 0:w], w_hi[j % 2][:, :, 0:w].bitcast(F32),
                                    ALU.subtract).then_inc(w_lo_s, 1)
                weight(0)
                parts = 0
                for j, (_, w, sink, dest) in enumerate(jobs):
                    for t in range(NT):
                        if t == 1 and j + 1 < len(jobs):
                            weight(j + 1)
                        i = j * NT + t
                        if sink == "parts":
                            parts += 1
                            v.wait_ge(hi_out, parts)
                            v.tensor_tensor(dest(t)[1], prod[i % 4][:, 0:w], dest(t)[0].bitcast(F32),
                                            ALU.subtract).then_inc(taken, 1)
                        elif sink == "add":
                            v.wait_ge(multiplied, i + 1)
                            v.tensor_tensor(dest(t), prod[i % 4][:, 0:w], dest(t), ALU.add).then_inc(taken, 1)
                        for k in pieces(i):
                            side.vector_piece(v, k)
                if side:
                    side.vector_end(v)


def logits_phase(nc, name, f_hi, f_lo, kbs, w_t, a_src, a_dst, heads, ident, cols, rows_dram):
    with Phase(nc, name) as ph:
        width, rest = w_t.shape
        cbs = width // P
        n = 2 * heads
        att = ph.sb("att", [P, cbs, 2])
        weight = ph.sb("weight", [P, cbs, rest])
        wa = ph.sb("wa", [P, kbs, n])
        wa_hi, wa_lo = ph.sb("wa_hi", [P, kbs, n], F32R), ph.sb("wa_lo", [P, kbs, n], F32R)
        by_head = ph.sb("by_head", [P, heads, NT])
        row = ph.sb("row", [NT * heads, P])
        wa_acc = ph.ps("wa_acc", [P, kbs, 2, heads])
        acc = ph.ps("acc", [P, NT, n])
        turned = ph.ps("turned", [P, P])
        att_in, wa_made, copied, split, multiplied, made, turned_s, taken, stored = (ph.sem(x) for x in (
            "att_in", "wa_made", "copied", "split", "multiplied", "made", "turned", "taken", "stored"))
        weight_in = [ph.sem(f"weight_in{k}") for k in range(2)]
        with nc.Block() as block:
            @block.sync
            def _(sp):
                for k, a in enumerate((a_src, a_dst)):
                    sp.dma_start(att[:, :, k], a.rearrange("h c -> (h c)").rearrange("(k p) -> p k", p=P),
                                 allow_slow_non_contiguous=True).then_inc(att_in, 16)
                for cb in range(cbs):
                    sp.dma_start(weight[:, cb, :], w_t[cb * P:(cb + 1) * P, :]).then_inc(weight_in[cb % 2], 16)
                sp.wait_ge(taken, 1)
                sp.dma_start(rows_dram.rearrange("h (t p) -> (h t) p", p=P), row[:, :]).then_inc(stored, 16)
                sp.wait_ge(stored, 16)

            @block.tensor
            def _(pe):
                pe.wait_ge(att_in, 32)
                for k in range(2):
                    pe.wait_ge(weight_in[k], cbs // 2 * 16)
                for cb in range(cbs):
                    for kb in range(kbs):
                        last = pe.matmul(wa_acc[:, kb, :, cb * heads // cbs], weight[:, cb, kb * P:(kb + 1) * P],
                                         att[:, cb, :], start=cb == 0 and kb == 0, stop=True, skip_group_check=True)
                last.then_inc(wa_made, 1)
                pe.wait_ge(split, 2)
                f, g = (f_hi, f_lo), (wa_hi, wa_lo)
                for t in range(NT):
                    for kb in range(kbs):
                        for a, b in ((0, 0), (0, 1), (1, 0)):
                            last = pe.matmul(acc[:, t, :], f[a][:, kb, t * P:(t + 1) * P], g[b][:, kb, :],
                                             start=t == 0 and kb == 0 and (a, b) == (0, 0), stop=True,
                                             skip_group_check=True)
                last.then_inc(multiplied, 1)
                pe.wait_ge(made, 2)
                pe.transpose(turned[0:NT * heads, :], by_head[:, :, :].rearrange("p h t -> p (h t)"), ident[:, :])\
                    .then_inc(turned_s, 1)

            @block.vector
            def _(v):
                v.wait_ge(wa_made, 1)
                v.tensor_copy(wa[:, :, :], wa_acc[:, :, :, :].rearrange("p k s h -> p k (s h)")).then_inc(copied, 1)
                v.wait_ge(split, 1)
                v.tensor_tensor(wa_lo[:, :, :], wa[:, :, :], wa_hi[:, :, :].bitcast(F32), ALU.subtract)\
                    .then_inc(split, 1)
                v.wait_ge(multiplied, 1)
                v.tensor_copy(cols[:, :, :], acc[:, :, :]).then_inc(made, 1)
                v.tensor_copy(by_head[:, :, :], acc[:, :, 0:heads].rearrange("p t h -> p h t")).then_inc(made, 1)
                v.wait_ge(turned_s, 1)
                v.tensor_copy(row[:, :], turned[0:NT * heads, :]).then_inc(taken, 1)

            @block.scalar
            def _(act):
                act.wait_ge(copied, 1)
                act.activation(wa_hi[:, :, :], wa[:, :, :], ACT.Copy).then_inc(split, 1)


class Maxima:

    def __init__(self, ph, heads, ident, cols, rows_dram, no_edge_dram, shift_dram):
        self.heads, self.pieces, self.ident, self.cols = heads, heads * NT, ident, cols
        self.rows_dram, self.no_edge_dram, self.shift_dram = rows_dram, no_edge_dram, shift_dram
        self.source = ph.sb("source", [P, heads, NP])
        self.none = ph.sb("none", [P, 2, NP])
        self.masked = ph.sb("masked", [P, 2, NP])
        self.top = ph.sb("top", [P, NT, heads])
        self.z, self.fifth, self.m = (ph.sb(x, [P, NT, heads]) for x in ("z", "fifth", "m"))
        self.shift = ph.sb("shift", [P, 2, heads, NT])
        self.row = ph.sb("row", [NT * heads, 2, P])
        self.turned = ph.ps("turned", [P, 2, P])
        self.source_in, self.top_s, self.small, self.turned_s, self.taken, self.stored = (ph.sem(x) for x in (
            "source_in", "top", "small", "shifts_turned", "shifts_taken", "shifts_stored"))
        self.none_in = [ph.sem(f"none_in{k}") for k in range(2)]

    def sync_begin(self, sp):
        for h in range(self.heads):
            sp.dma_start(self.source[:, h, :], self.rows_dram[h].partition_broadcast(P)).then_inc(self.source_in, 16)
        for t in range(2):
            self.load_none(sp, t)

    def load_none(self, sp, t):
        if t >= 2:
            sp.wait_ge(self.top_s, self.heads * (t - 1))
        sp.dma_start(self.none[:, t % 2, :], self.no_edge_dram[t * P:(t + 1) * P, :]).then_inc(self.none_in[t % 2], 16)

    def sync_piece(self, sp, i):
        if i % self.heads == self.heads - 1 and i // self.heads + 2 < NT:
            self.load_none(sp, i // self.heads + 2)

    def sync_end(self, sp):
        sp.wait_ge(self.taken, 1)
        for k in range(2):
            sp.dma_start(self.shift_dram[k].rearrange("h (t p) -> (h t) p", p=P), self.row[:, k, :])\
                .then_inc(self.stored, 16)
        sp.wait_ge(self.stored, 32)

    def vector_piece(self, v, i):
        t, h = divmod(i, self.heads)
        if i == 0:
            v.wait_ge(self.source_in, self.heads * 16)
        if h == 0:
            v.wait_ge(self.none_in[t % 2], (t // 2 + 1) * 16)
        if i >= 2:
            v.wait_ge(self.top_s, i - 1)
        v.tensor_tensor_reduce(out=self.masked[:, i % 2, :], in0=self.source[:, h, :], in1=self.none[:, t % 2, :],
                               scale=1.0, scalar=2 * NEVER, op0=ALU.add, op1=ALU.max,
                               accum_out=self.top[:, t, h:h + 1]).then_inc(self.top_s, 1)

    def vector_end(self, v):
        s = Steps(v, self.small)
        v.wait_ge(self.top_s, self.pieces)
        z, fifth, m = self.z, self.fifth, self.m
        ad = self.cols[:, :, self.heads:2 * self.heads]
        s.done(v.tensor_tensor(z[:, :, :], self.top[:, :, :], ad, ALU.add))
        s.done(v.tensor_scalar(fifth[:, :, :], ad, 0.2, None, ALU.mult))
        s.wait()
        s.done(v.scalar_tensor_tensor(out=m[:, :, :], in0=z[:, :, :], scalar=0.2, in1=z[:, :, :],
                                      op0=ALU.mult, op1=ALU.max))
        s.wait()
        for k, of in enumerate((ad, fifth[:, :, :])):
            s.done(v.tensor_tensor(self.shift[:, k, :, :].rearrange("p h t -> p t h"), of, m[:, :, :], ALU.subtract))
        v.wait_ge(self.turned_s, 1)
        v.tensor_copy(self.row[:, :, :], self.turned[0:NT * self.heads, :, :]).then_inc(self.taken, 1)

    def tensor_end(self, pe):
        pe.wait_ge(self.small, 5)
        for k in range(2):
            last = pe.transpose(self.turned[0:NT * self.heads, k, :],
                                self.shift[:, k, :, :].rearrange("p h t -> p (h t)"), self.ident[:, :])
        last.then_inc(self.turned_s, 1)


def aggregate_phase(nc, name, heads, c, cols, shift_dram, ctot_dram, xl_hi, xl_lo, out, bias):
    with Phase(nc, name) as ph:
        cut = [(0, c + 2)] if c + 2 <= 512 else [(0, SUM_AT + 2), (SUM_AT + 2, c - SUM_AT)]
        B = len(cut)
        chunks = CHUNKS if B == 1 else [(t, 2) for t in range(0, NT, 2)]
        NC, CW = len(chunks), chunks[0][1] * P
        sum_at = cut[0][1] - 2
        source_fifth = ph.sb("source_fifth", [P, NT, heads])
        shift = ph.sb("shift", [P, 2, 2, NP])
        counts = ph.sb("counts", [P, 4, CW])
        e1, e2 = ph.sb("e1", [P, 2, CW]), ph.sb("e2", [P, 2, CW])
        larger, weight = ph.sb("larger", [P, 2, CW]), ph.sb("weight", [P, 2, CW])
        p_hi = [ph.sb(f"p_hi{k}", [P, CW], F32R) for k in range(4)]
        p_lo = [ph.sb(f"p_lo{k}", [P, CW], F32R) for k in range(4)]
        total, inverse = ph.sb("total", [P, 8]), ph.sb("inverse", [P, 8])
        bias_row = ph.sb("bias", [P, heads * c])
        bias_in = ph.sem("bias_in")
        acc = [ph.ps(f"acc{k}", [P, 512]) for k in range(8)]
        fifth_s, e_made, larger_s, weight_s, hi_s, lo_s, used, small, out_s = (ph.sem(x) for x in (
            "fifth", "e_made", "larger", "weight", "hi", "lo", "used", "small", "out"))
        shift_in = [ph.sem(f"shift_in{k}") for k in range(2)]
        counts_in = [ph.sem(f"counts_in{k}") for k in range(4)]
        steps = [(h, i, t0, nt, s) for h in range(heads) for i, (t0, nt) in enumerate(chunks) for s in range(NT)]

        with nc.Block() as block:
            @block.sync
            def _(sp):
                sp.dma_start(bias_row[:, :], bias.partition_broadcast(P)).then_inc(bias_in, 16)
                for n, (h, i, t0, nt, s) in enumerate(steps):
                    if i == 0 and s == 0:
                        if h >= 2:
                            sp.wait_ge(e_made, (h - 1) * NC * NT)
                        for k in range(2):
                            sp.dma_start(shift[:, h % 2, k, :], shift_dram[k, h].partition_broadcast(P))\
                                .then_inc(shift_in[h % 2], 16)
                    if n >= 4:
                        sp.wait_ge(weight_s, n - 3)
                    sp.dma_start(counts[:, n % 4, 0:nt * P],
                                 ctot_dram[s * P:(s + 1) * P, t0 * P:(t0 + nt) * P]).then_inc(counts_in[n % 4], 16)

            @block.scalar
            def _(act):
                act.wait_ge(fifth_s, 1)

                def first_part(n):
                    nt = steps[n][3]
                    act.wait_ge(weight_s, n + 1)
                    if n >= 4:
                        act.wait_ge(used, n - 3)
                    act.activation(p_hi[n % 4][:, 0:nt * P], weight[:, n % 2, 0:nt * P], ACT.Copy).then_inc(hi_s, 1)
                for n, (h, i, t0, nt, s) in enumerate(steps):
                    if i == 0 and s == 0:
                        act.wait_ge(shift_in[h % 2], (h // 2 + 1) * 32)
                    if n >= 2:
                        act.wait_ge(larger_s, n - 1)
                    at = slice(t0 * P, (t0 + nt) * P)
                    act.activation(e1[:, n % 2, 0:nt * P], shift[:, h % 2, 0, at], ACT.Exp, bias=cols[:, s, h:h + 1])
                    act.activation(e2[:, n % 2, 0:nt * P], shift[:, h % 2, 1, at], ACT.Exp,
                                   bias=source_fifth[:, s, h:h + 1]).then_inc(e_made, 1)
                    if n:
                        first_part(n - 1)
                first_part(len(steps) - 1)

            @block.vector
            def _(v):
                v.tensor_scalar(source_fifth[:, :, :], cols[:, :, 0:heads], 0.2, None, ALU.mult).then_inc(fifth_s, 1)

                def second_part(n):
                    nt = steps[n][3]
                    v.wait_ge(hi_s, n + 1)
                    v.tensor_tensor(p_lo[n % 4][:, 0:nt * P], weight[:, n % 2, 0:nt * P],
                                    p_hi[n % 4][:, 0:nt * P].bitcast(F32), ALU.subtract).then_inc(lo_s, 1)
                small_n = Steps(v, small)
                v.wait_ge(bias_in, 16)

                def finish(g):
                    h, i = g // NC, g % NC
                    t0, nt = chunks[i]
                    v.wait_ge(used, (g + 1) * NT)
                    half = g % 2 * 4
                    for k in range(nt):
                        small_n.done(v.tensor_scalar(total[:, half + k:half + k + 1],
                                                     acc[half + k * B][:, sum_at:sum_at + 1], 1e-16, None, ALU.add))
                    small_n.wait()
                    small_n.done(v.reciprocal(inverse[:, half:half + nt], total[:, half:half + nt]))
                    small_n.wait()
                    for k in range(nt):
                        at = 0
                        for b, (_, w) in enumerate(cut):
                            w -= 2 if b == 0 else 0
                            here = slice(h * c + at, h * c + at + w)
                            last = v.scalar_tensor_tensor(out=out[:, t0 + k, here], in0=acc[half + k * B + b][:, 0:w],
                                                          scalar=inverse[:, half + k:half + k + 1],
                                                          in1=bias_row[:, here], op0=ALU.mult, op1=ALU.add)
                            at += w
                    last.then_inc(out_s, 1)
                for n, (h, i, t0, nt, s) in enumerate(steps):
                    v.wait_ge(e_made, n + 1)
                    v.wait_ge(counts_in[n % 4], (n // 4 + 1) * 16)
                    v.tensor_tensor(larger[:, n % 2, 0:nt * P], e1[:, n % 2, 0:nt * P], e2[:, n % 2, 0:nt * P],
                                    ALU.max).then_inc(larger_s, 1)
                    if n:
                        second_part(n - 1)
                    v.wait_ge(larger_s, n + 1)
                    v.scalar_tensor_tensor(out=weight[:, n % 2, 0:nt * P], in0=larger[:, n % 2, 0:nt * P], scalar=1.0,
                                           in1=counts[:, n % 4, 0:nt * P], op0=ALU.min, op1=ALU.mult)\
                        .then_inc(weight_s, 1)
                    if s == 4 and n > 4:
                        finish(n // NT - 1)
                second_part(len(steps) - 1)
                finish(heads * NC - 1)

            @block.tensor
            def _(pe):
                x = (xl_hi, xl_lo)
                for n, (h, i, t0, nt, s) in enumerate(steps):
                    g = n // NT
                    pe.wait_ge(lo_s, n + 1)
                    if s == 0 and g >= 2:
                        pe.wait_ge(out_s, g - 1)
                    for k in range(nt):
                        for b, (at, w) in enumerate(cut):
                            at += h * (c + 2)
                            for pa, xb in ((p_hi, 0), (p_hi, 1), (p_lo, 0)):
                                last = pe.matmul(acc[g % 2 * 4 + k * B + b][:, 0:w],
                                                 pa[n % 4][:, k * P:(k + 1) * P], x[xb][:, s, at:at + w],
                                                 start=s == 0 and pa is p_hi and xb == 0,
                                                 stop=s == NT - 1 and pa is p_lo)
                    last.then_inc(used, 1)


def layer_norm_phase(nc, name, rows, width, gain, shift, relu, others, more=None):
    with Phase(nc, name) as ph:
        pieces = width // 256
        vec = ph.sb("vec", [P, 3, width])
        stats = ph.sb("stats", [P, NT, pieces, 6])
        moments = ph.sb("moments", [P, NT, 2])
        eps, dev, inv, less = ph.sb("eps", [P, 1]), ph.sb("dev", [P, NT]), ph.sb("inv", [P, NT]), ph.sb("less", [P, NT])
        other = ph.sb("other", [P, 3, len(others), width])
        loaded, steps_s, dev_made, normed, tile_done = (ph.sem(x) for x in (
            "loaded", "steps", "dev_made", "normed", "tile_done"))
        other_in = [ph.sem(f"other_in{k}") for k in range(3)]
        rows_in = [a for a in (gain, shift, more) if a is not None]
        with nc.Block() as block:
            @block.sync
            def _(sp):
                for k, a in enumerate(rows_in):
                    sp.dma_start(vec[:, k, :], a.partition_broadcast(P)).then_inc(loaded, 16)
                for t in range(NT):
                    if t >= 3:
                        sp.wait_ge(tile_done, t - 2)
                    for k, a in enumerate(others):
                        sp.dma_start(other[:, t % 3, k, :], a[t * P:(t + 1) * P, :]).then_inc(other_in[t % 3], 16)

            @block.scalar
            def _(act):
                act.wait_ge(steps_s, 1 + NT * pieces + NT)
                act.activation(dev[:, :], moments[:, :, 1], ACT.Sqrt, bias=eps[:, 0:1]).then_inc(dev_made, 1)
                act.wait_ge(steps_s, 1 + NT * pieces + NT + 2)
                for t in range(NT):
                    act.activation(rows[:, t, :], rows[:, t, :], ACT.Identity, bias=less[:, t:t + 1],
                                   scale=inv[:, t:t + 1]).then_inc(normed, 1)

            @block.vector
            def _(v):
                s = Steps(v, steps_s)
                s.done(v.memset(eps[:, :], EPS))
                for t in range(NT):
                    for k in range(pieces):
                        s.done(v.bn_stats(stats[:, t, k, :], rows[:, t, k * 256:(k + 1) * 256]))
                s.wait()
                for t in range(NT):
                    s.done(v.bn_aggr(moments[:, t, :], stats[:, t, :, :].rearrange("p a b -> p (a b)")))
                v.wait_ge(dev_made, 1)
                s.done(v.reciprocal(inv[:, :], dev[:, :]))
                s.wait()
                s.done(v.scalar_tensor_tensor(out=less[:, :], in0=moments[:, :, 0], scalar=-1.0, in1=inv[:, :],
                                              op0=ALU.mult, op1=ALU.mult))
                v.wait_ge(loaded, 16 * len(rows_in))
                last = 1 + len(others) + (more is not None)
                count = {}

                def step(t, k):
                    r = rows[:, t, :]
                    if k == 0:
                        v.wait_ge(normed, t + 1)
                        i = v.tensor_tensor(r, r, vec[:, 0, :], ALU.mult)
                    else:
                        v.wait_ge(steps_s, count[t, k - 1])
                        if k == 2:
                            v.wait_ge(other_in[t % 3], (t // 3 + 1) * 16 * len(others))
                        if k == 1:
                            i = v.tensor_tensor(r, r, vec[:, 1, :], ALU.add)
                        else:
                            a = other[:, t % 3, k - 2, :] if k - 2 < len(others) else vec[:, 2, :]
                            if k == 2 and relu:
                                i = v.scalar_tensor_tensor(out=r, in0=r, scalar=0.0, in1=a, op0=ALU.max, op1=ALU.add)
                            else:
                                i = v.tensor_tensor(r, r, a, ALU.add)
                    if k == 1 + len(others):
                        i.then_inc(tile_done, 1)
                        if k < last:
                            v.wait_ge(tile_done, t + 1)
                        count[t, k] = s.n
                    else:
                        count[t, k] = s.done(i)
                for t in range(0, NT, 2):
                    for k in range(last + 1):
                        step(t, k)
                        step(t + 1, k)


def rows_phase(nc, name, rows, dram, to_dram):
    with Phase(nc, name) as ph:
        moved = ph.sem("moved")
        with nc.Block() as block:
            @block.sync
            def _(sp):
                there = dram.rearrange("(t p) d -> p t d", p=P)
                a, b = (there, rows[:, :, :]) if to_dram else (rows[:, :, :], there)
                sp.dma_start(a, b).then_inc(moved, 16)
                sp.wait_ge(moved, 16)


def ones_phase(nc, name, hi, lo, places):
    with Phase(nc, name) as ph:
        made = ph.sem("made")
        one, zero = ph.sb("one", [P, NT, 2]), ph.sb("zero", [P, NT, 2])
        with nc.Block() as block:
            @block.vector
            def _(v):
                v.memset(one[:, :, :], 1.0).then_inc(made, 1)
                v.memset(zero[:, :, :], 0.0).then_inc(made, 1)
                v.wait_ge(made, 2)
                for at in places:
                    v.tensor_copy(hi[:, :, at:at + 2], one[:, :, :])
                    v.tensor_copy(lo[:, :, at:at + 2], zero[:, :, :]).then_inc(made, 1)


def by_block(w, c0, c1):
    return w[:, c0:c1].rearrange("(k p) n -> p k n", p=P)


def gat_layers(nc, rows, rows_ctx, g, ident, ctot_dram, no_edge_dram):
    def dram(name, shape):
        return nc.dram_tensor(f"gat_{name}", shape, F32, kind="Internal").ap()
    heads, c1 = g["a_src1"].shape
    w1, wide = heads * (c1 + 2), heads * c1
    x2 = dram("x", (NP, D))
    res1, res2 = dram("res1", (NP, wide)), dram("res2", (NP, D))
    kb2 = wide // P
    with ExitStack() as ctx:
        cols = ctx.enter_context(nc.sbuf_tensor("gat_cols", [P, NT, 2 * heads], F32, side="right"))
        cols2 = ctx.enter_context(nc.sbuf_tensor("gat_cols2", [P, NT, 2], F32, side="right"))
        left, right = ExitStack(), ExitStack()
        right_sb = lambda name, shape, dt=F32: right.enter_context(nc.sbuf_tensor(name, shape, dt, side="right"))
        left_sb = lambda name, shape, dt=F32: left.enter_context(nc.sbuf_tensor(name, shape, dt))
        f_hi, f_lo = (right_sb(f"gat_f{k}", [P, KB, NP], F32R) for k in range(2))
        norm_phase(nc, "gat_norm", rows, ident, features=(f_hi, f_lo), keep=x2)
        rows_ctx.close()
        src_rows, shifts = dram("src1", (heads, NP)), dram("shifts1", (2, heads, NP))
        logits_phase(nc, "logits1", f_hi, f_lo, KB, g["w1_t"], g["a_src1"], g["a_dst1"], heads, ident, cols, src_rows)
        project_phase(nc, "res1", f_hi, f_lo, KB, [
            (by_block(g["Wr1"], j * 256, j * 256 + 256), 256, "dram",
             lambda t, j=j: res1[t * P:(t + 1) * P, j * 256:j * 256 + 256]) for j in range(wide // 256)],
            beside=lambda ph: Maxima(ph, heads, ident, cols, src_rows, no_edge_dram, shifts))
        xl_hi, xl_lo = (left_sb(f"gat_xl{k}", [P, NT, w1], F32R) for k in range(2))
        project_phase(nc, "xl1", f_hi, f_lo, KB, [
            (by_block(g["W1"], j * c1, j * c1 + c1), c1, "parts",
             lambda t, j=j: tuple(x[:, t, j * (c1 + 2):j * (c1 + 2) + c1] for x in (xl_hi, xl_lo)))
            for j in range(heads)])
        ones_phase(nc, "ones1", xl_hi, xl_lo, [j * (c1 + 2) + c1 for j in range(heads)])
        right.close()
        h1 = right_sb("gat_h1", [P, NT, wide])
        aggregate_phase(nc, "agg1", heads, c1, cols, shifts, ctot_dram, xl_hi, xl_lo, h1, g["b1"])
        left.close()
        layer_norm_phase(nc, "ln1", h1, wide, g["g1"], g["be1"], True, [res1], g["br1"])
        f_hi, f_lo = (left_sb(f"gat_g{k}", [P, kb2, NP], F32R) for k in range(2))
        turn_phase(nc, "turn1", h1, kb2, ident, f_hi, f_lo)
        right.close()
        src_rows, shifts = dram("src2", (1, NP)), dram("shifts2", (2, 1, NP))
        logits_phase(nc, "logits2", f_hi, f_lo, kb2, g["w2_t"], g["a_src2"], g["a_dst2"], 1, ident, cols2, src_rows)
        project_phase(nc, "res2", f_hi, f_lo, kb2, [
            (by_block(g["Wr2"], j * 256, j * 256 + 256), 256, "dram",
             lambda t, j=j: res2[t * P:(t + 1) * P, j * 256:j * 256 + 256]) for j in range(D // 256)],
            beside=lambda ph: Maxima(ph, 1, ident, cols2, src_rows, no_edge_dram, shifts))
        xl_hi, xl_lo = (right_sb(f"gat_xm{k}", [P, NT, D + 2], F32R) for k in range(2))

        def past_ones(c):
            return c + (2 if c >= SUM_AT else 0)
        project_phase(nc, "xl2", f_hi, f_lo, kb2, [
            (by_block(g["W2"], c, c + 256), 256, "parts",
             lambda t, c=c: tuple(x[:, t, past_ones(c):past_ones(c) + 256] for x in (xl_hi, xl_lo)))
            for c in range(0, D, 256)])
        ones_phase(nc, "ones2", xl_hi, xl_lo, [SUM_AT])
        left.close()
        rows_ctx = ExitStack()
        rows = rows_ctx.enter_context(nc.sbuf_tensor("gat_rows", [P, NT, D], F32))
        aggregate_phase(nc, "agg2", 1, D, cols2, shifts, ctot_dram, xl_hi, xl_lo, rows, g["b2"])
        right.close()
        layer_norm_phase(nc, "ln2", rows, D, g["g2"], g["be2"], False, [res2, x2], g["br2"])
        return rows, rows_ctx


NE1, RANK = 8, 16
HEADS, HC = 12, 64
LORA_SCALE = 2.0
assert NE1 * RANK == P and HEADS * HC == D


def route_phase(nc, f_hi, f_lo, w_gate_t, b_gate, a_t, down):
    with Phase(nc, "route") as ph:
        W = NE1 + P
        raw = ph.sb("raw", [P, KB, W])
        w_hi, w_lo = ph.sb("w_hi", [P, KB, W], F32R), ph.sb("w_lo", [P, KB, W], F32R)
        bias = ph.sb("bias", [P, NE1])
        logits, probs, equal, first, rest, second, dispatch = (ph.sb(x, [P, NT, NE1]) for x in (
            "logits", "probs", "equal", "first", "rest", "second", "dispatch"))
        top, total, inverse = (ph.sb(x, [P, NT]) for x in ("top", "total", "inverse"))
        free = ph.sb("free", [P, NE1, NT])
        acc = ph.ps("acc", [P, 4, 512])
        loaded, split, multiplied, steps_s, exp_made = (ph.sem(x) for x in (
            "loaded", "split", "multiplied", "steps", "exp_made"))

        def tile(t, c0, c1):
            return acc[:, t // 3, (t % 3) * W + c0:(t % 3) * W + c1]
        with nc.Block() as block:
            @block.sync
            def _(sp):
                sp.dma_start(raw[:, :, 0:NE1], w_gate_t.rearrange("(k p) n -> p k n", p=P)).then_inc(loaded, 16)
                sp.dma_start(raw[:, :, NE1:W], a_t.rearrange("(k p) n -> p k n", p=P)).then_inc(loaded, 16)
                sp.dma_start(bias[:, :], b_gate.partition_broadcast(P)).then_inc(loaded, 16)

            @block.tensor
            def _(pe):
                pe.wait_ge(split, 2)
                f, w = (f_hi, f_lo), (w_hi, w_lo)
                for t in range(NT):
                    for kb in range(KB):
                        for a, b in ((0, 0), (0, 1), (1, 0)):
                            last = pe.matmul(tile(t, 0, W), f[a][:, kb, t * P:(t + 1) * P], w[b][:, kb, :],
                                             start=t % 3 == 0 and kb == 0 and (a, b) == (0, 0), stop=True,
                                             skip_group_check=True)
                last.then_inc(multiplied, 1)

            @block.scalar
            def _(act):
                act.wait_ge(loaded, 48)
                act.activation(w_hi[:, :, :], raw[:, :, :], ACT.Copy).then_inc(split, 1)
                act.wait_ge(steps_s, NT + 2)
                act.activation(probs[:, :, :], logits[:, :, :], ACT.Exp).then_inc(exp_made, 1)

            @block.vector
            def _(v):
                s = Steps(v, steps_s)

                def by_token(a):
                    return a[:, :].unsqueeze(2).to_broadcast([P, NT, NE1])

                def first_of(values, out):
                    s.done(v.tensor_reduce(top[:, :], values[:, :, :], AXX, ALU.max))
                    s.wait()
                    s.done(v.tensor_tensor(equal[:, :, :], values[:, :, :], by_token(top), ALU.is_equal))
                    s.done(v.memset(free[:, 0, :], 1.0))
                    for e in range(NE1):
                        s.wait()
                        s.done(v.tensor_tensor(out[:, :, e], equal[:, :, e], free[:, e, :], ALU.mult))
                        if e + 1 < NE1:
                            s.wait()
                            s.done(v.tensor_tensor(free[:, e + 1, :], free[:, e, :], out[:, :, e], ALU.subtract))
                    s.wait()
                v.wait_ge(split, 1)
                v.tensor_tensor(w_lo[:, :, :], raw[:, :, :], w_hi[:, :, :].bitcast(F32), ALU.subtract)\
                    .then_inc(split, 1)
                v.wait_ge(multiplied, 1)
                for t in range(NT):
                    s.done(v.tensor_tensor(logits[:, t, :], tile(t, 0, NE1), bias[:, :], ALU.add))
                s.wait()
                s.done(v.tensor_reduce(top[:, :], logits[:, :, :], AXX, ALU.max))
                s.wait()
                s.done(v.tensor_tensor(logits[:, :, :], logits[:, :, :], by_token(top), ALU.subtract))
                v.wait_ge(exp_made, 1)
                s.done(v.tensor_reduce(total[:, :], probs[:, :, :], AXX, ALU.add))
                s.wait()
                s.done(v.reciprocal(inverse[:, :], total[:, :]))
                s.wait()
                s.done(v.tensor_tensor(probs[:, :, :], probs[:, :, :], by_token(inverse), ALU.mult))
                s.wait()
                first_of(probs, first)
                s.done(v.scalar_tensor_tensor(out=rest[:, :, :], in0=first[:, :, :], scalar=-2.0, in1=probs[:, :, :],
                                              op0=ALU.mult, op1=ALU.add))
                s.wait()
                first_of(rest, second)
                s.done(v.tensor_tensor(second[:, :, :], second[:, :, :], first[:, :, :], ALU.add))
                s.wait()
                s.done(v.scalar_tensor_tensor(out=dispatch[:, :, :], in0=second[:, :, :], scalar=LORA_SCALE,
                                              in1=probs[:, :, :], op0=ALU.mult, op1=ALU.mult))
                s.wait()
                for t in range(NT):
                    s.done(v.tensor_tensor(down[:, t, :].rearrange("p (n r) -> p n r", r=RANK),
                                           tile(t, NE1, W).rearrange("p (n r) -> p n r", r=RANK),
                                           dispatch[:, t, :].unsqueeze(2).to_broadcast([P, NE1, RANK]), ALU.mult))


def queries_keys_phase(nc, f_hi, f_lo, w_t, b_lora, b_qkv, qk_dram):
    K7, NC, CW, QB = KB + 1, len(CHUNKS), CHUNKS[0][1] * P, 2 * KB
    with Phase(nc, "qk") as ph:
        raw = ph.sb("raw", [P, 2, K7, P])
        w_hi = [ph.sb(f"w_hi{k}", [P, K7, P], F32R) for k in range(2)]
        w_lo = [ph.sb(f"w_lo{k}", [P, K7, P], F32R) for k in range(2)]
        bias = ph.sb("bias", [P, QB])
        value = ph.sb("value", [P, 2, CW])
        hi, lo = ph.sb("hi", [P, 2, NP], F32R), ph.sb("lo", [P, 2, NP], F32R)
        prod = [ph.ps(f"prod{k}", [P, 512]) for k in range(4)]
        bias_in, w_hi_s, w_lo_s, multiplied, value_s, hi_s, lo_s = (ph.sem(x) for x in (
            "bias_in", "w_hi_made", "w_lo_made", "multiplied", "value", "hi", "lo"))
        raw_in = [ph.sem(f"raw_in{k}") for k in range(2)]
        stored = [ph.sem(f"stored{k}") for k in range(2)]
        with nc.Block() as block:
            @block.sync
            def _(sp):
                def load(j):
                    if j >= 2:
                        sp.wait_ge(w_lo_s, j - 1)
                    sp.dma_start(raw[:, j % 2, 0:KB, :], by_block(w_t, j * P, (j + 1) * P)).then_inc(raw_in[j % 2], 16)
                    sp.dma_start(raw[:, j % 2, KB, :], b_lora[:, j * P:(j + 1) * P]).then_inc(raw_in[j % 2], 16)
                sp.dma_start(bias[:, :], b_qkv[0:QB * P].rearrange("(j p) -> p j", p=P),
                             allow_slow_non_contiguous=True).then_inc(bias_in, 16)
                load(0)
                load(1)
                for j in range(QB):
                    sp.wait_ge(lo_s, (j + 1) * NC)
                    rows = slice(j % KB * P, (j % KB + 1) * P)
                    sp.dma_start(qk_dram[j // KB * 2, rows, :], hi[:, j % 2, :].bitcast(F32)).then_inc(stored[j % 2], 16)
                    sp.dma_start(qk_dram[j // KB * 2 + 1, rows, :], lo[:, j % 2, :].bitcast(F32))\
                        .then_inc(stored[j % 2], 16)
                    if j + 2 < QB:
                        load(j + 2)
                for k in range(2):
                    sp.wait_ge(stored[k], QB // 2 * 32)

            @block.tensor
            def _(pe):
                f, w = (f_hi, f_lo), (w_hi, w_lo)
                for j in range(QB):
                    pe.wait_ge(w_lo_s, j + 1)
                    for c, (t0, nt) in enumerate(CHUNKS):
                        i = j * NC + c
                        if i >= 4:
                            pe.wait_ge(value_s, i - 3)
                        for kb in range(K7):
                            for a, b in ((0, 0), (0, 1), (1, 0)):
                                last = pe.matmul(prod[i % 4][:, 0:nt * P], w[a][j % 2][:, kb, :],
                                                 f[b][:, kb, t0 * P:(t0 + nt) * P],
                                                 start=kb == 0 and (a, b) == (0, 0), stop=kb == K7 - 1 and a == 1)
                        last.then_inc(multiplied, 1)

            @block.scalar
            def _(act):
                def weight(j):
                    act.wait_ge(raw_in[j % 2], (j // 2 + 1) * 32)
                    if j >= 2:
                        act.wait_ge(multiplied, (j - 1) * NC)
                    act.activation(w_hi[j % 2][:, :, :], raw[:, j % 2, :, :], ACT.Copy).then_inc(w_hi_s, 1)
                weight(0)
                for j in range(QB):
                    for c, (t0, nt) in enumerate(CHUNKS):
                        i = j * NC + c
                        if c == 1 and j + 1 < QB:
                            weight(j + 1)
                        act.wait_ge(value_s, i + 1)
                        if c == 0 and j >= 2:
                            act.wait_ge(stored[j % 2], j // 2 * 32)
                        act.activation(hi[:, j % 2, t0 * P:(t0 + nt) * P], value[:, i % 2, 0:nt * P], ACT.Copy)\
                            .then_inc(hi_s, 1)

            @block.vector
            def _(v):
                def weight(j):
                    v.wait_ge(w_hi_s, j + 1)
                    v.tensor_tensor(w_lo[j % 2][:, :, :], raw[:, j % 2, :, :], w_hi[j % 2][:, :, :].bitcast(F32),
                                    ALU.subtract).then_inc(w_lo_s, 1)
                v.wait_ge(bias_in, 16)
                weight(0)

                def second(i):
                    j, c = divmod(i, NC)
                    t0, nt = CHUNKS[c]
                    at = slice(t0 * P, (t0 + nt) * P)
                    v.wait_ge(hi_s, i + 1)
                    v.tensor_tensor(lo[:, j % 2, at], value[:, i % 2, 0:nt * P], hi[:, j % 2, at].bitcast(F32),
                                    ALU.subtract).then_inc(lo_s, 1)
                for j in range(QB):
                    for c, (t0, nt) in enumerate(CHUNKS):
                        i = j * NC + c
                        v.wait_ge(multiplied, i + 1)
                        if i >= 2:
                            v.wait_ge(lo_s, i - 1)
                        v.tensor_scalar(value[:, i % 2, 0:nt * P], prod[i % 4][:, 0:nt * P], bias[:, j:j + 1], None,
                                        ALU.add).then_inc(value_s, 1)
                        if i:
                            second(i - 1)
                        if c == 1 and j + 1 < QB:
                            weight(j + 1)
                second(QB * NC - 1)


def attention_phase(nc, qk_dram, v_hi, v_lo, v_bias, ident, out):
    with Phase(nc, "attn") as ph:
        TR = 2 * NT
        KEYS_AT = [(0, 512), (512, 512), (1024, N - 1024)]
        TURN = [(0, 4), (4, 4), (8, 2)]
        q = [ph.sb(f"q{k}", [P, NP], F32R) for k in range(2)]
        k_twice = [ph.sb(f"k_twice{k}", [P, NP], F32R) for k in range(2)]
        k_lo = [ph.sb(f"k_lo{k}", [HC, NP], F32R) for k in range(2)]
        values = [ph.sb(f"values{k}", [P, NT, 2 * HC], F32R) for k in range(2)]
        low_sums = ph.sb("low_sums", [P, 2, HC])
        bias = ph.sb("bias", [P, D])
        largest = ph.sb("largest", [P, 4, 4])
        least = ph.sb("least", [P, 4, 1])
        sums = ph.sb("sums", [P, 4, 3])
        total, inverse = ph.sb("total", [P, 2]), ph.sb("inverse", [P, 2])
        e = [ph.sb(f"e{k}", [P, NP]) for k in range(2)]
        p_hi = [ph.sb(f"p_hi{k}", [P, NT, P], F32R) for k in range(2)]
        p_lo = [ph.sb(f"p_lo{k}", [P, NT, P], F32R) for k in range(2)]
        seed = ph.sb("seed", [1, 16])
        score = [ph.ps(f"score{k}", [P, 512]) for k in range(4)]
        turned = [ph.ps(f"turned{k}", [P, 4, P]) for k in range(3)]
        acc = ph.ps("acc", [P, 512])
        bias_in, scored, piece_s, least_s, exp_s, turned_s = (ph.sem(x) for x in (
            "bias_in", "scored", "piece", "least", "exp", "turned"))
        hi_s, lo_s, summed, total_s, inverse_s, out_s, cleared = (ph.sem(x) for x in (
            "hi", "lo", "summed", "total", "inverse", "out", "cleared"))
        qk_in = [ph.sem(f"qk_in{k}") for k in range(2)]
        values_in = [ph.sem(f"values_in{k}") for k in range(2)]
        FREE = {"scored": 3 * TR, "exp": 6, "turned": 6, "lo": 6, "summed": TR, "out": 3, "least": 3}

        with nc.Block() as block:
            @block.sync
            def _(sp):
                sp.dma_start(bias[:, :], v_bias.partition_broadcast(P)).then_inc(bias_in, 16)
                with sp.Fori(0, HEADS // 2) as g:
                    for u in range(2):
                        rows = bass.ds((g * 2 + u) * HC, HC)
                        sp.wait_ge(scored, g * (3 * TR) + 3 * NT * (u + 1))
                        for dest, plane_ in ((q[u][0:HC], 0), (q[u][HC:P], 1), (k_twice[u][0:HC], 2),
                                             (k_twice[u][HC:P], 2), (k_lo[u][:, :], 3)):
                            sp.dma_start(dest.bitcast(F32), qk_dram[plane_, rows, :]).then_inc(qk_in[u], 16)
                        sp.wait_ge(summed, g * TR + NT * (u + 1))
                        for k, v in enumerate((v_hi, v_lo)):
                            sp.dma_start(values[u][:, :, k * HC:(k + 1) * HC].bitcast(F32),
                                         v[:, :, rows].bitcast(F32)).then_inc(values_in[u], 16)

            @block.gpsimd
            def _(pool):
                pool.memset(seed[:, 0:1], 0.0).then_inc(scored, FREE["scored"])
                pool.memset(seed[:, 1:2], 0.0).then_inc(exp_s, FREE["exp"])
                pool.memset(seed[:, 2:3], 0.0).then_inc(turned_s, FREE["turned"])
                pool.memset(seed[:, 3:4], 0.0).then_inc(lo_s, FREE["lo"])
                pool.memset(seed[:, 4:5], 0.0).then_inc(summed, FREE["summed"])
                pool.memset(seed[:, 5:6], 0.0).then_inc(out_s, FREE["out"])
                pool.memset(seed[:, 6:7], 0.0).then_inc(least_s, FREE["least"])
                for k in range(2):
                    pool.memset(e[k][:, N:NP], 0.0).then_inc(cleared, 1)

            @block.tensor
            def _(pe):
                def scores(g, k):
                    n, u, t = g * TR + k, k % TR // NT, k % NT
                    if t == 0:
                        pe.wait_ge(qk_in[u], (g + k // TR) * 80 + 80)
                    at = slice(t * P, (t + 1) * P)
                    for b, (k0, w) in enumerate(KEYS_AT):
                        bank = score[(3 * k + b) % 4]
                        pe.wait_ge(exp_s, n * 3 + b - 3 + FREE["exp"])
                        pe.matmul(bank[:, 0:w], q[u][:, at], k_twice[u][:, k0:k0 + w], start=True, stop=False)
                        pe.matmul(bank[:, 0:w], q[u][0:HC, at], k_lo[u][:, k0:k0 + w], start=False, stop=True)\
                            .then_inc(scored, 1)

                def turn(g, k):
                    n = g * TR + k
                    pe.wait_ge(exp_s, n * 3 + 3 + FREE["exp"])
                    for b, (s0, ns) in enumerate(TURN):
                        pe.wait_ge(lo_s, n * 3 + b - 2 + FREE["lo"])
                        for s in range(ns):
                            last = pe.transpose(turned[b][:, s, :], e[k % 2][:, (s0 + s) * P:(s0 + s + 1) * P],
                                                ident[:, :])
                        last.then_inc(turned_s, 1)

                def products(g, k):
                    n, u = g * TR + k, k // NT
                    if k % NT == 0:
                        pe.wait_ge(values_in[u], g * 32 + 32)
                    pe.wait_ge(lo_s, n * 3 + 3 + FREE["lo"])
                    pe.wait_ge(out_s, n + FREE["out"])
                    for s in range(NT):
                        pe.matmul(acc[:, 0:2 * HC], p_hi[k % 2][:, s, :], values[u][:, s, :], start=s == 0,
                                  stop=False, skip_group_check=True)
                        last = pe.matmul(acc[:, 0:HC], p_lo[k % 2][:, s, :], values[u][:, s, 0:HC], start=False,
                                         stop=True, skip_group_check=True)
                    last.then_inc(summed, 1)

                def round_(g, more):
                    for k in range(TR):
                        turn(g, k)
                        if k + 2 < TR or more:
                            scores(g, k + 2)
                        if k:
                            products(g, k - 1)
                    products(g, TR - 1)
                pe.wait_ge(cleared, 2)
                scores(0, 0)
                scores(0, 1)
                with pe.Fori(0, HEADS // 2 - 1) as g:
                    round_(g, True)
                round_(HEADS // 2 - 1, False)

            @block.scalar
            def _(act):
                def exponentials(g, k):
                    n = g * TR + k
                    act.wait_ge(least_s, n + 1 + FREE["least"])
                    act.wait_ge(turned_s, n * 3 - 3 + FREE["turned"])
                    act.wait_ge(out_s, n - 3 + FREE["out"])
                    for b, (k0, w) in enumerate(KEYS_AT):
                        act.activation(e[k % 2][:, k0:k0 + w], score[(3 * k + b) % 4][:, 0:w], ACT.Exp,
                                       bias=least[:, k % 4, :], scale=HC ** -0.5,
                                       accum_out=sums[:, k % 4, b:b + 1]).then_inc(exp_s, 1)

                def first_parts(g, k):
                    n = g * TR + k
                    act.wait_ge(summed, n - 1 + FREE["summed"])
                    for b, (s0, ns) in enumerate(TURN):
                        act.wait_ge(turned_s, n * 3 + b + 1 + FREE["turned"])
                        act.activation(p_hi[k % 2][:, s0:s0 + ns, :], turned[b][:, 0:ns, :], ACT.Copy)\
                            .then_inc(hi_s, 1)

                def round_(g, more):
                    for k in range(TR):
                        if k + 1 < TR or more:
                            exponentials(g, k + 1)
                        first_parts(g, k)
                act.wait_ge(cleared, 2)
                exponentials(0, 0)
                with act.Fori(0, HEADS // 2 - 1) as g:
                    round_(g, True)
                round_(HEADS // 2 - 1, False)

            @block.vector
            def _(v):
                def largest_of(g, k, b):
                    n, (k0, w) = g * TR + k, KEYS_AT[b]
                    if b == 0:
                        v.wait_ge(exp_s, n * 3 - 6 + FREE["exp"])
                    v.wait_ge(scored, n * 3 + b + 1 + FREE["scored"])
                    v.tensor_reduce(largest[:, k % 4, b:b + 1], score[(3 * k + b) % 4][:, 0:w], AXX, ALU.max)\
                        .then_inc(piece_s, 1)

                def largest_of_all(g, k):
                    n = g * TR + k
                    v.wait_ge(piece_s, n * 4 + 3)
                    v.tensor_reduce(largest[:, k % 4, 3:4], largest[:, k % 4, 0:3], AXX, ALU.max)\
                        .then_inc(piece_s, 1)

                def least_exponent(g, k):
                    n = g * TR + k
                    v.wait_ge(piece_s, n * 4 + 4)
                    v.tensor_scalar(least[:, k % 4, :], largest[:, k % 4, 3:4], -HC ** -0.5, None, ALU.mult)\
                        .then_inc(least_s, 1)

                def second_part(g, k, b):
                    n, (s0, ns) = g * TR + k, TURN[b]
                    v.wait_ge(hi_s, n * 3 + b + 1)
                    v.tensor_tensor(p_lo[k % 2][:, s0:s0 + ns, :], turned[b][:, 0:ns, :],
                                    p_hi[k % 2][:, s0:s0 + ns, :].bitcast(F32), ALU.subtract).then_inc(lo_s, 1)

                def sum_total(g, k):
                    n = g * TR + k
                    v.wait_ge(exp_s, n * 3 + 3 + FREE["exp"])
                    v.wait_ge(out_s, n - 1 + FREE["out"])
                    v.tensor_reduce(total[:, k % 2:k % 2 + 1], sums[:, k % 4, :], AXX, ALU.add).then_inc(total_s, 1)

                def invert(g, k):
                    n = g * TR + k
                    v.wait_ge(total_s, n + 1)
                    v.reciprocal(inverse[:, k % 2:k % 2 + 1], total[:, k % 2:k % 2 + 1]).then_inc(inverse_s, 1)

                def add_low_sums(g, k):
                    n, h = g * TR + k, g * 2 + k // NT
                    at = bass.ds(h * HC, HC)
                    v.wait_ge(inverse_s, 2 * n + 1)
                    v.wait_ge(summed, n + 1 + FREE["summed"])
                    v.scalar_tensor_tensor(out=low_sums[:, k % 2, :], in0=acc[:, HC:2 * HC],
                                           scalar=inverse[:, k % 2:k % 2 + 1], in1=bias[:, at],
                                           op0=ALU.mult, op1=ALU.add).then_inc(inverse_s, 1)

                def output(g, k):
                    n, h = g * TR + k, g * 2 + k // NT
                    v.wait_ge(inverse_s, 2 * n + 2)
                    v.scalar_tensor_tensor(out=out[:, k % NT, bass.ds(h * HC, HC)], in0=acc[:, 0:HC],
                                           scalar=inverse[:, k % 2:k % 2 + 1], in1=low_sums[:, k % 2, :],
                                           op0=ALU.mult, op1=ALU.add).then_inc(out_s, 1)

                def step(g, k, find, split, finish):
                    def part(tile, work, *args):
                        if tile is not None:
                            work(g, tile, *args)
                    part(find, largest_of, 0)
                    part(finish, sum_total)
                    part(find, largest_of, 1)
                    part(finish, invert)
                    part(find, largest_of, 2)
                    part(split, second_part, 0)
                    part(find, largest_of_all)
                    part(split, second_part, 1)
                    part(find, least_exponent)
                    part(finish, add_low_sums)
                    part(split, second_part, 2)
                    part(finish, output)

                def round_(g, more):
                    for k in range(TR):
                        step(g, k, k + 2 if k + 2 < TR or more else None, k, k - 1 if k else None)
                    step(g, TR, None, None, TR - 1)
                v.wait_ge(bias_in, 16)
                step(0, 0, 0, None, None)
                step(0, 0, 1, None, None)
                with v.Fori(0, HEADS // 2 - 1) as g:
                    round_(g, True)
                round_(HEADS // 2 - 1, False)


def finish_phase(nc, rows, row, out):
    with Phase(nc, "finish") as ph:
        bias = ph.sb("bias", [P, D])
        loaded, summed, stored = ph.sem("loaded"), ph.sem("summed"), ph.sem("stored")
        with nc.Block() as block:
            @block.sync
            def _(sp):
                sp.dma_start(bias[:, :], row.partition_broadcast(P)).then_inc(loaded, 16)
                for t in range(NT):
                    sp.wait_ge(summed, t + 1)
                    n = P if t < NT - 1 else LAST
                    sp.dma_start(out[t * P:t * P + n, :], rows[0:n, t, :]).then_inc(stored, 16)
                sp.wait_ge(stored, NT * 16)

            @block.vector
            def _(v):
                v.wait_ge(loaded, 16)
                for t in range(NT):
                    v.tensor_tensor(rows[:, t, :], rows[:, t, :], bias[:, :], ALU.add).then_inc(summed, 1)


def attention_layer(nc, rows, rows_ctx, w_qkv_t, b_qkv, w_gate_t, b_gate, a_t, b_lora, w_proj_t, b_proj, ident, out):
    x3 = nc.dram_tensor("attn_x", (NP, D), F32, kind="Internal").ap()
    qk_dram = nc.dram_tensor("attn_qk", (4, D, NP), F32, kind="Internal").ap()
    left, right = ExitStack(), ExitStack()
    right_sb = lambda name, shape, dt=F32: right.enter_context(nc.sbuf_tensor(name, shape, dt, side="right"))
    left_sb = lambda name, shape, dt=F32: left.enter_context(nc.sbuf_tensor(name, shape, dt))
    f_hi, f_lo = (right_sb(f"attn_f{k}", [P, KB + 1, NP], F32R) for k in range(2))
    norm_phase(nc, "attn_norm", rows, ident, features=(f_hi, f_lo), keep=x3)
    rows_ctx.close()
    with nc.sbuf_tensor("attn_down", [P, NT, P], F32) as down:
        route_phase(nc, f_hi, f_lo, w_gate_t, b_gate, a_t, down)
        turn_phase(nc, "turn_down", down, 1, ident, f_hi, f_lo, at=KB)
    queries_keys_phase(nc, f_hi, f_lo, w_qkv_t, b_lora, b_qkv, qk_dram)
    v_hi, v_lo = (left_sb(f"attn_v{k}", [P, NT, D], F32R) for k in range(2))
    project_phase(nc, "values", f_hi, f_lo, KB + 1, [
        ([(by_block(w_qkv_t, 2 * D + c0, 2 * D + c0 + 256), 0, KB),
          (b_lora[:, 2 * D + c0:2 * D + c0 + 256].rearrange("(k p) n -> p k n", p=P), KB, KB + 1)], 256, "parts",
         lambda t, c0=c0: tuple(x[:, t, c0:c0 + 256] for x in (v_hi, v_lo))) for c0 in range(0, D, 256)])
    right.close()
    attended = right_sb("attended", [P, NT, D])
    attention_phase(nc, qk_dram, v_hi, v_lo, b_qkv[2 * D:3 * D], ident, attended)
    left.close()
    g_hi, g_lo = (left_sb(f"attn_g{k}", [P, KB, NP], F32R) for k in range(2))
    turn_phase(nc, "turn_attended", attended, KB, ident, g_hi, g_lo)
    right.close()
    rows = right_sb("attn_rows", [P, NT, D])
    rows_phase(nc, "back3", rows, x3, False)
    project_phase(nc, "proj", g_hi, g_lo, KB, [
        (by_block(w_proj_t, c0, c0 + HD), HD, "add", lambda t, c0=c0: rows[:, t, c0:c0 + HD])
        for c0 in range(0, D, HD)])
    left.close()
    finish_phase(nc, rows, b_proj, out)
    right.close()


def identity_phase(nc, ident, ident_r):
    with Phase(nc, "identity") as ph:
        made = ph.sem("made")
        ones = ph.sb("ones", [P, P])
        with nc.Block() as block:
            @block.gpsimd
            def _(pool):
                pool.memset(ones[:, :], 1.0).then_inc(made, 1)
                pool.wait_ge(made, 1)
                pool.affine_select(out=ident[:, :], in_=ones[:, :], pattern=[[-1, P]], compare_op=ALU.is_equal,
                                   fill=0.0, base=0, channel_multiplier=1).then_inc(made, 1)

            @block.vector
            def _(v):
                v.wait_ge(made, 2)
                v.tensor_copy(ident_r[:, :], ident[:, :])


def build(nc, a, out):
    def dram(name, shape):
        return nc.dram_tensor(name, shape, F32, kind="Internal").ap()
    edge_dram, c_dram = dram("edge_records", (EP * 4,)), dram("edge_counts", (2 * PLANES, NP, NP))
    counts, inv_dram = dram("in_degrees", (PLANES, NP)), dram("inverse_degrees", (R, NP))
    ctot_dram, no_edge_dram = dram("counts_with_loops", (NP, NP)), dram("no_edge", (NP, NP))
    with ExitStack() as ctx:
        sb = lambda c, name, shape, dt=F32: c.enter_context(nc.sbuf_tensor(name, shape, dt))
        ident, ident_r = sb(ctx, "ident", [P, P]), sb(ctx, "ident_r", [P, P], F32R)
        flag = sb(ctx, "flag", [1, 1], I32)
        pool_loads = [ctx.enter_context(nc.semaphore(f"pool_load{k}")) for k in range(8)]
        identity_phase(nc, ident, ident_r)
        with nc.sbuf_tensor("starts", [1, BLOCKS], I32) as starts:
            edges_phase(nc, a["src"], a["dst"], a["edge_type_8"], edge_dram, starts, flag)
            adjacency_phase(nc, edge_dram, starts, flag, c_dram, counts)
        whole_adjacency_phase(nc, edge_dram, flag, c_dram, counts)
        inverses_phase(nc, counts, inv_dram)
        loops_phase(nc, c_dram, ident, ctot_dram, no_edge_dram)
        add_low_phase(nc, flag, c_dram, ctot_dram)
        rows_ctx = ExitStack()
        rows = sb(rows_ctx, "rows", [P, NT, D])
        load_rows(nc, a["x"], rows)
        with ExitStack() as parts:
            t_hi, t_lo = (sb(parts, f"x_part{k}", [P, NT, D], F32R) for k in range(2))
            norm_phase(nc, "norm1", rows, ident, tokens=(t_hi, t_lo))
            rgcn_phase(nc, "rgcn1", t_hi, t_lo, rows, a["L0_gnn_W1"], a["L0_gnn_root1"], c_dram, inv_dram, ident_r, flag,
                       pool_loads[0:4])
            relu_phase(nc, "relu", rows, a["L0_gnn_b1"], t_hi, t_lo)
            rgcn_phase(nc, "rgcn2", t_hi, t_lo, rows, a["L0_gnn_W2"], a["L0_gnn_root2"], c_dram, inv_dram, ident_r, flag,
                       pool_loads[4:8])
        load_rows(nc, a["x"], rows, row=a["L0_gnn_b2"])
        with ExitStack() as parts:
            f_hi, f_lo = (sb(parts, f"f_part{k}", [P, KB, NP], F32R) for k in range(2))
            norm_phase(nc, "norm2", rows, ident, features=(f_hi, f_lo))
            experts_phase(nc, f_hi, f_lo, rows, *(a[f"L0_ffn_{k}"] for k in ("Wg", "bg", "W1", "b1", "W2", "b2")))
        gat = {name[len("L1_gnn_"):]: v for name, v in a.items() if name.startswith("L1_gnn_")}
        gat["w1_t"], gat["w2_t"] = a["gat_w1_t"], a["gat_w2_t"]
        rows, rows_ctx = gat_layers(nc, rows, rows_ctx, gat, ident, ctot_dram, no_edge_dram)
        attention_layer(nc, rows, rows_ctx, a["w_qkv_t"], a["L1_ffn_b_qkv"], a["w_gate_t"], a["L1_ffn_b_gate"],
                        a["a_t"], a["b_lora_t"], a["w_proj_t"], a["L1_ffn_b_proj"], ident, out)


def kernel(**inputs):
    import numpy as np
    import concourse.bacc as bacc
    from concourse.bass_utils import run_bass_kernel_spmd

    arrays = {name: np.asarray(v) for name, v in inputs.items()}
    arrays["w_qkv_t"] = arrays.pop("L1_ffn_W_qkv").T
    arrays["w_proj_t"] = arrays.pop("L1_ffn_W_proj").T
    arrays["w_gate_t"] = arrays.pop("L1_ffn_W_gate").T
    arrays["a_t"] = arrays.pop("L1_ffn_A").reshape(NE1 * RANK, D).T
    arrays["b_lora_t"] = arrays.pop("L1_ffn_B_lora").transpose(0, 2, 1).reshape(NE1 * RANK, 3 * D)
    arrays["gat_w1_t"], arrays["gat_w2_t"] = arrays["L1_gnn_W1"].T, arrays["L1_gnn_W2"].T
    arrays = {name: np.ascontiguousarray(v) for name, v in arrays.items()}
    nc = bacc.Bacc("TRN2", target_bir_lowering=False, num_devices=1)
    a = {name: nc.dram_tensor(name, v.shape, mybir.dt.from_np(v.dtype), kind="ExternalInput").ap()
         for name, v in arrays.items()}
    out = nc.dram_tensor("out", (N, D), F32, kind="ExternalOutput").ap()
    build(nc, a, out)
    return run_bass_kernel_spmd(nc, [arrays], core_ids=[0]).results[0]["out"]
```

```python
from contextlib import ExitStack, contextmanager

import concourse.bass as bass
from concourse import mybir

ALU = mybir.AluOpType
ACT = mybir.ActivationFunctionType
AXX = mybir.AxisListType.X
F32, F32R, F16, I32 = mybir.dt.float32, mybir.dt.float32r, mybir.dt.float16, mybir.dt.int32

P = 128
N = 1250
NT = -(-N // P)
NP = NT * P
LAST = N - (NT - 1) * P
D = 768
KB = D // P
HD = D // 2
R = 8
E = 40000
CHUNKS = [(0, 4), (4, 4), (8, 2)]
EPS = 1e-5

NODES_PER_BLOCK = 16
BLOCKS = NP // NODES_PER_BLOCK
PLANES = R + 1
COLS = PLANES * NODES_PER_BLOCK
KEYS = R * NODES_PER_BLOCK
EC = 5
GROUP = EC * P
ER = 320
EP = P * ER
ALL_GROUPS = -(-E // GROUP)
KEY = 2048
BPG = P // NODES_PER_BLOCK
assert E % ER == 0 and E // ER < P and N < KEY and ALL_GROUPS * GROUP <= EP


class Phase:

    def __init__(self, nc, name):
        self.nc, self.name, self.ctx, self.sems = nc, name, ExitStack(), []

    def __enter__(self):
        return self

    def sb(self, name, shape, dt=F32):
        return self.ctx.enter_context(self.nc.sbuf_tensor(f"{self.name}_{name}", shape, dt))

    def ps(self, name, shape, dt=F32):
        return self.ctx.enter_context(self.nc.psum_tensor(f"{self.name}_{name}", shape, dt))

    def sem(self, name):
        s = self.ctx.enter_context(self.nc.semaphore(f"{self.name}_{name}"))
        self.sems.append(s)
        return s

    def __exit__(self, *exc):
        if exc[0] is None:
            with self.nc.Block() as block:
                @block.gpsimd
                def _(pool):
                    for s in self.sems:
                        pool.sem_clear(s)
        self.ctx.close()


class Steps:

    def __init__(self, engine, sem):
        self.engine, self.sem, self.n = engine, sem, 0

    def done(self, instruction):
        instruction.then_inc(self.sem, 1)
        self.n += 1
        return self.n

    def wait(self, base=0):
        self.engine.wait_ge(self.sem, base + self.n)


def edges_phase(nc, src, dst, etype, edge_dram, starts, flag):
    rows = E // ER
    with Phase(nc, "edges") as ph:
        raw = ph.sb("raw", [P, 3, ER], I32)
        nxt = ph.sb("next", [P, ER], I32)
        fl = ph.sb("float", [P, 3, ER])
        nfl = ph.sb("nextf", [P, ER])
        rec = ph.sb("rec", [P, ER, 4])
        below = ph.sb("below", [P, BLOCKS + 2])
        junk = ph.sb("junk", [P, 2, ER], F16)
        ends = ph.sb("ends", [P, ER], F16)
        ones = ph.sb("ones", [P, P])
        row = ph.sb("row", [1, BLOCKS + 2])
        width = ph.sb("width", [1, BLOCKS])
        few = ph.sb("few", [1, 8])
        total = ph.ps("total", [P, BLOCKS + 2])
        loaded, zeroed, dve, summed, stored = (ph.sem(x) for x in ("loaded", "zeroed", "dve", "summed", "stored"))
        ready = ph.sem("records")
        with nc.Block() as block:
            @block.sync
            def _(sp):
                for k, a in enumerate((src, dst, etype)):
                    sp.dma_start(raw[0:rows, k, :], a.rearrange("(p n) -> p n", n=ER)).then_inc(loaded, 16)
                sp.wait_ge(zeroed, 1)
                sp.dma_start(nxt[0:rows - 1, :],
                             dst[1:1 + (rows - 1) * ER].rearrange("(p n) -> p n", n=ER)).then_inc(loaded, 16)
                sp.dma_start(nxt[rows - 1:rows, 0:ER - 1],
                             dst[1 + (rows - 1) * ER:E].rearrange("(p n) -> p n", p=1)).then_inc(loaded, 16)
                sp.wait_ge(ready, 1)
                sp.dma_start(edge_dram.rearrange("(p n) -> p n", p=P),
                             rec[:, :, :].rearrange("p n c -> p (n c)")).then_inc(stored, 16)
                sp.wait_ge(stored, 16)

            @block.vector
            def _(dve_):
                v, s = dve_, Steps(dve_, dve)
                v.memset(nxt[:, :], NP).then_inc(zeroed, 1)
                s.done(v.memset(rec[:, :, :], -1.0))
                s.done(v.memset(ones[:, :], 1.0))
                s.done(v.memset(below[:, :], 0.0))
                v.wait_ge(loaded, 80)
                s.done(v.tensor_copy(fl[0:rows, :, :], raw[0:rows, :, :]))
                s.done(v.tensor_copy(ends[0:rows, :], raw[0:rows, 1, :]))
                s.done(v.tensor_copy(nfl[0:rows, :], nxt[0:rows, :]))
                s.wait()
                s.done(v.tensor_copy(rec[0:rows, :, 0], fl[0:rows, 0, :]))
                s.done(v.tensor_copy(rec[0:rows, :, 2], fl[0:rows, 1, :]))
                v.scalar_tensor_tensor(out=rec[0:rows, :, 1], in0=fl[0:rows, 2, :], scalar=float(KEY),
                                       in1=fl[0:rows, 1, :], op0=ALU.mult, op1=ALU.add).then_inc(ready, 1)
                for b in range(BLOCKS + 1):
                    if b >= 2:
                        v.wait_ge(dve, s.n - 1)
                    s.done(v.tensor_scalar(junk[0:rows, b % 2, :], ends[0:rows, :], float(b * NODES_PER_BLOCK),
                                           0.0, ALU.is_lt, ALU.add, accum_out=below[0:rows, b:b + 1]))
                s.wait()
                s.done(v.tensor_tensor(junk[0:rows, 0, :], nfl[0:rows, :], fl[0:rows, 1, :], ALU.is_lt))
                s.wait()
                s.done(v.tensor_reduce(below[0:rows, BLOCKS + 1:BLOCKS + 2], junk[0:rows, 0, :], AXX, ALU.add))
                v.wait_ge(summed, 1)
                s.done(v.tensor_copy(row[:, :], total[0:1, :]))
                s.wait()
                s.done(v.tensor_tensor(width[:, :], row[:, 1:BLOCKS + 1], row[:, 0:BLOCKS], ALU.subtract))
                s.wait()
                s.done(v.tensor_reduce(few[:, 0:1], width[:, :], AXX, ALU.max))
                s.wait()
                s.done(v.tensor_scalar(few[:, 1:2], few[:, 0:1], float(GROUP), None, ALU.is_gt))
                s.done(v.tensor_scalar(few[:, 2:3], row[:, BLOCKS + 1:BLOCKS + 2], 0.0, None, ALU.is_gt))
                s.wait()
                s.done(v.tensor_tensor(few[:, 3:4], few[:, 1:2], few[:, 2:3], ALU.max))
                s.wait()
                s.done(v.tensor_scalar(few[:, 4:5], few[:, 3:4], -1.0, 1.0, ALU.mult, ALU.add))
                s.done(v.tensor_copy(flag[:, :], few[:, 3:4]))
                s.wait()
                s.done(v.tensor_scalar(starts[:, :], row[:, 0:BLOCKS], few[:, 4:5], None, ALU.mult))

            @block.tensor
            def _(pe):
                pe.wait_ge(dve, BLOCKS + 11)
                pe.matmul(total[:, :], ones[0:rows, :], below[0:rows, :], start=True, stop=True).then_inc(summed, 1)


def plane(r, part):
    return part * R + r if r < R else 2 * R + part


def where_flag(engine, flag, run, wanted):
    found = engine.value_load(flag[0:1, 0:1], min_val=0, max_val=1)
    with engine.If(found > 0 if wanted else found < 1):
        run()
        engine.nop()


def hot_column_row(pool, out, ids, record):
    pool.tensor_scalar(out[:, 0:KEYS], ids[:, 0:KEYS], record[:, 1:2], None, ALU.is_equal)
    return pool.tensor_scalar(out[:, KEYS:COLS], ids[:, KEYS:COLS], record[:, 2:3], None, ALU.is_equal)


def count_products(pe, acc, source, column, ones, first):
    for m in range(NT):
        pe.matmul(acc[:, m // 3, (m % 3) * COLS:(m % 3 + 1) * COLS], source[:, m * P:(m + 1) * P], column,
                  start=first and m % 3 == 0, stop=True, skip_group_check=True)
    return pe.matmul(acc[:, 3, COLS:2 * COLS], ones[:, :], column, start=False, stop=True,
                     skip_group_check=True)


def count_banks(acc):
    for bank in range(4):
        m0, m1 = 3 * bank, min(3 * bank + 3, NT)
        yield m0, m1, acc[:, bank, 0:(m1 - m0) * COLS].rearrange("p (m c) -> p m c", c=COLS)


def make_ids(pool, s, source_ids, ids, ones, step):
    s.done(pool.iota(source_ids[:, :], pattern=[[1, NP]], base=0, channel_multiplier=0,
                     allow_small_or_imprecise_dtypes=True))
    s.done(pool.iota(ids[:, 0, 0:KEYS], pattern=[[KEY, R], [1, NODES_PER_BLOCK]], base=0,
                     channel_multiplier=0, allow_small_or_imprecise_dtypes=True))
    s.done(pool.iota(ids[:, 0, KEYS:COLS], pattern=[[1, NODES_PER_BLOCK]], base=0,
                     channel_multiplier=0, allow_small_or_imprecise_dtypes=True))
    s.done(pool.memset(ones[:, :], 1.0))
    s.done(pool.memset(step[:, :], float(NODES_PER_BLOCK)))
    s.wait()


def adjacency_phase(nc, edge_dram, starts, flag, c_dram, counts):
    with Phase(nc, "adj") as ph:
        NREC, NHOT = 4, 4
        ROUND = 2 * BPG
        rec = ph.sb("rec", [P, NREC, EC, 4])
        source_ids = ph.sb("source_ids", [P, NP], F16)
        ids = ph.sb("ids", [P, 2, COLS])
        hot_source = ph.sb("hot_source", [P, NHOT, NP], F16)
        hot_column = ph.sb("hot_column", [P, NHOT, COLS], F16)
        ones = ph.sb("ones", [P, P], F16)
        step = ph.sb("step", [P, 1])
        stage = [ph.sb(f"stage{k}", [P, NT, PLANES, P], F32R) for k in range(2)]
        count = ph.sb("count", [1, 2, PLANES, P])
        seed = ph.sb("seed", [1, 16])
        acc = [ph.ps(f"acc{k}", [P, 4, 512]) for k in range(2)]
        rec_loaded = [ph.sem(f"rec{k}_loaded") for k in range(NREC)]
        pool_done, ids_made, source_made, column_made, products_done = (ph.sem(x) for x in (
            "pool_done", "ids_made", "source_made", "column_made", "products_done"))
        block_taken = ph.sem("block_taken")
        stage_stored = [ph.sem(f"stage{k}_stored") for k in range(2)]
        rounds = BLOCKS // ROUND
        assert rounds * ROUND == BLOCKS and ROUND * EC % NHOT == 0 and ROUND % NREC == 0

        with nc.Block() as block:
            @block.sync
            def _(sp):
                def run():
                    with sp.Fori(0, rounds) as g:
                        for j in range(ROUND):
                            b = g * ROUND + j
                            sp.wait_ge(source_made, b * EC + 1)
                            sp.wait_ge(column_made, b * EC + 1)
                            sp.nop(nofuse=True)
                            start = sp.value_load(starts[0:1, bass.ds(b, 1)], min_val=0, max_val=E)
                            sp.dma_start(rec[:, j % NREC, :, :].rearrange("p a b -> p (a b)"),
                                         edge_dram[bass.ds(start * 4, GROUP * 4)].rearrange("(p n) -> p n", p=P))\
                                .then_inc(rec_loaded[j % NREC], 16)
                where_flag(sp, flag, run, False)

            @block.gpsimd
            def _(pool):
                def run():
                    make_ids(pool, Steps(pool, pool_done), source_ids, ids, ones, step)
                    pool.memset(seed[:, 0:1], 0.0).then_inc(ids_made, 2)
                    pool.memset(seed[:, 1:2], 0.0).then_inc(column_made, (NREC - 1) * EC + 1)
                    with pool.Fori(0, rounds) as g:
                        for j in range(ROUND):
                            b, k = g * ROUND + j, j % 2
                            pool.wait_ge(rec_loaded[j % NREC], g * (ROUND // NREC * 16) + (j // NREC + 1) * 16)
                            pool.wait_ge(ids_made, b + 2)
                            for c in range(EC):
                                pool.wait_ge(products_done, b * EC + c + 1)
                                pool.nop(nofuse=True)
                                pool.tensor_scalar(hot_column[:, (j * EC + c) % NHOT, KEYS:COLS], ids[:, k, KEYS:COLS],
                                                   rec[:, j % NREC, c, 2:3], None, ALU.is_equal)\
                                    .then_inc(column_made, 1)
                            pool.wait_ge(column_made, b * EC + (NREC - 1) * EC + 1)
                            pool.wait_ge(source_made, b * EC + (NREC - 1) * EC + 1)
                            pool.tensor_tensor(ids[:, 1 - k, :], ids[:, k, :], step[:, :].to_broadcast([P, COLS]),
                                               ALU.add).then_inc(ids_made, 1)
                where_flag(pool, flag, run, False)

            @block.vector
            def _(v):
                def run():
                    v.memset(seed[:, 3:4], 0.0).then_inc(source_made, (NREC - 1) * EC + 1)
                    v.wait_ge(pool_done, 5)
                    with v.Fori(0, rounds) as g:
                        for j in range(ROUND):
                            b = g * ROUND + j
                            v.wait_ge(ids_made, b + 2)
                            v.wait_ge(rec_loaded[j % NREC], g * (ROUND // NREC * 16) + (j // NREC + 1) * 16)
                            for c in range(EC):
                                v.wait_ge(products_done, b * EC + c + 1)
                                v.tensor_scalar(hot_column[:, (j * EC + c) % NHOT, 0:KEYS], ids[:, j % 2, 0:KEYS],
                                                rec[:, j % NREC, c, 1:2], None, ALU.is_equal)
                                v.tensor_scalar(hot_source[:, (j * EC + c) % NHOT, :], source_ids[:, :],
                                                rec[:, j % NREC, c, 0:1], None, ALU.is_equal)\
                                    .then_inc(source_made, 1)
                where_flag(v, flag, run, False)

            @block.tensor
            def _(pe):
                def run():
                    pe.wait_ge(pool_done, 5)
                    with pe.Fori(0, rounds) as g:
                        for j in range(ROUND):
                            b = g * ROUND + j
                            pe.wait_ge(block_taken, b + 1)
                            for c in range(EC):
                                slot = (j * EC + c) % NHOT
                                pe.wait_ge(source_made, b * EC + (NREC - 1) * EC + c + 2)
                                pe.wait_ge(column_made, b * EC + (NREC - 1) * EC + c + 2)
                                count_products(pe, acc[j % 2], hot_source[:, slot, :], hot_column[:, slot, :],
                                               ones, c == 0).then_inc(products_done, 1)
                where_flag(pe, flag, run, False)

            @block.scalar
            def _(act):
                def run():
                    act.activation(seed[:, 8:9], flag[:, :].bitcast(F32), ACT.Copy).then_inc(products_done, NHOT)
                    act.activation(seed[:, 9:10], flag[:, :].bitcast(F32), ACT.Copy).then_inc(block_taken, 2)
                    for h in range(2):
                        act.activation(seed[:, 10 + h:11 + h], flag[:, :].bitcast(F32), ACT.Copy)\
                            .then_inc(stage_stored[h], (PLANES + 1) * 16)
                    with act.Fori(0, rounds) as g:
                        for j in range(ROUND):
                            b, h = g * ROUND + j, j // BPG
                            nodes = bass.ts(j % BPG, NODES_PER_BLOCK)
                            act.wait_ge(products_done, b * EC + NHOT + EC)
                            if j % BPG == 0:
                                act.wait_ge(stage_stored[h], (g + 1) * ((PLANES + 1) * 16))
                            for m0, m1, lot in count_banks(acc[j % 2]):
                                act.activation(stage[h][:, m0:m1, :, nodes],
                                               lot.rearrange("p m (r n) -> p m r n", r=PLANES), ACT.Copy)
                            act.activation(count[:, h, :, nodes],
                                           acc[j % 2][0:1, 3, COLS:2 * COLS].rearrange("p (r n) -> p r n", r=PLANES),
                                           ACT.Copy).then_inc(block_taken, 1)
                            if j % BPG == BPG - 1:
                                act.wait_ge(block_taken, b + 3)
                                to = bass.ds((g * 2 + h) * P, P)
                                for r in range(PLANES):
                                    act.dma_start(c_dram[plane(r, 0)].rearrange("(m p) d -> p m d", p=P)[:, :, to],
                                                  stage[h][:, :, r, :].bitcast(F32)).then_inc(stage_stored[h], 16)
                                act.dma_start(counts[:, to].rearrange("(a r) d -> a r d", a=1),
                                              count[:, h, :, :]).then_inc(stage_stored[h], 16)
                    for h in range(2):
                        act.wait_ge(stage_stored[h], (rounds + 1) * ((PLANES + 1) * 16))
                where_flag(act, flag, run, False)


def whole_adjacency_phase(nc, edge_dram, flag, c_dram, counts):
    with Phase(nc, "whole") as ph:
        rec = ph.sb("rec", [P, EC, 4])
        source_ids = ph.sb("source_ids", [P, NP], F16)
        ids = ph.sb("ids", [P, 1, COLS])
        source = ph.sb("source", [P, EC, NP], F16)
        column = ph.sb("column", [P, EC, COLS], F16)
        ones = ph.sb("ones", [P, P], F16)
        step = ph.sb("step", [P, 1])
        zeros = ph.sb("zeros", [P, P], F16)
        hi = ph.sb("hi", [P, NT, COLS], F32R)
        lo = ph.sb("lo", [P, NT, COLS], F32R)
        count = ph.sb("count", [1, COLS])
        seed = ph.sb("seed", [1, 16])
        acc = ph.ps("acc", [P, 4, 512])
        pool_done, loaded, source_made, column_made, group_done, begun = (ph.sem(x) for x in (
            "pool_done", "loaded", "source_made", "column_made", "group_done", "begun"))
        hi_made, lo_made, stored = (ph.sem(x) for x in ("hi_made", "lo_made", "stored"))
        STORES = 2 * PLANES + 1
        with nc.Block() as block:
            @block.sync
            def _(sp):
                def run():
                    with sp.Fori(0, BLOCKS) as b:
                        with sp.Fori(0, ALL_GROUPS) as q:
                            sp.wait_ge(group_done, b * ALL_GROUPS + q + 1)
                            sp.dma_start(rec[:, :, :].rearrange("p a b -> p (a b)"),
                                         edge_dram[bass.ds(q * (GROUP * 4), GROUP * 4)]
                                         .rearrange("(p n) -> p n", p=P)).then_inc(loaded, 16)
                        sp.wait_ge(hi_made, b + 1)
                        sp.wait_ge(lo_made, b + 1)
                        to = bass.ds(b * NODES_PER_BLOCK, NODES_PER_BLOCK)
                        for r in range(PLANES):
                            for k, part in enumerate((hi, lo)):
                                sp.dma_start(c_dram[plane(r, k)].rearrange("(m p) d -> p m d", p=P)[:, :, to],
                                             part[:, :, bass.ts(r, NODES_PER_BLOCK)].bitcast(F32)).then_inc(stored, 16)
                        sp.dma_start(counts[:, to].rearrange("(a r) d -> a r d", a=1),
                                     count[:, :].rearrange("a (r d) -> a r d", r=PLANES)).then_inc(stored, 16)
                    sp.wait_ge(stored, BLOCKS * STORES * 16)
                where_flag(sp, flag, run, True)

            @block.gpsimd
            def _(pool):
                def run():
                    make_ids(pool, Steps(pool, pool_done), source_ids, ids, ones, step)
                    pool.memset(zeros[:, :], 0.0).then_inc(group_done, 1)
                    with pool.Fori(0, BLOCKS) as b:
                        with pool.Fori(0, ALL_GROUPS) as q:
                            pool.wait_ge(loaded, (b * ALL_GROUPS + q + 1) * 16)
                            pool.nop(nofuse=True)
                            for c in range(EC):
                                hot_column_row(pool, column[:, c, :], ids[:, 0, :], rec[:, c, :])\
                                    .then_inc(column_made, 1)
                        pool.wait_ge(column_made, (b + 1) * (ALL_GROUPS * EC) + b)
                        pool.tensor_tensor(ids[:, 0, :], ids[:, 0, :], step[:, :].to_broadcast([P, COLS]),
                                           ALU.add).then_inc(column_made, 1)
                        pool.wait_ge(column_made, (b + 1) * (ALL_GROUPS * EC + 1))
                where_flag(pool, flag, run, True)

            @block.vector
            def _(v):
                def run():
                    v.wait_ge(pool_done, 5)
                    with v.Fori(0, BLOCKS) as b:
                        with v.Fori(0, ALL_GROUPS) as q:
                            v.wait_ge(loaded, (b * ALL_GROUPS + q + 1) * 16)
                            for c in range(EC):
                                v.tensor_scalar(source[:, c, :], source_ids[:, :], rec[:, c, 0:1], None,
                                                ALU.is_equal).then_inc(source_made, 1)
                        v.wait_ge(hi_made, b + 1)
                        for m0, m1, lot in count_banks(acc):
                            last = v.tensor_tensor(lo[:, m0:m1, :], lot, hi[:, m0:m1, :].bitcast(F32), ALU.subtract)
                        last.then_inc(lo_made, 1)
                where_flag(v, flag, run, True)

            @block.tensor
            def _(pe):
                def run():
                    pe.wait_ge(pool_done, 5)
                    pe.wait_ge(group_done, 1)
                    with pe.Fori(0, BLOCKS) as b:
                        pe.wait_ge(begun, b + 1)
                        for bank in range(4):
                            pe.matmul(acc[:, bank, 0:P], zeros[:, :], zeros[:, :], start=True, stop=True,
                                      skip_group_check=True)
                        with pe.Fori(0, ALL_GROUPS) as q:
                            pe.wait_ge(source_made, (b * ALL_GROUPS + q + 1) * EC)
                            pe.wait_ge(column_made, (b * ALL_GROUPS + q + 1) * EC + b)
                            for c in range(EC):
                                last = count_products(pe, acc, source[:, c, :], column[:, c, :], ones, False)
                            last.then_inc(group_done, 1)
                where_flag(pe, flag, run, True)

            @block.scalar
            def _(act):
                def run():
                    act.activation(seed[:, 8:9], flag[:, :].bitcast(F32), ACT.Copy).then_inc(begun, 1)
                    with act.Fori(0, BLOCKS) as b:
                        act.wait_ge(group_done, (b + 1) * ALL_GROUPS + 1)
                        for m0, m1, lot in count_banks(acc):
                            act.activation(hi[:, m0:m1, :], lot, ACT.Copy)
                        act.activation(count[:, :], acc[0:1, 3, COLS:2 * COLS], ACT.Copy).then_inc(hi_made, 1)
                        act.wait_ge(lo_made, b + 1)
                        act.wait_ge(stored, (b + 1) * (STORES * 16))
                        act.activation(seed[:, 9:10], flag[:, :].bitcast(F32), ACT.Copy).then_inc(begun, 1)
                where_flag(act, flag, run, True)


def inverses_phase(nc, counts, inv_dram):
    with Phase(nc, "inv") as ph:
        count = ph.sb("count", [R * NT, P])
        least = ph.sb("least", [R * NT, P])
        inverse = ph.sb("inverse", [R * NT, P])
        loaded, made, stored = ph.sem("loaded"), ph.sem("made"), ph.sem("stored")
        with nc.Block() as block:
            @block.sync
            def _(sp):
                sp.dma_start(count[:, :], counts[0:R, :].rearrange("r (t d) -> (r t) d", d=P)).then_inc(loaded, 16)
                sp.wait_ge(made, 2)
                sp.dma_start(inv_dram.rearrange("r (t d) -> (r t) d", d=P), inverse[:, :]).then_inc(stored, 16)
                sp.wait_ge(stored, 16)

            @block.vector
            def _(v):
                v.wait_ge(loaded, 16)
                v.tensor_scalar(least[:, :], count[:, :], 1.0, None, ALU.max).then_inc(made, 1)
                v.wait_ge(made, 1)
                v.reciprocal(inverse[:, :], least[:, :]).then_inc(made, 1)


def norm_phase(nc, name, x, ident, tokens=None, features=None, keep=None, load=None,
               after=None):
    with Phase(nc, name) as ph:
        kept = ph.sem("kept")
        stats = ph.sb("stats", [P, NT, 2, 6])
        moments = ph.sb("moments", [P, NT, 2])
        eps = ph.sb("eps", [P, 1])
        dev = ph.sb("dev", [P, NT])
        inv = ph.sb("inv", [P, NT])
        xn = ph.sb("xn", [P, 2, D])
        turned = [ph.ps(f"turned{k}", [P, 4, P]) for k in range(4)] if features else None
        v_s, dev_made, normed, turned_s, hi_made, lo_made = (ph.sem(x) for x in (
            "vector", "dev_made", "normed", "turned", "hi_made", "lo_made"))
        cleared = ph.sem("cleared")
        loaded = [ph.sem(f"loaded{k}") for k in range(NT // 2)] if load is not None else None

        def ready(engine):
            engine.wait_ge(lo_made, 2 * NT)
        follower = after(ph, ready) if after else None
        with nc.Block() as block:
            @block.sync
            def _(sp):
                if load is not None:
                    for t in range(NT):
                        if t == NT - 1:
                            sp.wait_ge(cleared, 1)
                        n = P if t < NT - 1 else LAST
                        sp.dma_start(x[0:n, t, :], load[t * P:t * P + n, :]).then_inc(loaded[t // 2], 16)
                if follower:
                    follower.sync_begin(sp)
                if keep is not None:
                    sp.dma_start(keep.rearrange("(t p) d -> p t d", p=P), x[:, :, :]).then_inc(kept, 16)
                    sp.wait_ge(kept, 16)
                if follower:
                    follower.sync_end(sp)

            @block.vector
            def _(v):
                s = Steps(v, v_s)
                s.done(v.memset(eps[:, :], EPS))
                if load is not None:
                    v.memset(x[:, NT - 1, :], 0.0).then_inc(cleared, 1)
                if follower:
                    follower.vector_begin(v)
                for t in range(NT):
                    if load is not None and t % 2 == 0:
                        v.wait_ge(loaded[t // 2], 32)
                    for h in range(2):
                        s.done(v.bn_stats(stats[:, t, h, :], x[:, t, h * HD:(h + 1) * HD]))
                s.wait()
                for t in range(NT):
                    s.done(v.bn_aggr(moments[:, t, :], stats[:, t, :, :].rearrange("p a b -> p (a b)")))
                v.wait_ge(dev_made, 1)
                s.done(v.reciprocal(inv[:, :], dev[:, :]))
                s.wait()
                for t in range(NT + 1):
                    if t < NT:
                        if t >= 2:
                            if tokens:
                                v.wait_ge(lo_made, t - 1)
                            else:
                                v.wait_ge(turned_s, 2 * t - 2)
                        v.tensor_scalar(xn[:, t % 2, :], x[:, t, :], moments[:, t, 0:1], inv[:, t:t + 1],
                                        ALU.subtract, ALU.mult).then_inc(normed, 1)
                    if t == 0:
                        continue
                    u = t - 1
                    if tokens:
                        v.wait_ge(hi_made, t)
                        v.tensor_tensor(tokens[1][:, u, :], xn[:, u % 2, :], tokens[0][:, u, :].bitcast(F32),
                                        ALU.subtract).then_inc(lo_made, 1)
                    else:
                        for h in range(2):
                            v.wait_ge(hi_made, 2 * u + h + 1)
                            at = (slice(None), slice(3 * h, 3 * h + 3), slice(u * P, u * P + P))
                            v.tensor_tensor(features[1][at], turned[(2 * u + h) % 4][:, 0:3, :],
                                            features[0][at].bitcast(F32), ALU.subtract).then_inc(lo_made, 1)
                if follower:
                    follower.vector_end(v)

            @block.scalar
            def _(act):
                act.wait_ge(v_s, 1 + 3 * NT)
                act.activation(dev[:, :], moments[:, :, 1], ACT.Sqrt, bias=eps[:, 0:1]).then_inc(dev_made, 1)
                for t in range(NT):
                    if tokens:
                        act.wait_ge(normed, t + 1)
                        act.activation(tokens[0][:, t, :], xn[:, t % 2, :], ACT.Copy).then_inc(hi_made, 1)
                    else:
                        for h in range(2):
                            act.wait_ge(turned_s, 2 * t + h + 1)
                            act.activation(features[0][:, 3 * h:3 * h + 3, t * P:t * P + P],
                                           turned[(2 * t + h) % 4][:, 0:3, :], ACT.Copy).then_inc(hi_made, 1)
                if follower:
                    follower.scalar(act)

            if features:
                @block.tensor
                def _(pe):
                    for t in range(NT):
                        pe.wait_ge(normed, t + 1)
                        for h in range(2):
                            if t >= 2:
                                pe.wait_ge(lo_made, 2 * t + h - 3)
                            for k in range(3):
                                last = pe.transpose(turned[(2 * t + h) % 4][:, k, :],
                                                    xn[:, t % 2, (3 * h + k) * P:(3 * h + k + 1) * P], ident[:, :])
                            last.then_inc(turned_s, 1)
                    if follower:
                        follower.tensor(pe)


def rgcn_phase(nc, name, x_hi, x_lo, out, w, root, c_dram, inv_dram, ident_r, flag, pool_loads,
               base=None):
    with Phase(nc, name) as ph:
        NC, NW, CS = len(CHUNKS), 2, 5
        CW = CHUNKS[0][1] * P
        m_hi = [ph.sb(f"m_hi{k}", [P, KB, CW], F32R) for k in range(2)]
        m_lo = [ph.sb(f"m_lo{k}", [P, KB, CW], F32R) for k in range(2)]
        w_hi, w_lo = ph.sb("w_hi", [P, KB, D], F32R), ph.sb("w_lo", [P, KB, D], F32R)
        w_raw = ph.sb("w_raw", [P, NW, D])
        counts = ph.sb("counts", [P, CS, CW], F32R)
        inv = ph.sb("inv", [P, 2, CW])
        mean = ph.sb("mean", [P, 2, CW])
        seed = ph.sb("seed", [1, 4])
        sums = [ph.ps(f"sums{k}", [P, 512]) for k in range(KB)]
        prod = [ph.ps(f"prod{k}", [P, 512]) for k in range(2)]
        counts_in = [ph.sem(f"counts{k}_in") for k in range(CS)]
        w_in, inv_in = pool_loads[0:NW], pool_loads[NW:NW + 2]
        counts_used, summed, scaled, m_hi_made, m_lo_made = (ph.sem(x) for x in (
            "counts_used", "summed", "scaled", "m_hi_made", "m_lo_made"))
        w_hi_made, w_lo_made, multiplied, added, begun = (ph.sem(x) for x in (
            "w_hi_made", "w_lo_made", "multiplied", "added", "begun"))
        SUMS, PRODS, TILES = NC * KB, 2 * NT, NC * (NT - 1)

        def width(c):
            t0, nt = CHUNKS[c]
            return min(nt * P, N - t0 * P)

        def half(h):
            return slice(h * HD, (h + 1) * HD)

        def relations(engine, body):
            passes = engine.value_load(flag[0:1, 0:1], min_val=0, max_val=1) + 1
            with engine.Fori(0, passes) as again:
                with engine.Fori(0, R // 2) as g:
                    for u in range(2):
                        body(g * 2 + u, again * R + g * 2 + u, u)
            return passes * R

        based, base_in = ph.sem("based"), ph.sem("base_in")
        base_row = ph.sb("base_row", [P, D]) if base else None
        with nc.Block() as block:
            @block.sync
            def _(sp):
                if base and base[0] is not None:
                    sp.dma_start(out[:, 0:NT - 1, :], base[0][0:(NT - 1) * P, :].rearrange("(t p) d -> p t d", p=P))\
                        .then_inc(base_in, 16)
                    sp.wait_ge(based, 1)
                    sp.dma_start(out[0:LAST, NT - 1, :], base[0][(NT - 1) * P:N, :]).then_inc(base_in, 16)
                if base:
                    sp.dma_start(base_row[:, :], base[1].partition_broadcast(P)).then_inc(base_in, 16)

                def body(r, m, u):
                    for c, (t0, nt) in enumerate(CHUNKS):
                        for s in range(NT):
                            if s == NT - 1 - CS:
                                sp.wait_ge(summed, (m + 1) * SUMS + c * KB)
                            else:
                                sp.wait_ge(counts_used, m * TILES + c * (NT - 1) + s + (2 if s < CS else 1))
                            sp.dma_start(counts[:, s % CS, 0:width(c)].bitcast(F32),
                                         c_dram[bass.ds(m, 1), s * P:(s + 1) * P, t0 * P:t0 * P + width(c)]
                                         .rearrange("a p d -> (a p) d")).then_inc(counts_in[s % CS], 16)
                relations(sp, body)

            @block.gpsimd
            def _(pool):
                def weight_blocks(source, n):
                    for kb in range(KB):
                        pool.wait_ge(w_lo_made, n * KB + kb + 1)
                        pool.wait_ge(begun, 1)
                        pool.dma_start(w_raw[:, kb % NW, :], source(slice(kb * P, (kb + 1) * P)))\
                            .then_inc(w_in[kb % NW], 16)

                def inverse_row(r, m, c, row):
                    t0, nt = CHUNKS[c]
                    pool.wait_ge(scaled, m * SUMS + c * KB + 2 * KB)
                    pool.wait_ge(begun, 1)
                    pool.dma_start(inv[:, row, 0:width(c)],
                                   inv_dram[bass.ds(r, 1), t0 * P:t0 * P + width(c)]
                                   .rearrange("a d -> (a d)").partition_broadcast(P)).then_inc(inv_in[row], 16)

                def body(r, m, u):
                    inverse_row(r, m, 0, u)
                    inverse_row(r, m, 1, 1 - u)
                    weight_blocks(lambda at: w[bass.ds(r, 1), at, :].rearrange("a p d -> (a p) d"), m + 1)
                    inverse_row(r, m, 2, u)
                pool.memset(seed[:, 0:1], 0.0).then_inc(w_lo_made, NW)
                pool.memset(seed[:, 1:2], 0.0).then_inc(counts_used, CS)
                pool.memset(seed[:, 2:3], 0.0).then_inc(begun, 1)
                weight_blocks(lambda at: root[at, :], 0)
                relations(pool, body)

            @block.tensor
            def _(pe):
                def products_of(n, c, k):
                    t0, nt = CHUNKS[c]
                    pe.wait_ge(m_lo_made, n * SUMS + (c + 1) * KB)
                    if c == 0:
                        pe.wait_ge(w_lo_made, n * KB + KB + NW)
                    for t in range(nt):
                        at = slice(t * P, (t + 1) * P)
                        for h in range(2):
                            pe.wait_ge(added, n * PRODS + (t0 + t) * 2 + h + 1)
                            for f in range(KB):
                                for a, b in ((m_hi, w_hi), (m_hi, w_lo), (m_lo, w_hi)):
                                    last = pe.matmul(prod[h][:, 0:HD], a[k][:, f, at], b[:, f, half(h)],
                                                     start=f == 0 and b is w_hi and a is m_hi,
                                                     stop=f == KB - 1 and a is m_lo)
                            last.then_inc(multiplied, 1)

                for c, (t0, nt) in enumerate(CHUNKS):
                    if c:
                        pe.wait_ge(scaled, c * KB)
                    for f in range(KB):
                        for t in range(nt):
                            for part in (x_hi, x_lo):
                                last = pe.matmul(sums[f][:, t * P:(t + 1) * P],
                                                 part[:, t0 + t, f * P:(f + 1) * P], ident_r[:, :],
                                                 start=part is x_hi and t == 0, stop=True, skip_group_check=True)
                        last.then_inc(summed, 1)
                    if c:
                        products_of(0, c - 1, (c - 1) % 2)

                def body(r, m, u):
                    for c, (t0, nt) in enumerate(CHUNKS):
                        pe.wait_ge(scaled, m * SUMS + SUMS + c * KB)
                        for s in range(NT):
                            pe.wait_ge(counts_in[s % CS], (m * NC + c) * (NT // CS * 16) + (s // CS + 1) * 16)
                            for f in range(KB):
                                for part in (x_hi, x_lo):
                                    last = pe.matmul(sums[f][:, 0:width(c)], part[:, s, f * P:(f + 1) * P],
                                                     counts[:, s % CS, 0:width(c)], start=s == 0 and part is x_hi,
                                                     stop=s == NT - 1 and part is x_lo)
                                if s == NT - 1:
                                    last.then_inc(summed, 1)
                            if s < NT - 1:
                                last.then_inc(counts_used, 1)
                        products_of(m + 1 if c else m, (c - 1) % NC, (u + c) % 2)
                planes = relations(pe, body)
                products_of(planes, NC - 1, (R + NC - 1) % 2)

            @block.scalar
            def _(act):
                def weight(n):
                    for kb in range(KB):
                        act.wait_ge(w_in[kb % NW], n * (KB // NW * 16) + (kb // NW + 1) * 16)
                        act.activation(w_hi[:, kb, :], w_raw[:, kb % NW, :], ACT.Copy).then_inc(w_hi_made, 1)

                def first_parts(n, c, k):
                    for f in range(KB):
                        act.wait_ge(scaled, n * SUMS + c * KB + f + 1)
                        act.activation(m_hi[k][:, f, 0:width(c)], mean[:, f % 2, 0:width(c)], ACT.Copy)\
                            .then_inc(m_hi_made, 1)
                for c in range(NC):
                    first_parts(0, c, c % 2)
                    if c == 0:
                        weight(0)

                def body(r, m, u):
                    for c in range(NC):
                        first_parts(m + 1, c, (u + 1 + c) % 2)
                        if c == 0:
                            act.wait_ge(multiplied, (m + 1) * PRODS)
                            weight(m + 1)
                relations(act, body)

            @block.vector
            def _(v):
                def second_parts(n, c, k, f):
                    v.wait_ge(m_hi_made, n * SUMS + c * KB + f + 1)
                    v.tensor_tensor(m_lo[k][:, f, 0:width(c)], mean[:, f % 2, 0:width(c)],
                                    m_hi[k][:, f, 0:width(c)].bitcast(F32), ALU.subtract).then_inc(m_lo_made, 1)

                def means(n, c, k, fs, inv_row):
                    for f in fs:
                        at = n * SUMS + c * KB + f
                        v.wait_ge(summed, at + 1)
                        if not isinstance(at, int) or at >= 2:
                            v.wait_ge(m_lo_made, at - 1)
                        if inv_row is None:
                            last = v.tensor_copy(mean[:, f % 2, 0:width(c)], sums[f][:, 0:width(c)])
                        else:
                            last = v.tensor_tensor(mean[:, f % 2, 0:width(c)], sums[f][:, 0:width(c)],
                                                   inv[:, inv_row, 0:width(c)], ALU.mult)
                        last.then_inc(scaled, 1)
                        if f > fs[0]:
                            second_parts(n, c, k, f - 1)
                    second_parts(n, c, k, fs[-1])

                def add(n, c, i, over):
                    t, h = CHUNKS[c][0] + i // 2, i % 2
                    v.wait_ge(multiplied, n * PRODS + t * 2 + h + 1)
                    if over:
                        last = v.tensor_copy(out[:, t, half(h)], prod[h][:, 0:HD])
                    else:
                        last = v.tensor_tensor(out[:, t, half(h)], prod[h][:, 0:HD], out[:, t, half(h)], ALU.add)
                    last.then_inc(added, 1)

                def weight(n):
                    for kb in range(KB):
                        v.wait_ge(w_hi_made, n * KB + kb + 1)
                        v.tensor_tensor(w_lo[:, kb, :], w_raw[:, kb % NW, :], w_hi[:, kb, :].bitcast(F32),
                                        ALU.subtract).then_inc(w_lo_made, 1)

                if base:
                    if base[0] is not None:
                        v.memset(out[:, NT - 1, :], 0.0).then_inc(based, 1)
                    v.memset(seed[:, 3:4], 0.0).then_inc(added, 2)
                else:
                    v.memset(out[:, CHUNKS[-1][0]:NT, :], 0.0).then_inc(added, 2)
                for c in range(NC):
                    means(0, c, c % 2, (0, 1, 2), None)
                    if c:
                        add(0, c - 1, 0, not base)
                    means(0, c, c % 2, (3, 4, 5), None)
                    for i in range(1, 2 * CHUNKS[c - 1][1] if c else 0):
                        add(0, c - 1, i, not base)
                    if c == 0:
                        weight(0)
                    if c == 0 and base:
                        v.wait_ge(base_in, 48 if base[0] is not None else 16)
                        for t in range(NT):
                            if base[0] is not None:
                                last = v.tensor_tensor(out[:, t, :], out[:, t, :], base_row[:, :], ALU.add)
                            else:
                                last = v.tensor_copy(out[:, t, :], base_row[:, :])
                            last.then_inc(based, 1)
                        v.wait_ge(based, NT + (base[0] is not None))

                def body(r, m, u):
                    for c in range(NC):
                        row = (u + c) % 2
                        v.wait_ge(inv_in[row], m_half(m, u) + ((3 * u + c) // 2 + 1) * 16)
                        before = (m + 1 if c else m, (c - 1) % NC)
                        means(m + 1, c, (u + 1 + c) % 2, (0, 1, 2), row)
                        add(*before, 0, False)
                        means(m + 1, c, (u + 1 + c) % 2, (3, 4, 5), row)
                        for i in range(1, 2 * CHUNKS[before[1]][1]):
                            add(*before, i, False)
                        if c == 0:
                            weight(m + 1)

                def m_half(m, u):
                    return (m - u) * (NC * 16 // 2)
                planes = relations(v, body)
                for i in range(2 * CHUNKS[-1][1]):
                    add(planes, NC - 1, i, False)


H_FFN, N_EXP0 = 384, 4
HB = H_FFN // P


def relu_phase(nc, name, rows, hi, lo):
    with Phase(nc, name) as ph:
        hi_made = ph.sem("hi_made")
        with nc.Block() as block:
            @block.scalar
            def _(act):
                for t in range(NT):
                    act.activation(hi[:, t, :], rows[:, t, :], ACT.Relu).then_inc(hi_made, 1)

            @block.vector
            def _(v):
                for t in range(NT):
                    v.wait_ge(hi_made, t + 1)
                    v.scalar_tensor_tensor(out=lo[:, t, :], in0=rows[:, t, :], scalar=0.0,
                                           in1=hi[:, t, :].bitcast(F32), op0=ALU.max, op1=ALU.subtract)


def experts_phase(nc, f_hi, f_lo, rows, wg, bg, w1, b1, w2, b2, ident):
    with Phase(nc, "experts") as ph:
        NC, CW = len(CHUNKS), CHUNKS[0][1] * P
        NE = N_EXP0
        g_raw = ph.sb("g_raw", [P, KB, P])
        g_hi, g_lo = ph.sb("g_hi", [P, KB, P], F32R), ph.sb("g_lo", [P, KB, P], F32R)
        gate_row = ph.sb("gate_row", [NE, NP])
        blank_s, row_made, row_taken = ph.sem("blank"), ph.sem("row_made"), ph.sem("row_taken")
        g_bias = ph.sb("g_bias", [P, NE])
        logits, largest = ph.sb("logits", [P, NT, NE]), ph.sb("largest", [P, NT])
        equal, chosen = ph.sb("equal", [P, NT, NE]), ph.sb("chosen", [P, NT, NE])
        free = ph.sb("free", [P, NE, NT])
        raw1, raw2 = ph.sb("raw1", [P, KB, H_FFN]), ph.sb("raw2", [P, HB, D])
        w1_hi, w1_lo = ph.sb("w1_hi", [P, KB, H_FFN], F32R), ph.sb("w1_lo", [P, KB, H_FFN], F32R)
        w2_hi, w2_lo = ph.sb("w2_hi", [P, HB, D], F32R), ph.sb("w2_lo", [P, HB, D], F32R)
        b1_col = ph.sb("b1_col", [P, NE, HB])
        b2_row = ph.sb("b2_row", [P, NE, D])
        act_out = ph.sb("act_out", [P, 2, CW])
        h_hi, h_lo = ph.sb("h_hi", [P, 2, HB, CW], F32R), ph.sb("h_lo", [P, 2, HB, CW], F32R)
        hid = [ph.ps(f"hid{k}", [P, 512]) for k in range(HB)]
        prod = [ph.ps(f"prod{k}", [P, 512]) for k in range(4)]
        gate = ph.ps("gate", [P, NT, NE])
        loaded, raw1_in, raw2_in = ph.sem("loaded"), ph.sem("raw1_in"), ph.sem("raw2_in")
        v_s, gate_split, gated, w1_hi_s, w1_lo_s, w2_hi_s, w2_lo_s = (ph.sem(x) for x in (
            "vector", "gate_split", "gated", "w1_hi_made", "w1_lo_made", "w2_hi_made", "w2_lo_made"))
        hid_made, gelu_made, h_hi_s, h_lo_s, multiplied, added, biased, gate_hi = (ph.sem(x) for x in (
            "hid_made", "gelu_made", "h_hi_made", "h_lo_made", "multiplied", "added", "biased", "gate_hi"))
        PARTS = ((0, 0), (0, 1), (1, 0))

        with nc.Block() as block:
            @block.sync
            def _(sp):
                sp.dma_start(raw1[:, :, :], w1[0].rearrange("(k p) n -> p k n", p=P)).then_inc(raw1_in, 16)
                sp.wait_ge(blank_s, 1)
                sp.dma_start(g_raw[:, :, 0:NE], wg.rearrange("(k p) n -> p k n", p=P)).then_inc(loaded, 16)
                sp.dma_start(g_bias[:, :], bg.partition_broadcast(P)).then_inc(loaded, 16)
                sp.dma_start(b1_col[:, :, :], b1.rearrange("e (k p) -> p e k", p=P),
                             allow_slow_non_contiguous=True).then_inc(loaded, 16)
                sp.dma_start(b2_row[:, :, :], b2.partition_broadcast(P)).then_inc(loaded, 16)
                for e in range(NE):
                    if e:
                        sp.wait_ge(w1_lo_s, e)
                        sp.dma_start(raw1[:, :, :], w1[e].rearrange("(k p) n -> p k n", p=P)).then_inc(raw1_in, 16)
                    if e:
                        sp.wait_ge(w2_lo_s, e)
                    sp.dma_start(raw2[:, :, :], w2[e].rearrange("(k p) n -> p k n", p=P)).then_inc(raw2_in, 16)

            @block.tensor
            def _(pe):
                f, g = (f_hi, f_lo), (g_hi, g_lo)
                h, w1p, w2p = (h_hi, h_lo), (w1_hi, w1_lo), (w2_hi, w2_lo)

                def hidden(e, c):
                    t0, nt = CHUNKS[c]
                    if c == 0:
                        pe.wait_ge(w1_lo_s, e + 1)
                    for m in range(HB):
                        if (e, c) != (0, 0):
                            pe.wait_ge(gelu_made, (e * NC + c - 1) * HB + m + 1)
                        for kb in range(KB):
                            for a, b in PARTS:
                                last = pe.matmul(hid[m][:, 0:nt * P], w1p[a][:, kb, m * P:(m + 1) * P],
                                                 f[b][:, kb, t0 * P:(t0 + nt) * P],
                                                 start=kb == 0 and (a, b) == (0, 0), stop=kb == KB - 1 and a == 1)
                        last.then_inc(hid_made, 1)

                def products(e, c):
                    t0, nt = CHUNKS[c]
                    k = (e * NC + c) % 2
                    pe.wait_ge(h_lo_s, (e * NC + c + 1) * HB)
                    if c == 0:
                        pe.wait_ge(w2_lo_s, e + 1)
                    for t in range(nt):
                        for half in range(2):
                            n = (e * NT + t0 + t) * 2 + half
                            if n >= 4:
                                pe.wait_ge(added, n - 3)
                            for m in range(HB):
                                for a, b in PARTS:
                                    last = pe.matmul(prod[n % 4][:, 0:HD], h[a][:, k, m, t * P:(t + 1) * P],
                                                     w2p[b][:, m, half * HD:(half + 1) * HD],
                                                     start=m == 0 and (a, b) == (0, 0), stop=m == HB - 1 and a == 1)
                            last.then_inc(multiplied, 1)
                def gate_rows():
                    pe.wait_ge(gate_split, 1)
                    for c, (t0, nt) in enumerate(CHUNKS):
                        for kb in range(KB):
                            for a, b in PARTS:
                                last = pe.matmul(prod[c][:, 0:nt * P], g[a][:, kb, :],
                                                 f[b][:, kb, t0 * P:(t0 + nt) * P],
                                                 start=kb == 0 and (a, b) == (0, 0), stop=kb == KB - 1 and a == 1)
                        last.then_inc(row_made, 1)

                def gates():
                    pe.wait_ge(row_taken, NC)
                    for t in range(NT):
                        last = pe.transpose(gate[:, t, :], gate_row[:, t * P:(t + 1) * P], ident[0:NE, 0:NE])
                    last.then_inc(gated, 1)

                order = [(e, c) for e in range(NE) for c in range(NC)]
                for i, (e, c) in enumerate(order):
                    hidden(e, c)
                    if i == 0:
                        gate_rows()
                    else:
                        if i == 1:
                            gates()
                        products(*order[i - 1])
                products(*order[-1])

            @block.scalar
            def _(act):

                def weight(e):
                    act.wait_ge(raw1_in, 16 * (e + 1))
                    if e:
                        act.wait_ge(hid_made, e * NC * HB)
                    act.activation(w1_hi[:, :, :], raw1[:, :, :], ACT.Copy).then_inc(w1_hi_s, 1)
                weight(0)
                act.wait_ge(loaded, 64)
                act.activation(g_hi[:, :, :], g_raw[:, :, :], ACT.Copy).then_inc(gate_hi, 1)
                for e in range(NE):
                    for c, (t0, nt) in enumerate(CHUNKS):
                        i = e * NC + c
                        for m in range(HB):
                            at = i * HB + m
                            act.wait_ge(hid_made, at + 1)
                            if at >= 2:
                                act.wait_ge(h_lo_s, at - 1)
                            act.activation(act_out[:, at % 2, 0:nt * P], hid[m][:, 0:nt * P], ACT.Gelu,
                                           bias=b1_col[:, e, m:m + 1]).then_inc(gelu_made, 1)
                            act.wait_ge(gelu_made, at + 1)
                            if m == 0 and i >= 2:
                                act.wait_ge(multiplied, 2 * (e * NT + t0) - 2 * (CHUNKS[c - 1][1] if c or e else 0))
                            act.activation(h_hi[:, i % 2, m, 0:nt * P], act_out[:, at % 2, 0:nt * P], ACT.Copy)\
                                .then_inc(h_hi_s, 1)
                        if c == 0:
                            act.wait_ge(raw2_in, 16 * (e + 1))
                            if e:
                                act.wait_ge(multiplied, e * NT * 2)
                            act.activation(w2_hi[:, :, :], raw2[:, :, :], ACT.Copy).then_inc(w2_hi_s, 1)
                    if e + 1 < NE:
                        weight(e + 1)

            @block.vector
            def _(v):
                s = Steps(v, v_s)
                v.memset(g_raw[:, :, :], 0.0).then_inc(blank_s, 1)

                def weight1(e):
                    v.wait_ge(w1_hi_s, e + 1)
                    v.tensor_tensor(w1_lo[:, :, :], raw1[:, :, :], w1_hi[:, :, :].bitcast(F32), ALU.subtract)\
                        .then_inc(w1_lo_s, 1)
                weight1(0)
                v.wait_ge(gate_hi, 1)
                v.tensor_tensor(g_lo[:, :, :], g_raw[:, :, :], g_hi[:, :, :].bitcast(F32), ALU.subtract)\
                    .then_inc(gate_split, 1)
                def take_rows():
                    for c, (t0, nt) in enumerate(CHUNKS):
                        v.wait_ge(row_made, c + 1)
                        v.tensor_copy(gate_row[:, t0 * P:(t0 + nt) * P], prod[c][0:NE, 0:nt * P])\
                            .then_inc(row_taken, 1)

                def choose():
                    v.wait_ge(gated, 1)
                    s.done(v.tensor_tensor(logits[:, :, :], gate[:, :, :],
                                           g_bias[:, :].unsqueeze(1).to_broadcast([P, NT, NE]), ALU.add))
                    s.wait()
                    s.done(v.tensor_reduce(largest[:, :], logits[:, :, :], AXX, ALU.max))
                    s.wait()
                    s.done(v.tensor_tensor(equal[:, :, :], logits[:, :, :],
                                           largest[:, :].unsqueeze(2).to_broadcast([P, NT, NE]), ALU.is_equal))
                    s.done(v.memset(free[:, 0, :], 1.0))
                    for e in range(NE):
                        s.wait()
                        s.done(v.tensor_tensor(chosen[:, :, e], equal[:, :, e], free[:, e, :], ALU.mult))
                        if e + 1 < NE:
                            s.wait()
                            s.done(v.tensor_tensor(free[:, e + 1, :], free[:, e, :], chosen[:, :, e], ALU.subtract))
                    s.wait()

                def add(e, t0, i):
                    t, half = t0 + i // 2, i % 2
                    n = (e * NT + t) * 2 + half
                    v.wait_ge(multiplied, n + 1)
                    if not half:
                        if e:
                            v.wait_ge(added, ((e - 1) * NT + t) * 2 + 2)
                        v.scalar_tensor_tensor(out=rows[:, t, :], in0=b2_row[:, e, :], scalar=chosen[:, t, e:e + 1],
                                               in1=rows[:, t, :], op0=ALU.mult, op1=ALU.add).then_inc(biased, 1)
                        v.wait_ge(biased, e * NT + t + 1)
                    at = (slice(None), t, slice(half * HD, (half + 1) * HD))
                    v.scalar_tensor_tensor(out=rows[at], in0=prod[n % 4][:, 0:HD], scalar=chosen[:, t, e:e + 1],
                                           in1=rows[at], op0=ALU.mult, op1=ALU.add).then_inc(added, 1)

                order = [(e, c) for e in range(NE) for c in range(NC)]
                for i, (e, c) in enumerate(order):
                    nt = CHUNKS[c][1]
                    for m in range(HB):
                        at = i * HB + m
                        v.wait_ge(h_hi_s, at + 1)
                        v.tensor_tensor(h_lo[:, i % 2, m, 0:nt * P], act_out[:, at % 2, 0:nt * P],
                                        h_hi[:, i % 2, m, 0:nt * P].bitcast(F32), ALU.subtract).then_inc(h_lo_s, 1)
                    if i == 1:
                        choose()
                    if i:
                        pe_, pc = order[i - 1]
                        for n in range(2 * CHUNKS[pc][1]):
                            add(pe_, CHUNKS[pc][0], n)
                    if c == 0:
                        v.wait_ge(w2_hi_s, e + 1)
                        v.tensor_tensor(w2_lo[:, :, :], raw2[:, :, :], w2_hi[:, :, :].bitcast(F32), ALU.subtract)\
                            .then_inc(w2_lo_s, 1)
                    if i == 0:
                        take_rows()
                    if c == NC - 1 and e + 1 < NE:
                        weight1(e + 1)
                for n in range(2 * CHUNKS[-1][1]):
                    add(NE - 1, CHUNKS[-1][0], n)


SUM_AT = 256
NEVER = -1e38


def loops_phase(nc, ident, ctot_dram, no_edge_dram):
    with Phase(nc, "loops") as ph:
        SLOTS = 4
        total = ph.sb("total", [P, SLOTS, NP])
        none = ph.sb("none", [P, 2, NP])
        turned_sb = ph.sb("turned_sb", [P, 2, NP])
        turned = [ph.ps(f"turned{k}", [P, 3, 512]) for k in range(2)]
        loaded = [ph.sem(f"loaded{k}") for k in range(SLOTS)]
        counts_out = [ph.sem(f"counts_out{k}") for k in range(SLOTS)]
        none_out = [ph.sem(f"none_out{k}") for k in range(2)]
        looped, none_made, turned_s, taken = (ph.sem(x) for x in ("looped", "none_made", "turned", "taken"))
        def store(sp, t):
            sp.wait_ge(looped, t + 1)
            own = slice(t * P, (t + 1) * P)
            sp.dma_start(ctot_dram[own, own], total[:, t % SLOTS, own]).then_inc(counts_out[t % SLOTS], 16)
            sp.wait_ge(taken, t + 1)
            sp.dma_start(no_edge_dram[:, t * P:(t + 1) * P].rearrange("(j p) s -> p j s", p=P),
                         turned_sb[:, t % 2, :].rearrange("p (j s) -> p j s", s=P)).then_inc(none_out[t % 2], 16)

        with nc.Block() as block:
            @block.sync
            def _(sp):
                for t in range(NT):
                    if t >= SLOTS:
                        sp.wait_ge(counts_out[t % SLOTS], t // SLOTS * 16)
                        sp.wait_ge(none_made, t - SLOTS + 1)
                    sp.dma_start(total[:, t % SLOTS, :], ctot_dram[t * P:(t + 1) * P, :])\
                        .then_inc(loaded[t % SLOTS], 16)
                    if t >= SLOTS - 1:
                        store(sp, t - SLOTS + 1)
                for t in range(NT - SLOTS + 1, NT):
                    store(sp, t)
                for k in range(SLOTS):
                    sp.wait_ge(counts_out[k], len(range(k, NT, SLOTS)) * 16)
                for k in range(2):
                    sp.wait_ge(none_out[k], NT // 2 * 16)

            @block.vector
            def _(v):
                for t in range(NT):
                    v.wait_ge(loaded[t % SLOTS], (t // SLOTS + 1) * 16)
                    if t >= 2:
                        v.wait_ge(turned_s, t - 1)
                    v.tensor_tensor(total[:, t % SLOTS, t * P:(t + 1) * P], total[:, t % SLOTS, t * P:(t + 1) * P],
                                    ident[:, :], ALU.add).then_inc(looped, 1)
                    v.wait_ge(looped, t + 1)
                    v.tensor_scalar(none[:, t % 2, :], total[:, t % SLOTS, :], 0.0, NEVER, ALU.is_equal,
                                    ALU.mult).then_inc(none_made, 1)

            @block.tensor
            def _(pe):
                for t in range(NT):
                    pe.wait_ge(none_made, t + 1)
                    if t >= 2:
                        pe.wait_ge(taken, t - 1)
                    for j in range(NT):
                        last = pe.transpose(turned[t % 2][:, j // 4, (j % 4) * P:(j % 4 + 1) * P],
                                            none[:, t % 2, j * P:(j + 1) * P], ident[:, :])
                    last.then_inc(turned_s, 1)

            @block.scalar
            def _(act):
                for t in range(NT):
                    act.wait_ge(turned_s, t + 1)
                    if t >= 2:
                        act.wait_ge(none_out[t % 2], t // 2 * 16)
                    act.activation(turned_sb[:, t % 2, :],
                                   turned[t % 2].rearrange("p b c -> p (b c)")[:, 0:NP], ACT.Copy).then_inc(taken, 1)


def add_low_phase(nc, flag, c_dram, ctot_dram):
    with Phase(nc, "low") as ph:
        high, low = ph.sb("high", [P, NP]), ph.sb("low", [P, NP])
        loaded, summed, stored = ph.sem("loaded"), ph.sem("summed"), ph.sem("stored")
        with nc.Block() as block:
            @block.sync
            def _(sp):
                def run():
                    for t in range(NT):
                        if t:
                            sp.wait_ge(stored, t * 16)
                        sp.dma_start(high[:, :], ctot_dram[t * P:(t + 1) * P, :]).then_inc(loaded, 16)
                        sp.dma_start(low[:, :], c_dram[plane(R, 1), t * P:(t + 1) * P, :]).then_inc(loaded, 16)
                        sp.wait_ge(summed, t + 1)
                        sp.dma_start(ctot_dram[t * P:(t + 1) * P, :], high[:, :]).then_inc(stored, 16)
                    sp.wait_ge(stored, NT * 16)
                where_flag(sp, flag, run, True)

            @block.vector
            def _(v):
                def run():
                    for t in range(NT):
                        v.wait_ge(loaded, (t + 1) * 32)
                        v.tensor_tensor(high[:, :], high[:, :], low[:, :], ALU.add).then_inc(summed, 1)
                where_flag(v, flag, run, True)


class Logits:

    def __init__(self, ph, f_hi, f_lo, kbs, w_t, a_src, a_dst, heads, ident, cols, rows_dram, ready):
        self.f, self.kbs, self.w_t, self.atts, self.heads, self.ident = (f_hi, f_lo), kbs, w_t, (a_src, a_dst), heads, ident
        self.cols, self.rows_dram, self.ready = cols, rows_dram, ready
        width, rest = w_t.shape
        self.cbs, self.rest, n = width // P, rest, 2 * heads
        self.att = ph.sb("att", [P, self.cbs, 2, heads])
        self.weight = ph.sb("weight", [P, self.cbs, rest])
        self.wa_row = ph.sb("wa_row", [n, rest])
        self.wa_hi, self.wa_lo = ph.sb("wa_hi", [P, kbs, P], F32R), ph.sb("wa_lo", [P, kbs, P], F32R)
        self.blank = ph.sb("blank", [P, kbs, P])
        self.row = ph.sb("row", [P, NP])
        self.acc = ph.ps("logit_acc", [P, 3, 512])
        self.turned = ph.ps("logits_turned", [P, NT, 2, heads])
        (self.blank_s, self.att_in, self.weight_in, self.wa_made, self.wa_taken, self.wa_turned, self.wa_whole, self.split,
         self.multiplied, self.taken, self.turned_s, self.stored) = (ph.sem(x) for x in (
             "blank", "att_in", "weight_in", "wa_made", "wa_taken", "wa_turned", "wa_whole", "split",
             "multiplied", "logits_taken", "logits_turned", "logits_stored"))

    def sync_begin(self, sp):
        sp.wait_ge(self.blank_s, 1)
        per = self.cbs // self.heads
        for k, a in enumerate(self.atts):
            for h in range(self.heads):
                sp.dma_start(self.att[:, h * per:(h + 1) * per, k, h], a[h].rearrange("(k p) -> p k", p=P),
                             allow_slow_non_contiguous=True).then_inc(self.att_in, 16)
        for cb in range(self.cbs):
            sp.dma_start(self.weight[:, cb, :], self.w_t[cb * P:(cb + 1) * P, :]).then_inc(self.weight_in, 16)

    def sync_end(self, sp):
        sp.wait_ge(self.taken, 1)
        sp.dma_start(self.rows_dram, self.row[0:self.heads, :]).then_inc(self.stored, 16)
        sp.wait_ge(self.stored, 16)

    def halves(self):
        half = self.rest // 2
        return [(0, half), (half, self.rest)]

    def tensor(self, pe):
        n = 2 * self.heads
        pe.wait_ge(self.att_in, 2 * self.heads * 16)
        pe.wait_ge(self.weight_in, self.cbs * 16)
        for cb in range(self.cbs):
            for b, (c0, c1) in enumerate(self.halves()):
                last = pe.matmul(self.acc[0:n, b, 0:c1 - c0], self.att[:, cb, :, :].rearrange("p s h -> p (s h)"),
                                 self.weight[:, cb, c0:c1], start=cb == 0, stop=cb == self.cbs - 1)
        last.then_inc(self.wa_made, 1)
        pe.wait_ge(self.wa_taken, 2)
        for kb in range(self.kbs):
            last = pe.transpose(self.turned[:, kb, :, :].rearrange("p s h -> p (s h)"),
                                self.wa_row[:, kb * P:(kb + 1) * P], self.ident[0:n, 0:n])
        last.then_inc(self.wa_turned, 1)
        pe.wait_ge(self.split, 2)
        self.ready(pe)
        g = (self.wa_hi, self.wa_lo)
        for c, (t0, nt) in enumerate(CHUNKS):
            for kb in range(self.kbs):
                for a, b in ((0, 0), (0, 1), (1, 0)):
                    last = pe.matmul(self.acc[:, c, 0:nt * P], g[a][:, kb, :],
                                     self.f[b][:, kb, t0 * P:(t0 + nt) * P], start=kb == 0 and (a, b) == (0, 0),
                                     stop=kb == self.kbs - 1 and a == 1)
        last.then_inc(self.multiplied, 1)
        pe.wait_ge(self.taken, 1)
        for t in range(NT):
            last = pe.transpose(self.turned[:, t, :, :].rearrange("p s h -> p (s h)"),
                                self.row[0:n, t * P:(t + 1) * P], self.ident[0:n, 0:n])
        last.then_inc(self.turned_s, 1)

    def vector_begin(self, v):
        v.memset(self.att[:, :, :, :], 0.0).then_inc(self.blank_s, 1)
        v.memset(self.blank[:, :, :], 0.0).then_inc(self.blank_s, 1)

    def vector_end(self, v):
        n = 2 * self.heads
        v.wait_ge(self.wa_made, 1)
        for b, (c0, c1) in enumerate(self.halves()):
            v.tensor_copy(self.wa_row[:, c0:c1], self.acc[0:n, b, 0:c1 - c0]).then_inc(self.wa_taken, 1)
        v.wait_ge(self.wa_turned, 1)
        v.wait_ge(self.blank_s, 2)
        v.tensor_copy(self.blank[:, :, 0:n], self.turned[:, 0:self.kbs, :, :].rearrange("p k s h -> p k (s h)"))\
            .then_inc(self.wa_whole, 1)
        v.wait_ge(self.split, 1)
        v.tensor_tensor(self.wa_lo[:, :, :], self.blank[:, :, :], self.wa_hi[:, :, :].bitcast(F32), ALU.subtract)\
            .then_inc(self.split, 1)
        v.wait_ge(self.multiplied, 1)
        v.tensor_copy(self.row[:, :], self.acc.rearrange("p b c -> p (b c)")[:, 0:NP]).then_inc(self.taken, 1)
        v.wait_ge(self.turned_s, 1)
        v.tensor_copy(self.cols[:, :, :], self.turned[:, :, :, :].rearrange("p t s h -> p t (s h)"))

    def scalar(self, act):
        act.wait_ge(self.wa_whole, 1)
        act.activation(self.wa_hi[:, :, :], self.blank[:, :, :], ACT.Copy).then_inc(self.split, 1)


def turn_phase(nc, name, rows, blocks, ident, f_hi, f_lo, at=0, after=None, load=None):
    with Phase(nc, name) as ph:
        turned_s, hi_made, lo_made, load_s = (ph.sem(x) for x in ("turned", "hi_made", "lo_made", "load"))
        steps = [(t, f, min(4, blocks - f)) for t in range(NT) for f in range(0, blocks, 4)]

        def ready(engine):
            engine.wait_ge(lo_made, len(steps))
        follower = after(ph, ready) if after else None
        turned = [ph.ps(f"turned{k}", [P, 4, P]) for k in range(4)]

        def where(t, f, n):
            return slice(None), slice(at + f, at + f + n), slice(t * P, (t + 1) * P)
        with nc.Block() as block:
            @block.sync
            def _(sp):
                if load:
                    sp.dma_start(load[0][:, :, :], load[1].rearrange("(t p) d -> p t d", p=P)).then_inc(load_s, 16)
                if follower:
                    follower.sync_begin(sp)
                    follower.sync_end(sp)
                if load:
                    sp.wait_ge(load_s, 16)

            @block.tensor
            def _(pe):
                for i, (t, f, n) in enumerate(steps):
                    if i >= 4:
                        pe.wait_ge(lo_made, i - 3)
                    for k in range(n):
                        last = pe.transpose(turned[i % 4][:, k, :], rows[:, t, (f + k) * P:(f + k + 1) * P],
                                            ident[:, :])
                    last.then_inc(turned_s, 1)
                if follower:
                    follower.tensor(pe)

            @block.scalar
            def _(act):
                for i, (t, f, n) in enumerate(steps):
                    act.wait_ge(turned_s, i + 1)
                    act.activation(f_hi[where(t, f, n)], turned[i % 4][:, 0:n, :], ACT.Copy).then_inc(hi_made, 1)
                if follower:
                    follower.scalar(act)

            @block.vector
            def _(v):
                if follower:
                    follower.vector_begin(v)
                for i, (t, f, n) in enumerate(steps):
                    v.wait_ge(hi_made, i + 1)
                    v.tensor_tensor(f_lo[where(t, f, n)], turned[i % 4][:, 0:n, :],
                                    f_hi[where(t, f, n)].bitcast(F32), ALU.subtract).then_inc(lo_made, 1)
                if follower:
                    follower.vector_end(v)


def project_phase(nc, name, f_hi, f_lo, kbs, jobs, beside=None, finish=None):
    with Phase(nc, name) as ph:
        side = beside(ph) if beside else None
        finish_row = ph.sb("finish_row", [P, D]) if finish else None
        row_in, row_added, out_stored = ph.sem("row_in"), ph.sem("row_added"), ph.sem("out_stored")
        width = max(w for _, w, _, _ in jobs)
        raw = ph.sb("raw", [P, kbs, width])
        w_hi = [ph.sb(f"w_hi{k}", [P, kbs, width], F32R) for k in range(2)]
        w_lo = [ph.sb(f"w_lo{k}", [P, kbs, width], F32R) for k in range(2)]
        stage = ph.sb("stage", [P, 2, width])
        prod = [ph.ps(f"prod{k}", [P, 512]) for k in range(4)]
        raw_in, w_hi_s, w_lo_s, multiplied, hi_out, taken = (ph.sem(x) for x in (
            "raw_in", "w_hi_made", "w_lo_made", "multiplied", "hi_out", "taken"))
        stored = [ph.sem(f"stored{k}") for k in range(2)]

        def weights(j):
            return jobs[j][0] if isinstance(jobs[j][0], list) else [(jobs[j][0], 0, kbs)]

        def pieces(i):
            n = len(jobs) * NT
            return range(i * side.pieces // n, (i + 1) * side.pieces // n) if side else ()
        DRAM_JOBS = [j for j, job in enumerate(jobs) if job[2] == "dram"]

        def stores_before(j, t, k):
            return sum(1 for i in DRAM_JOBS for u in range(NT) if (i, u) < (j, t) and u % 2 == k)
        with nc.Block() as block:
            @block.sync
            def _(sp):
                def load(j):
                    if j:
                        sp.wait_ge(w_lo_s, j)
                    for view, k0, k1 in weights(j):
                        sp.dma_start(raw[:, k0:k1, 0:jobs[j][1]], view).then_inc(raw_in, 16)
                load(0)
                if finish:
                    sp.dma_start(finish_row[:, :], finish[1].partition_broadcast(P)).then_inc(row_in, 16)
                if side:
                    side.sync_begin(sp)
                for j, (_, w, sink, dest) in enumerate(jobs):
                    if j + 1 < len(jobs):
                        load(j + 1)
                    for t in range(NT):
                        if sink == "dram":
                            sp.wait_ge(taken, j * NT + t + 1)
                            sp.dma_start(dest(t), stage[:, t % 2, 0:w]).then_inc(stored[t % 2], 16)
                        for i in pieces(j * NT + t):
                            side.sync_piece(sp, i)
                        if finish and j == len(jobs) - 1:
                            sp.wait_ge(taken, j * NT + t + 1)
                            n = P if t < NT - 1 else LAST
                            sp.dma_start(finish[2][t * P:t * P + n, :], finish[0][0:n, t, :]).then_inc(out_stored, 16)
                if finish:
                    sp.wait_ge(out_stored, NT * 16)
                if side:
                    side.sync_end(sp)
                for k in range(2):
                    if DRAM_JOBS:
                        sp.wait_ge(stored[k], 16 * stores_before(len(jobs), 0, k))

            @block.tensor
            def _(pe):
                f, w_parts = (f_hi, f_lo), (w_hi, w_lo)
                for j, (_, w, _, _) in enumerate(jobs):
                    pe.wait_ge(w_lo_s, j + 1)
                    for t in range(NT):
                        i = j * NT + t
                        if i >= 4:
                            pe.wait_ge(taken, i - 3)
                        for kb in range(kbs):
                            for a, b in ((0, 0), (0, 1), (1, 0)):
                                last = pe.matmul(prod[i % 4][:, 0:w], f[a][:, kb, t * P:(t + 1) * P],
                                                 w_parts[b][j % 2][:, kb, 0:w], start=kb == 0 and (a, b) == (0, 0),
                                                 stop=kb == kbs - 1 and a == 1)
                        last.then_inc(multiplied, 1)
                if side:
                    side.tensor_end(pe)

            @block.scalar
            def _(act):
                def weight(j):
                    act.wait_ge(raw_in, 16 * sum(len(weights(i)) for i in range(j + 1)))
                    if j >= 2:
                        act.wait_ge(multiplied, (j - 1) * NT)
                    w = jobs[j][1]
                    act.activation(w_hi[j % 2][:, :, 0:w], raw[:, :, 0:w], ACT.Copy).then_inc(w_hi_s, 1)
                weight(0)
                for j, (_, w, sink, dest) in enumerate(jobs):
                    for t in range(NT):
                        if t == 1 and j + 1 < len(jobs):
                            weight(j + 1)
                        i = j * NT + t
                        if sink == "parts":
                            act.wait_ge(multiplied, i + 1)
                            act.activation(dest(t)[0], prod[i % 4][:, 0:w], ACT.Copy).then_inc(hi_out, 1)
                        elif sink == "dram":
                            act.wait_ge(multiplied, i + 1)
                            if stores_before(j, t, t % 2):
                                act.wait_ge(stored[t % 2], 16 * stores_before(j, t, t % 2))
                            act.activation(stage[:, t % 2, 0:w], prod[i % 4][:, 0:w], ACT.Copy).then_inc(taken, 1)

            @block.vector
            def _(v):
                def weight(j):
                    w = jobs[j][1]
                    v.wait_ge(w_hi_s, j + 1)
                    v.tensor_tensor(w_lo[j % 2][:, :, 0:w], raw[:, :, 0:w], w_hi[j % 2][:, :, 0:w].bitcast(F32),
                                    ALU.subtract).then_inc(w_lo_s, 1)
                weight(0)
                if finish:
                    v.wait_ge(row_in, 16)
                    for t in range(NT):
                        v.tensor_tensor(finish[0][:, t, :], finish[0][:, t, :], finish_row[:, :], ALU.add)\
                            .then_inc(row_added, 1)
                    v.wait_ge(row_added, NT)
                parts = 0
                for j, (_, w, sink, dest) in enumerate(jobs):
                    for t in range(NT):
                        if t == 1 and j + 1 < len(jobs):
                            weight(j + 1)
                        i = j * NT + t
                        if sink == "parts":
                            parts += 1
                            v.wait_ge(hi_out, parts)
                            v.tensor_tensor(dest(t)[1], prod[i % 4][:, 0:w], dest(t)[0].bitcast(F32),
                                            ALU.subtract).then_inc(taken, 1)
                        elif sink == "add":
                            v.wait_ge(multiplied, i + 1)
                            v.tensor_tensor(dest(t), prod[i % 4][:, 0:w], dest(t), ALU.add).then_inc(taken, 1)
                        for k in pieces(i):
                            side.vector_piece(v, k)
                if side:
                    side.vector_end(v)


class Maxima:

    def __init__(self, ph, heads, ident, cols, rows_dram, no_edge_dram, shift_dram):
        self.heads, self.pieces, self.ident, self.cols = heads, heads * NT, ident, cols
        self.rows_dram, self.no_edge_dram, self.shift_dram = rows_dram, no_edge_dram, shift_dram
        self.source = ph.sb("source", [P, heads, NP])
        self.none = ph.sb("none", [P, 2, NP])
        self.masked = ph.sb("masked", [P, 2, NP])
        self.top = ph.sb("top", [P, NT, heads])
        self.z, self.fifth, self.m = (ph.sb(x, [P, NT, heads]) for x in ("z", "fifth", "m"))
        self.shift = ph.sb("shift", [P, 2, heads, NT])
        self.row = ph.sb("row", [NT * heads, 2, P])
        self.turned = ph.ps("turned", [P, 2, P])
        self.source_in, self.top_s, self.small, self.turned_s, self.taken, self.stored = (ph.sem(x) for x in (
            "source_in", "top", "small", "shifts_turned", "shifts_taken", "shifts_stored"))
        self.none_in = [ph.sem(f"none_in{k}") for k in range(2)]

    def sync_begin(self, sp):
        for h in range(self.heads):
            sp.dma_start(self.source[:, h, :], self.rows_dram[h].partition_broadcast(P)).then_inc(self.source_in, 16)
        for t in range(2):
            self.load_none(sp, t)

    def load_none(self, sp, t):
        if t >= 2:
            sp.wait_ge(self.top_s, self.heads * (t - 1))
        sp.dma_start(self.none[:, t % 2, :], self.no_edge_dram[t * P:(t + 1) * P, :]).then_inc(self.none_in[t % 2], 16)

    def sync_piece(self, sp, i):
        if i % self.heads == self.heads - 1 and i // self.heads + 2 < NT:
            self.load_none(sp, i // self.heads + 2)

    def sync_end(self, sp):
        sp.wait_ge(self.taken, 1)
        for k in range(2):
            sp.dma_start(self.shift_dram[k].rearrange("h (t p) -> (h t) p", p=P), self.row[:, k, :])\
                .then_inc(self.stored, 16)
        sp.wait_ge(self.stored, 32)

    def vector_piece(self, v, i):
        t, h = divmod(i, self.heads)
        if i == 0:
            v.wait_ge(self.source_in, self.heads * 16)
        if h == 0:
            v.wait_ge(self.none_in[t % 2], (t // 2 + 1) * 16)
        if i >= 2:
            v.wait_ge(self.top_s, i - 1)
        v.tensor_tensor_reduce(out=self.masked[:, i % 2, :], in0=self.source[:, h, :], in1=self.none[:, t % 2, :],
                               scale=1.0, scalar=2 * NEVER, op0=ALU.add, op1=ALU.max,
                               accum_out=self.top[:, t, h:h + 1]).then_inc(self.top_s, 1)

    def vector_end(self, v):
        s = Steps(v, self.small)
        v.wait_ge(self.top_s, self.pieces)
        z, fifth, m = self.z, self.fifth, self.m
        ad = self.cols[:, :, self.heads:2 * self.heads]
        s.done(v.tensor_tensor(z[:, :, :], self.top[:, :, :], ad, ALU.add))
        s.done(v.tensor_scalar(fifth[:, :, :], ad, 0.2, None, ALU.mult))
        s.wait()
        s.done(v.scalar_tensor_tensor(out=m[:, :, :], in0=z[:, :, :], scalar=0.2, in1=z[:, :, :],
                                      op0=ALU.mult, op1=ALU.max))
        s.wait()
        for k, of in enumerate((ad, fifth[:, :, :])):
            s.done(v.tensor_tensor(self.shift[:, k, :, :].rearrange("p h t -> p t h"), of, m[:, :, :], ALU.subtract))
        v.wait_ge(self.turned_s, 1)
        v.tensor_copy(self.row[:, :, :], self.turned[0:NT * self.heads, :, :]).then_inc(self.taken, 1)

    def tensor_end(self, pe):
        pe.wait_ge(self.small, 5)
        for k in range(2):
            last = pe.transpose(self.turned[0:NT * self.heads, k, :],
                                self.shift[:, k, :, :].rearrange("p h t -> p (h t)"), self.ident[:, :])
        last.then_inc(self.turned_s, 1)


def aggregate_phase(nc, name, heads, c, cols, shift_dram, ctot_dram, xl_hi, xl_lo, out, bias):
    with Phase(nc, name) as ph:
        cut = [(0, c + 2)] if c + 2 <= 512 else [(0, SUM_AT + 2), (SUM_AT + 2, c - SUM_AT)]
        B = len(cut)
        chunks = CHUNKS if B == 1 else [(t, 2) for t in range(0, NT, 2)]
        NC, CW = len(chunks), chunks[0][1] * P
        sum_at = cut[0][1] - 2
        source_fifth = ph.sb("source_fifth", [P, NT, heads])
        shift = ph.sb("shift", [P, 2, 2, NP])
        counts = ph.sb("counts", [P, 4, CW])
        e1, e2 = ph.sb("e1", [P, 2, CW]), ph.sb("e2", [P, 2, CW])
        larger, weight = ph.sb("larger", [P, 2, CW]), ph.sb("weight", [P, 3, CW])
        p_hi = [ph.sb(f"p_hi{k}", [P, CW], F32R) for k in range(4)]
        p_lo = [ph.sb(f"p_lo{k}", [P, CW], F32R) for k in range(4)]
        total, inverse = ph.sb("total", [P, 8]), ph.sb("inverse", [P, 8])
        bias_row = ph.sb("bias", [P, heads * c])
        bias_in = ph.sem("bias_in")
        acc = [ph.ps(f"acc{k}", [P, 512]) for k in range(8)]
        fifth_s, e_made, larger_s, weight_s, hi_s, lo_s, used, small, out_s = (ph.sem(x) for x in (
            "fifth", "e_made", "larger", "weight", "hi", "lo", "used", "small", "out"))
        shift_in = [ph.sem(f"shift_in{k}") for k in range(2)]
        counts_in = [ph.sem(f"counts_in{k}") for k in range(4)]
        steps = [(h, i, t0, nt, s) for h in range(heads) for i, (t0, nt) in enumerate(chunks) for s in range(NT)]

        with nc.Block() as block:
            @block.sync
            def _(sp):
                sp.dma_start(bias_row[:, :], bias.partition_broadcast(P)).then_inc(bias_in, 16)
                for n, (h, i, t0, nt, s) in enumerate(steps):
                    if i == 0 and s == 0:
                        if h >= 2:
                            sp.wait_ge(e_made, (h - 1) * NC * NT)
                        for k in range(2):
                            sp.dma_start(shift[:, h % 2, k, :], shift_dram[k, h].partition_broadcast(P))\
                                .then_inc(shift_in[h % 2], 16)
                    if n >= 4:
                        sp.wait_ge(weight_s, n - 3)
                    sp.dma_start(counts[:, n % 4, 0:nt * P],
                                 ctot_dram[s * P:(s + 1) * P, t0 * P:(t0 + nt) * P]).then_inc(counts_in[n % 4], 16)

            @block.scalar
            def _(act):
                act.wait_ge(fifth_s, 1)

                def first_part(n):
                    nt = steps[n][3]
                    act.wait_ge(weight_s, n + 1)
                    if n >= 4:
                        act.wait_ge(used, n - 3)
                    act.activation(p_hi[n % 4][:, 0:nt * P], weight[:, n % 3, 0:nt * P], ACT.Copy).then_inc(hi_s, 1)
                for n, (h, i, t0, nt, s) in enumerate(steps):
                    if i == 0 and s == 0:
                        act.wait_ge(shift_in[h % 2], (h // 2 + 1) * 32)
                    if n >= 2:
                        act.wait_ge(larger_s, n - 1)
                    at = slice(t0 * P, (t0 + nt) * P)
                    act.activation(e1[:, n % 2, 0:nt * P], shift[:, h % 2, 0, at], ACT.Exp, bias=cols[:, s, h:h + 1])
                    act.activation(e2[:, n % 2, 0:nt * P], shift[:, h % 2, 1, at], ACT.Exp,
                                   bias=source_fifth[:, s, h:h + 1]).then_inc(e_made, 1)
                    if n:
                        first_part(n - 1)
                first_part(len(steps) - 1)

            @block.vector
            def _(v):
                v.tensor_scalar(source_fifth[:, :, :], cols[:, :, 0:heads], 0.2, None, ALU.mult).then_inc(fifth_s, 1)

                def second_part(n):
                    nt = steps[n][3]
                    v.wait_ge(hi_s, n + 1)
                    v.tensor_tensor(p_lo[n % 4][:, 0:nt * P], weight[:, n % 3, 0:nt * P],
                                    p_hi[n % 4][:, 0:nt * P].bitcast(F32), ALU.subtract).then_inc(lo_s, 1)
                small_n = Steps(v, small)
                v.wait_ge(bias_in, 16)

                def finish(g):
                    h, i = g // NC, g % NC
                    t0, nt = chunks[i]
                    v.wait_ge(used, (g + 1) * NT)
                    half = g % 2 * 4
                    for k in range(nt):
                        small_n.done(v.tensor_scalar(total[:, half + k:half + k + 1],
                                                     acc[half + k * B][:, sum_at:sum_at + 1], 1e-16, None, ALU.add))
                    small_n.wait()
                    small_n.done(v.reciprocal(inverse[:, half:half + nt], total[:, half:half + nt]))
                    small_n.wait()
                    for k in range(nt):
                        at = 0
                        for b, (_, w) in enumerate(cut):
                            w -= 2 if b == 0 else 0
                            here = slice(h * c + at, h * c + at + w)
                            last = v.scalar_tensor_tensor(out=out[:, t0 + k, here], in0=acc[half + k * B + b][:, 0:w],
                                                          scalar=inverse[:, half + k:half + k + 1],
                                                          in1=bias_row[:, here], op0=ALU.mult, op1=ALU.add)
                            at += w
                    last.then_inc(out_s, 1)
                for n, (h, i, t0, nt, s) in enumerate(steps):
                    v.wait_ge(e_made, n + 1)
                    v.wait_ge(counts_in[n % 4], (n // 4 + 1) * 16)
                    v.tensor_tensor(larger[:, n % 2, 0:nt * P], e1[:, n % 2, 0:nt * P], e2[:, n % 2, 0:nt * P],
                                    ALU.max).then_inc(larger_s, 1)
                    if n > 1:
                        second_part(n - 2)
                    v.wait_ge(larger_s, n + 1)
                    v.scalar_tensor_tensor(out=weight[:, n % 3, 0:nt * P], in0=larger[:, n % 2, 0:nt * P], scalar=1.0,
                                           in1=counts[:, n % 4, 0:nt * P], op0=ALU.min, op1=ALU.mult)\
                        .then_inc(weight_s, 1)
                    if s == 5 and n > 5:
                        finish(n // NT - 1)
                second_part(len(steps) - 2)
                second_part(len(steps) - 1)
                finish(heads * NC - 1)

            @block.tensor
            def _(pe):
                x = (xl_hi, xl_lo)
                for n, (h, i, t0, nt, s) in enumerate(steps):
                    g = n // NT
                    pe.wait_ge(lo_s, n + 1)
                    if s == 0 and g >= 2:
                        pe.wait_ge(out_s, g - 1)
                    for k in range(nt):
                        for b, (at, w) in enumerate(cut):
                            at += h * (c + 2)
                            for pa, xb in ((p_hi, 0), (p_hi, 1), (p_lo, 0)):
                                last = pe.matmul(acc[g % 2 * 4 + k * B + b][:, 0:w],
                                                 pa[n % 4][:, k * P:(k + 1) * P], x[xb][:, s, at:at + w],
                                                 start=s == 0 and pa is p_hi and xb == 0,
                                                 stop=s == NT - 1 and pa is p_lo)
                    last.then_inc(used, 1)


def layer_norm_phase(nc, name, rows, width, gain, shift, relu, others, more):
    with Phase(nc, name) as ph:
        pieces = width // 256
        vec = ph.sb("vec", [P, 3, width])
        stats = ph.sb("stats", [P, NT, pieces, 6])
        moments = ph.sb("moments", [P, NT, 2])
        eps, dev, inv, less = ph.sb("eps", [P, 1]), ph.sb("dev", [P, NT]), ph.sb("inv", [P, NT]), ph.sb("less", [P, NT])
        other = ph.sb("other", [P, 3, len(others), width])
        loaded, steps_s, dev_made, normed, tile_done = (ph.sem(x) for x in (
            "loaded", "steps", "dev_made", "normed", "tile_done"))
        others_summed = ph.sem("others_summed")
        other_in = [ph.sem(f"other_in{k}") for k in range(3)]
        rows_in = (gain, shift, more)
        with nc.Block() as block:
            @block.sync
            def _(sp):
                for k, a in enumerate(rows_in):
                    sp.dma_start(vec[:, k, :], a.partition_broadcast(P)).then_inc(loaded, 16)
                for t in range(NT):
                    if t >= 3:
                        sp.wait_ge(tile_done, t - 2)
                    for k, a in enumerate(others):
                        sp.dma_start(other[:, t % 3, k, :], a[t * P:(t + 1) * P, :]).then_inc(other_in[t % 3], 16)

            @block.gpsimd
            def _(pool):
                pool.wait_ge(loaded, 16 * len(rows_in))
                for t in range(NT):
                    pool.wait_ge(other_in[t % 3], (t // 3 + 1) * 16 * len(others))
                    for k, a in enumerate([vec[:, 2, :], *(other[:, t % 3, i, :] for i in range(1, len(others)))]):
                        if k:
                            pool.wait_ge(others_summed, t * len(others) + k)
                        pool.tensor_tensor(other[:, t % 3, 0, :], other[:, t % 3, 0, :], a, ALU.add)\
                            .then_inc(others_summed, 1)

            @block.scalar
            def _(act):
                act.wait_ge(steps_s, 1 + NT * pieces + NT)
                act.activation(dev[:, :], moments[:, :, 1], ACT.Sqrt, bias=eps[:, 0:1]).then_inc(dev_made, 1)
                act.wait_ge(steps_s, 1 + NT * pieces + NT + 2)
                for t in range(NT):
                    act.activation(rows[:, t, :], rows[:, t, :], ACT.Identity, bias=less[:, t:t + 1],
                                   scale=inv[:, t:t + 1]).then_inc(normed, 1)

            @block.vector
            def _(v):
                s = Steps(v, steps_s)
                s.done(v.memset(eps[:, :], EPS))
                for t in range(NT):
                    for k in range(pieces):
                        s.done(v.bn_stats(stats[:, t, k, :], rows[:, t, k * 256:(k + 1) * 256]))
                s.wait()
                for t in range(NT):
                    s.done(v.bn_aggr(moments[:, t, :], stats[:, t, :, :].rearrange("p a b -> p (a b)")))
                v.wait_ge(dev_made, 1)
                s.done(v.reciprocal(inv[:, :], dev[:, :]))
                s.wait()
                s.done(v.scalar_tensor_tensor(out=less[:, :], in0=moments[:, :, 0], scalar=-1.0, in1=inv[:, :],
                                              op0=ALU.mult, op1=ALU.mult))
                v.wait_ge(loaded, 16 * len(rows_in))
                last = 2
                count = {}

                def step(t, k):
                    r = rows[:, t, :]
                    if k == 0:
                        v.wait_ge(normed, t + 1)
                        i = v.tensor_tensor(r, r, vec[:, 0, :], ALU.mult)
                    else:
                        v.wait_ge(steps_s, count[t, k - 1])
                        if k == 1:
                            i = v.tensor_tensor(r, r, vec[:, 1, :], ALU.add)
                        else:
                            v.wait_ge(others_summed, (t + 1) * len(others))
                            a = other[:, t % 3, 0, :]
                            if relu:
                                i = v.scalar_tensor_tensor(out=r, in0=r, scalar=0.0, in1=a, op0=ALU.max, op1=ALU.add)
                            else:
                                i = v.tensor_tensor(r, r, a, ALU.add)
                    if k == last:
                        i.then_inc(tile_done, 1)
                    else:
                        count[t, k] = s.done(i)
                for t in range(0, NT, 2):
                    for k in range(last + 1):
                        step(t, k)
                        step(t + 1, k)


def ones_phase(nc, name, hi, lo, places):
    with Phase(nc, name) as ph:
        made = ph.sem("made")
        one, zero = ph.sb("one", [P, NT, 2]), ph.sb("zero", [P, NT, 2])
        with nc.Block() as block:
            @block.vector
            def _(v):
                v.memset(one[:, :, :], 1.0).then_inc(made, 1)
                v.memset(zero[:, :, :], 0.0).then_inc(made, 1)
                v.wait_ge(made, 2)
                for at in places:
                    v.tensor_copy(hi[:, :, at:at + 2], one[:, :, :])
                    v.tensor_copy(lo[:, :, at:at + 2], zero[:, :, :]).then_inc(made, 1)


def by_block(w, c0, c1):
    return w[:, c0:c1].rearrange("(k p) n -> p k n", p=P)


def gat_layers(nc, rows, rows_ctx, g, ident, ctot_dram, no_edge_dram):
    def dram(name, shape):
        return nc.dram_tensor(f"gat_{name}", shape, F32, kind="Internal").ap()
    heads, c1 = g["a_src1"].shape
    w1, wide = heads * (c1 + 2), heads * c1
    x2 = dram("x", (NP, D))
    res1, res2 = dram("res1", (NP, wide)), dram("res2", (NP, D))
    kb2 = wide // P
    with ExitStack() as ctx:
        cols = ctx.enter_context(nc.sbuf_tensor("gat_cols", [P, NT, 2 * heads], F32, side="right"))
        cols2 = ctx.enter_context(nc.sbuf_tensor("gat_cols2", [P, NT, 2], F32, side="right"))
        left, right = ExitStack(), ExitStack()
        right_sb = lambda name, shape, dt=F32: right.enter_context(nc.sbuf_tensor(name, shape, dt, side="right"))
        left_sb = lambda name, shape, dt=F32: left.enter_context(nc.sbuf_tensor(name, shape, dt))
        f_hi, f_lo = (right_sb(f"gat_f{k}", [P, KB, NP], F32R) for k in range(2))
        src_rows, shifts = dram("src1", (heads, NP)), dram("shifts1", (2, heads, NP))
        norm_phase(nc, "gat_norm", rows, ident, features=(f_hi, f_lo), keep=x2, after=lambda ph, ready: Logits(
            ph, f_hi, f_lo, KB, g["w1_t"], g["a_src1"], g["a_dst1"], heads, ident, cols, src_rows, ready))
        rows_ctx.close()
        project_phase(nc, "res1", f_hi, f_lo, KB, [
            (by_block(g["Wr1"], j * 256, j * 256 + 256), 256, "dram",
             lambda t, j=j: res1[t * P:(t + 1) * P, j * 256:j * 256 + 256]) for j in range(wide // 256)],
            beside=lambda ph: Maxima(ph, heads, ident, cols, src_rows, no_edge_dram, shifts))
        xl_hi, xl_lo = (left_sb(f"gat_xl{k}", [P, NT, w1], F32R) for k in range(2))
        project_phase(nc, "xl1", f_hi, f_lo, KB, [
            (by_block(g["W1"], j * c1, j * c1 + c1), c1, "parts",
             lambda t, j=j: tuple(x[:, t, j * (c1 + 2):j * (c1 + 2) + c1] for x in (xl_hi, xl_lo)))
            for j in range(heads)])
        ones_phase(nc, "ones1", xl_hi, xl_lo, [j * (c1 + 2) + c1 for j in range(heads)])
        right.close()
        h1 = right_sb("gat_h1", [P, NT, wide])
        aggregate_phase(nc, "agg1", heads, c1, cols, shifts, ctot_dram, xl_hi, xl_lo, h1, g["b1"])
        left.close()
        layer_norm_phase(nc, "ln1", h1, wide, g["g1"], g["be1"], True, [res1], g["br1"])
        f_hi, f_lo = (left_sb(f"gat_g{k}", [P, kb2, NP], F32R) for k in range(2))
        src_rows, shifts = dram("src2", (1, NP)), dram("shifts2", (2, 1, NP))
        turn_phase(nc, "turn1", h1, kb2, ident, f_hi, f_lo, after=lambda ph, ready: Logits(
            ph, f_hi, f_lo, kb2, g["w2_t"], g["a_src2"], g["a_dst2"], 1, ident, cols2, src_rows, ready))
        right.close()
        project_phase(nc, "res2", f_hi, f_lo, kb2, [
            (by_block(g["Wr2"], j * 256, j * 256 + 256), 256, "dram",
             lambda t, j=j: res2[t * P:(t + 1) * P, j * 256:j * 256 + 256]) for j in range(D // 256)],
            beside=lambda ph: Maxima(ph, 1, ident, cols2, src_rows, no_edge_dram, shifts))
        xl_hi, xl_lo = (right_sb(f"gat_xm{k}", [P, NT, D + 2], F32R) for k in range(2))

        def past_ones(c):
            return c + (2 if c >= SUM_AT else 0)
        project_phase(nc, "xl2", f_hi, f_lo, kb2, [
            (by_block(g["W2"], c, c + 256), 256, "parts",
             lambda t, c=c: tuple(x[:, t, past_ones(c):past_ones(c) + 256] for x in (xl_hi, xl_lo)))
            for c in range(0, D, 256)])
        ones_phase(nc, "ones2", xl_hi, xl_lo, [SUM_AT])
        left.close()
        rows_ctx = ExitStack()
        rows = rows_ctx.enter_context(nc.sbuf_tensor("gat_rows", [P, NT, D], F32))
        aggregate_phase(nc, "agg2", 1, D, cols2, shifts, ctot_dram, xl_hi, xl_lo, rows, g["b2"])
        right.close()
        layer_norm_phase(nc, "ln2", rows, D, g["g2"], g["be2"], False, [res2, x2], g["br2"])
        return rows, rows_ctx


NE1, RANK = 8, 16
HEADS, HC = 12, 64
LORA_SCALE = 2.0
assert NE1 * RANK == P and HEADS * HC == D


def route_phase(nc, f_hi, f_lo, w_gate_t, b_gate, a_t, down):
    with Phase(nc, "route") as ph:
        W = NE1 + P
        raw = ph.sb("raw", [P, KB, W])
        w_hi, w_lo = ph.sb("w_hi", [P, KB, W], F32R), ph.sb("w_lo", [P, KB, W], F32R)
        bias = ph.sb("bias", [P, NE1])
        logits, probs, equal, first, rest, second, dispatch = (ph.sb(x, [P, NT, NE1]) for x in (
            "logits", "probs", "equal", "first", "rest", "second", "dispatch"))
        top, total, inverse = (ph.sb(x, [P, NT]) for x in ("top", "total", "inverse"))
        free = ph.sb("free", [P, NE1, NT])
        acc = ph.ps("acc", [P, 4, 512])
        loaded, split, multiplied, steps_s, exp_made = (ph.sem(x) for x in (
            "loaded", "split", "multiplied", "steps", "exp_made"))

        def tile(t, c0, c1):
            return acc[:, t // 3, (t % 3) * W + c0:(t % 3) * W + c1]
        with nc.Block() as block:
            @block.sync
            def _(sp):
                sp.dma_start(raw[:, :, 0:NE1], w_gate_t.rearrange("(k p) n -> p k n", p=P)).then_inc(loaded, 16)
                sp.dma_start(raw[:, :, NE1:W], a_t.rearrange("(k p) n -> p k n", p=P)).then_inc(loaded, 16)
                sp.dma_start(bias[:, :], b_gate.partition_broadcast(P)).then_inc(loaded, 16)

            @block.tensor
            def _(pe):
                pe.wait_ge(split, 2)
                f, w = (f_hi, f_lo), (w_hi, w_lo)
                for t in range(NT):
                    for kb in range(KB):
                        for a, b in ((0, 0), (0, 1), (1, 0)):
                            last = pe.matmul(tile(t, 0, W), f[a][:, kb, t * P:(t + 1) * P], w[b][:, kb, :],
                                             start=t % 3 == 0 and kb == 0 and (a, b) == (0, 0), stop=True,
                                             skip_group_check=True)
                last.then_inc(multiplied, 1)

            @block.scalar
            def _(act):
                act.wait_ge(loaded, 48)
                act.activation(w_hi[:, :, :], raw[:, :, :], ACT.Copy).then_inc(split, 1)
                act.wait_ge(steps_s, NT + 2)
                act.activation(probs[:, :, :], logits[:, :, :], ACT.Exp).then_inc(exp_made, 1)

            @block.vector
            def _(v):
                s = Steps(v, steps_s)

                def by_token(a):
                    return a[:, :].unsqueeze(2).to_broadcast([P, NT, NE1])

                def first_of(values, out):
                    s.done(v.tensor_reduce(top[:, :], values[:, :, :], AXX, ALU.max))
                    s.wait()
                    s.done(v.tensor_tensor(equal[:, :, :], values[:, :, :], by_token(top), ALU.is_equal))
                    s.done(v.memset(free[:, 0, :], 1.0))
                    for e in range(NE1):
                        s.wait()
                        s.done(v.tensor_tensor(out[:, :, e], equal[:, :, e], free[:, e, :], ALU.mult))
                        if e + 1 < NE1:
                            s.wait()
                            s.done(v.tensor_tensor(free[:, e + 1, :], free[:, e, :], out[:, :, e], ALU.subtract))
                    s.wait()
                v.wait_ge(split, 1)
                v.tensor_tensor(w_lo[:, :, :], raw[:, :, :], w_hi[:, :, :].bitcast(F32), ALU.subtract)\
                    .then_inc(split, 1)
                v.wait_ge(multiplied, 1)
                for t in range(NT):
                    s.done(v.tensor_tensor(logits[:, t, :], tile(t, 0, NE1), bias[:, :], ALU.add))
                s.wait()
                s.done(v.tensor_reduce(top[:, :], logits[:, :, :], AXX, ALU.max))
                s.wait()
                s.done(v.tensor_tensor(logits[:, :, :], logits[:, :, :], by_token(top), ALU.subtract))
                v.wait_ge(exp_made, 1)
                s.done(v.tensor_reduce(total[:, :], probs[:, :, :], AXX, ALU.add))
                s.wait()
                s.done(v.reciprocal(inverse[:, :], total[:, :]))
                s.wait()
                s.done(v.tensor_tensor(probs[:, :, :], probs[:, :, :], by_token(inverse), ALU.mult))
                s.wait()
                first_of(probs, first)
                s.done(v.scalar_tensor_tensor(out=rest[:, :, :], in0=first[:, :, :], scalar=-2.0, in1=probs[:, :, :],
                                              op0=ALU.mult, op1=ALU.add))
                s.wait()
                first_of(rest, second)
                s.done(v.tensor_tensor(second[:, :, :], second[:, :, :], first[:, :, :], ALU.add))
                s.wait()
                s.done(v.scalar_tensor_tensor(out=dispatch[:, :, :], in0=second[:, :, :], scalar=LORA_SCALE,
                                              in1=probs[:, :, :], op0=ALU.mult, op1=ALU.mult))
                s.wait()
                for t in range(NT):
                    s.done(v.tensor_tensor(down[:, t, :].rearrange("p (n r) -> p n r", r=RANK),
                                           tile(t, NE1, W).rearrange("p (n r) -> p n r", r=RANK),
                                           dispatch[:, t, :].unsqueeze(2).to_broadcast([P, NE1, RANK]), ALU.mult))


def queries_keys_phase(nc, f_hi, f_lo, w_t, b_lora, b_qkv, qk_dram):
    K7, NC, CW, QB = KB + 1, len(CHUNKS), CHUNKS[0][1] * P, 2 * KB
    with Phase(nc, "qk") as ph:
        raw = ph.sb("raw", [P, 2, K7, P])
        w_hi = [ph.sb(f"w_hi{k}", [P, K7, P], F32R) for k in range(2)]
        w_lo = [ph.sb(f"w_lo{k}", [P, K7, P], F32R) for k in range(2)]
        bias = ph.sb("bias", [P, QB])
        value = ph.sb("value", [P, 2, CW])
        hi, lo = ph.sb("hi", [P, 2, NP], F32R), ph.sb("lo", [P, 2, NP], F32R)
        prod = [ph.ps(f"prod{k}", [P, 512]) for k in range(4)]
        bias_in, w_hi_s, w_lo_s, multiplied, value_s, hi_s, lo_s = (ph.sem(x) for x in (
            "bias_in", "w_hi_made", "w_lo_made", "multiplied", "value", "hi", "lo"))
        raw_in = [ph.sem(f"raw_in{k}") for k in range(2)]
        stored = [ph.sem(f"stored{k}") for k in range(2)]
        with nc.Block() as block:
            @block.sync
            def _(sp):
                def load(j):
                    if j >= 2:
                        sp.wait_ge(w_lo_s, j - 1)
                    sp.dma_start(raw[:, j % 2, 0:KB, :], by_block(w_t, j * P, (j + 1) * P)).then_inc(raw_in[j % 2], 16)
                    sp.dma_start(raw[:, j % 2, KB, :], b_lora[:, j * P:(j + 1) * P]).then_inc(raw_in[j % 2], 16)
                sp.dma_start(bias[:, :], b_qkv[0:QB * P].rearrange("(j p) -> p j", p=P),
                             allow_slow_non_contiguous=True).then_inc(bias_in, 16)
                load(0)
                load(1)
                for j in range(QB):
                    if j + 2 < QB:
                        load(j + 2)
                    sp.wait_ge(lo_s, (j + 1) * NC)
                    rows = slice(j % KB * P, (j % KB + 1) * P)
                    sp.dma_start(qk_dram[j // KB * 2, rows, :], hi[:, j % 2, :].bitcast(F32)).then_inc(stored[j % 2], 16)
                    sp.dma_start(qk_dram[j // KB * 2 + 1, rows, :], lo[:, j % 2, :].bitcast(F32))\
                        .then_inc(stored[j % 2], 16)
                for k in range(2):
                    sp.wait_ge(stored[k], QB // 2 * 32)

            @block.tensor
            def _(pe):
                f, w = (f_hi, f_lo), (w_hi, w_lo)
                for j in range(QB):
                    pe.wait_ge(w_lo_s, j + 1)
                    for c, (t0, nt) in enumerate(CHUNKS):
                        i = j * NC + c
                        if i >= 4:
                            pe.wait_ge(value_s, i - 3)
                        for kb in range(K7):
                            for a, b in ((0, 0), (0, 1), (1, 0)):
                                last = pe.matmul(prod[i % 4][:, 0:nt * P], w[a][j % 2][:, kb, :],
                                                 f[b][:, kb, t0 * P:(t0 + nt) * P],
                                                 start=kb == 0 and (a, b) == (0, 0), stop=kb == K7 - 1 and a == 1)
                        last.then_inc(multiplied, 1)

            @block.scalar
            def _(act):
                def weight(j):
                    act.wait_ge(raw_in[j % 2], (j // 2 + 1) * 32)
                    if j >= 2:
                        act.wait_ge(multiplied, (j - 1) * NC)
                    act.activation(w_hi[j % 2][:, :, :], raw[:, j % 2, :, :], ACT.Copy).then_inc(w_hi_s, 1)
                weight(0)
                for j in range(QB):
                    for c, (t0, nt) in enumerate(CHUNKS):
                        i = j * NC + c
                        if c == 1 and j + 1 < QB:
                            weight(j + 1)
                        act.wait_ge(value_s, i + 1)
                        if c == 0 and j >= 2:
                            act.wait_ge(stored[j % 2], j // 2 * 32)
                        act.activation(hi[:, j % 2, t0 * P:(t0 + nt) * P], value[:, i % 2, 0:nt * P], ACT.Copy)\
                            .then_inc(hi_s, 1)

            @block.vector
            def _(v):
                def weight(j):
                    v.wait_ge(w_hi_s, j + 1)
                    v.tensor_tensor(w_lo[j % 2][:, :, :], raw[:, j % 2, :, :], w_hi[j % 2][:, :, :].bitcast(F32),
                                    ALU.subtract).then_inc(w_lo_s, 1)
                v.wait_ge(bias_in, 16)
                weight(0)

                def second(i):
                    j, c = divmod(i, NC)
                    t0, nt = CHUNKS[c]
                    at = slice(t0 * P, (t0 + nt) * P)
                    v.wait_ge(hi_s, i + 1)
                    v.tensor_tensor(lo[:, j % 2, at], value[:, i % 2, 0:nt * P], hi[:, j % 2, at].bitcast(F32),
                                    ALU.subtract).then_inc(lo_s, 1)
                for j in range(QB):
                    for c, (t0, nt) in enumerate(CHUNKS):
                        i = j * NC + c
                        v.wait_ge(multiplied, i + 1)
                        if i >= 2:
                            v.wait_ge(lo_s, i - 1)
                        v.tensor_scalar(value[:, i % 2, 0:nt * P], prod[i % 4][:, 0:nt * P], bias[:, j:j + 1], None,
                                        ALU.add).then_inc(value_s, 1)
                        if i:
                            second(i - 1)
                        if c == 1 and j + 1 < QB:
                            weight(j + 1)
                second(QB * NC - 1)


def attention_phase(nc, qk_dram, v_hi, v_lo, v_bias, ident, out):
    with Phase(nc, "attn") as ph:
        TR = 2 * NT
        KEYS_AT = [(0, 512), (512, 512), (1024, N - 1024)]
        TURN = [(0, 4), (4, 4), (8, 2)]
        q = [ph.sb(f"q{k}", [P, NP], F32R) for k in range(2)]
        k_twice = [ph.sb(f"k_twice{k}", [P, NP], F32R) for k in range(2)]
        k_lo = [ph.sb(f"k_lo{k}", [HC, NP], F32R) for k in range(2)]
        values = [ph.sb(f"values{k}", [P, NT, 2 * HC], F32R) for k in range(2)]
        low_sums = ph.sb("low_sums", [P, 2, HC])
        bias = ph.sb("bias", [P, D])
        largest = ph.sb("largest", [P, 4, 4])
        least = ph.sb("least", [P, 4, 1])
        sums = ph.sb("sums", [P, 4, 3])
        total, inverse = ph.sb("total", [P, 2]), ph.sb("inverse", [P, 2])
        e = [ph.sb(f"e{k}", [P, NP]) for k in range(2)]
        p_hi = [ph.sb(f"p_hi{k}", [P, NT, P], F32R) for k in range(2)]
        p_lo = [ph.sb(f"p_lo{k}", [P, NT, P], F32R) for k in range(2)]
        seed = ph.sb("seed", [1, 16])
        score = [ph.ps(f"score{k}", [P, 512]) for k in range(4)]
        turned = [ph.ps(f"turned{k}", [P, 4, P]) for k in range(3)]
        acc = ph.ps("acc", [P, 512])
        bias_in, scored, piece_s, least_s, exp_s, turned_s = (ph.sem(x) for x in (
            "bias_in", "scored", "piece", "least", "exp", "turned"))
        hi_s, lo_s, summed, total_s, inverse_s, out_s, cleared = (ph.sem(x) for x in (
            "hi", "lo", "summed", "total", "inverse", "out", "cleared"))
        qk_in = [ph.sem(f"qk_in{k}") for k in range(2)]
        values_in = [ph.sem(f"values_in{k}") for k in range(2)]
        FREE = {"scored": 3 * TR, "exp": 6, "turned": 6, "lo": 6, "summed": TR, "out": 3, "least": 3}

        with nc.Block() as block:
            @block.sync
            def _(sp):
                sp.dma_start(bias[:, :], v_bias.partition_broadcast(P)).then_inc(bias_in, 16)
                with sp.Fori(0, HEADS // 2) as g:
                    for u in range(2):
                        rows = bass.ds((g * 2 + u) * HC, HC)
                        sp.wait_ge(scored, g * (3 * TR) + 3 * NT * (u + 1))
                        for dest, plane_ in ((q[u][0:HC], 0), (q[u][HC:P], 1), (k_twice[u][0:HC], 2),
                                             (k_twice[u][HC:P], 2), (k_lo[u][:, :], 3)):
                            sp.dma_start(dest.bitcast(F32), qk_dram[plane_, rows, :]).then_inc(qk_in[u], 16)
                        sp.wait_ge(summed, g * TR + NT * (u + 1))
                        for k, v in enumerate((v_hi, v_lo)):
                            sp.dma_start(values[u][:, :, k * HC:(k + 1) * HC].bitcast(F32),
                                         v[:, :, rows].bitcast(F32)).then_inc(values_in[u], 16)

            @block.gpsimd
            def _(pool):
                pool.memset(seed[:, 0:1], 0.0).then_inc(scored, FREE["scored"])
                pool.memset(seed[:, 1:2], 0.0).then_inc(exp_s, FREE["exp"])
                pool.memset(seed[:, 2:3], 0.0).then_inc(turned_s, FREE["turned"])
                pool.memset(seed[:, 3:4], 0.0).then_inc(lo_s, FREE["lo"])
                pool.memset(seed[:, 4:5], 0.0).then_inc(summed, FREE["summed"])
                pool.memset(seed[:, 5:6], 0.0).then_inc(out_s, FREE["out"])
                pool.memset(seed[:, 6:7], 0.0).then_inc(least_s, FREE["least"])
                for k in range(2):
                    pool.memset(e[k][:, N:NP], 0.0).then_inc(cleared, 1)

            @block.tensor
            def _(pe):
                def scores(g, k):
                    n, u, t = g * TR + k, k % TR // NT, k % NT
                    if t == 0:
                        pe.wait_ge(qk_in[u], (g + k // TR) * 80 + 80)
                    at = slice(t * P, (t + 1) * P)
                    for b, (k0, w) in enumerate(KEYS_AT):
                        bank = score[(3 * k + b) % 4]
                        pe.wait_ge(exp_s, n * 3 + b - 3 + FREE["exp"])
                        pe.matmul(bank[:, 0:w], q[u][:, at], k_twice[u][:, k0:k0 + w], start=True, stop=False)
                        pe.matmul(bank[:, 0:w], q[u][0:HC, at], k_lo[u][:, k0:k0 + w], start=False, stop=True)\
                            .then_inc(scored, 1)

                def turn(g, k):
                    n = g * TR + k
                    pe.wait_ge(exp_s, n * 3 + 3 + FREE["exp"])
                    for b, (s0, ns) in enumerate(TURN):
                        pe.wait_ge(lo_s, n * 3 + b - 2 + FREE["lo"])
                        for s in range(ns):
                            last = pe.transpose(turned[b][:, s, :], e[k % 2][:, (s0 + s) * P:(s0 + s + 1) * P],
                                                ident[:, :])
                        last.then_inc(turned_s, 1)

                def products(g, k):
                    n, u = g * TR + k, k % TR // NT
                    if k % NT == 0:
                        pe.wait_ge(values_in[u], g * 32 + 32)
                    pe.wait_ge(lo_s, n * 3 + 3 + FREE["lo"])
                    pe.wait_ge(out_s, n + FREE["out"])
                    for s in range(NT):
                        pe.matmul(acc[:, 0:2 * HC], p_hi[k % 2][:, s, :], values[u][:, s, :], start=s == 0,
                                  stop=False, skip_group_check=True)
                        last = pe.matmul(acc[:, 0:HC], p_lo[k % 2][:, s, :], values[u][:, s, 0:HC], start=False,
                                         stop=True, skip_group_check=True)
                    last.then_inc(summed, 1)

                def round_(g, first=False, last=False):
                    for k in range(TR):
                        turn(g, k)
                        if k + 2 < TR or not last:
                            scores(g, k + 2)
                        if k or not first:
                            products(g, k - 1)
                    if last:
                        products(g, TR - 1)
                pe.wait_ge(cleared, 2)
                scores(0, 0)
                scores(0, 1)
                round_(0, first=True)
                with pe.Fori(1, HEADS // 2 - 1) as g:
                    round_(g)
                round_(HEADS // 2 - 1, last=True)

            @block.scalar
            def _(act):
                def exponentials(g, k):
                    n = g * TR + k
                    act.wait_ge(least_s, n + 1 + FREE["least"])
                    act.wait_ge(turned_s, n * 3 - 3 + FREE["turned"])
                    act.wait_ge(out_s, n - 3 + FREE["out"])
                    for b, (k0, w) in enumerate(KEYS_AT):
                        act.activation(e[k % 2][:, k0:k0 + w], score[(3 * k + b) % 4][:, 0:w], ACT.Exp,
                                       bias=least[:, k % 4, :], scale=HC ** -0.5,
                                       accum_out=sums[:, k % 4, b:b + 1]).then_inc(exp_s, 1)

                def first_parts(g, k):
                    n = g * TR + k
                    act.wait_ge(summed, n - 1 + FREE["summed"])
                    for b, (s0, ns) in enumerate(TURN):
                        act.wait_ge(turned_s, n * 3 + b + 1 + FREE["turned"])
                        act.activation(p_hi[k % 2][:, s0:s0 + ns, :], turned[b][:, 0:ns, :], ACT.Copy)\
                            .then_inc(hi_s, 1)

                def round_(g, more):
                    for k in range(TR):
                        if k + 1 < TR or more:
                            exponentials(g, k + 1)
                        first_parts(g, k)
                act.wait_ge(cleared, 2)
                exponentials(0, 0)
                with act.Fori(0, HEADS // 2 - 1) as g:
                    round_(g, True)
                round_(HEADS // 2 - 1, False)

            @block.vector
            def _(v):
                def largest_of(g, k, b):
                    n, (k0, w) = g * TR + k, KEYS_AT[b]
                    if b == 0:
                        v.wait_ge(exp_s, n * 3 - 6 + FREE["exp"])
                    v.wait_ge(scored, n * 3 + b + 1 + FREE["scored"])
                    v.tensor_reduce(largest[:, k % 4, b:b + 1], score[(3 * k + b) % 4][:, 0:w], AXX, ALU.max)\
                        .then_inc(piece_s, 1)

                def largest_of_all(g, k):
                    n = g * TR + k
                    v.wait_ge(piece_s, n * 4 + 3)
                    v.tensor_reduce(largest[:, k % 4, 3:4], largest[:, k % 4, 0:3], AXX, ALU.max)\
                        .then_inc(piece_s, 1)

                def least_exponent(g, k):
                    n = g * TR + k
                    v.wait_ge(piece_s, n * 4 + 4)
                    v.tensor_scalar(least[:, k % 4, :], largest[:, k % 4, 3:4], -HC ** -0.5, None, ALU.mult)\
                        .then_inc(least_s, 1)

                def second_part(g, k, b):
                    n, (s0, ns) = g * TR + k, TURN[b]
                    v.wait_ge(hi_s, n * 3 + b + 1)
                    v.tensor_tensor(p_lo[k % 2][:, s0:s0 + ns, :], turned[b][:, 0:ns, :],
                                    p_hi[k % 2][:, s0:s0 + ns, :].bitcast(F32), ALU.subtract).then_inc(lo_s, 1)

                def sum_total(g, k):
                    n = g * TR + k
                    v.wait_ge(exp_s, n * 3 + 3 + FREE["exp"])
                    v.wait_ge(out_s, n - 1 + FREE["out"])
                    v.tensor_reduce(total[:, k % 2:k % 2 + 1], sums[:, k % 4, :], AXX, ALU.add).then_inc(total_s, 1)

                def invert(g, k):
                    n = g * TR + k
                    v.wait_ge(total_s, n + 1)
                    v.reciprocal(inverse[:, k % 2:k % 2 + 1], total[:, k % 2:k % 2 + 1]).then_inc(inverse_s, 1)

                def add_low_sums(g, k):
                    n, h = g * TR + k, g * 2 + k // NT
                    at = bass.ds(h * HC, HC)
                    v.wait_ge(inverse_s, 2 * n + 1)
                    v.wait_ge(summed, n + 1 + FREE["summed"])
                    v.scalar_tensor_tensor(out=low_sums[:, k % 2, :], in0=acc[:, HC:2 * HC],
                                           scalar=inverse[:, k % 2:k % 2 + 1], in1=bias[:, at],
                                           op0=ALU.mult, op1=ALU.add).then_inc(inverse_s, 1)

                def output(g, k):
                    n, h = g * TR + k, g * 2 + k // NT
                    v.wait_ge(inverse_s, 2 * n + 2)
                    v.scalar_tensor_tensor(out=out[:, k % NT, bass.ds(h * HC, HC)], in0=acc[:, 0:HC],
                                           scalar=inverse[:, k % 2:k % 2 + 1], in1=low_sums[:, k % 2, :],
                                           op0=ALU.mult, op1=ALU.add).then_inc(out_s, 1)

                def step(g, k, find, split, finish):
                    def part(tile, work, *args):
                        if tile is not None:
                            work(g, tile, *args)
                    part(find, largest_of, 0)
                    part(finish, sum_total)
                    part(find, largest_of, 1)
                    part(finish, invert)
                    part(find, largest_of, 2)
                    part(split, second_part, 0)
                    part(find, largest_of_all)
                    part(split, second_part, 1)
                    part(find, least_exponent)
                    part(finish, add_low_sums)
                    part(split, second_part, 2)
                    part(finish, output)

                def round_(g, first=False, last=False):
                    for k in range(TR):
                        step(g, k, k + 2 if k + 2 < TR or not last else None, k,
                             k - 1 if k or not first else None)
                    if last:
                        step(g, TR, None, None, TR - 1)
                v.wait_ge(bias_in, 16)
                step(0, 0, 0, None, None)
                step(0, 0, 1, None, None)
                round_(0, first=True)
                with v.Fori(1, HEADS // 2 - 1) as g:
                    round_(g)
                round_(HEADS // 2 - 1, last=True)


def attention_layer(nc, rows, rows_ctx, w_qkv_t, b_qkv, w_gate_t, b_gate, a_t, b_lora, w_proj_t, b_proj, ident, out):
    x3 = nc.dram_tensor("attn_x", (NP, D), F32, kind="Internal").ap()
    qk_dram = nc.dram_tensor("attn_qk", (4, D, NP), F32, kind="Internal").ap()
    left, right = ExitStack(), ExitStack()
    right_sb = lambda name, shape, dt=F32: right.enter_context(nc.sbuf_tensor(name, shape, dt, side="right"))
    left_sb = lambda name, shape, dt=F32: left.enter_context(nc.sbuf_tensor(name, shape, dt))
    f_hi, f_lo = (right_sb(f"attn_f{k}", [P, KB + 1, NP], F32R) for k in range(2))
    norm_phase(nc, "attn_norm", rows, ident, features=(f_hi, f_lo), keep=x3)
    rows_ctx.close()
    with nc.sbuf_tensor("attn_down", [P, NT, P], F32) as down:
        route_phase(nc, f_hi, f_lo, w_gate_t, b_gate, a_t, down)
        turn_phase(nc, "turn_down", down, 1, ident, f_hi, f_lo, at=KB)
    queries_keys_phase(nc, f_hi, f_lo, w_qkv_t, b_lora, b_qkv, qk_dram)
    v_hi, v_lo = (left_sb(f"attn_v{k}", [P, NT, D], F32R) for k in range(2))
    project_phase(nc, "values", f_hi, f_lo, KB + 1, [
        ([(by_block(w_qkv_t, 2 * D + c0, 2 * D + c0 + 256), 0, KB),
          (b_lora[:, 2 * D + c0:2 * D + c0 + 256].rearrange("(k p) n -> p k n", p=P), KB, KB + 1)], 256, "parts",
         lambda t, c0=c0: tuple(x[:, t, c0:c0 + 256] for x in (v_hi, v_lo))) for c0 in range(0, D, 256)])
    right.close()
    attended = right_sb("attended", [P, NT, D])
    attention_phase(nc, qk_dram, v_hi, v_lo, b_qkv[2 * D:3 * D], ident, attended)
    left.close()
    g_hi, g_lo = (left_sb(f"attn_g{k}", [P, KB, NP], F32R) for k in range(2))
    rows = right_sb("attn_rows", [P, NT, D])
    turn_phase(nc, "turn_attended", attended, KB, ident, g_hi, g_lo, load=(rows, x3))
    project_phase(nc, "proj", g_hi, g_lo, KB, [
        (by_block(w_proj_t, c0, c0 + HD), HD, "add", lambda t, c0=c0: rows[:, t, c0:c0 + HD])
        for c0 in range(0, D, HD)], finish=(rows, b_proj, out))
    left.close()
    right.close()


def identity_phase(nc, ident, ident_r):
    with Phase(nc, "identity") as ph:
        made = ph.sem("made")
        ones = ph.sb("ones", [P, P])
        with nc.Block() as block:
            @block.gpsimd
            def _(pool):
                pool.memset(ones[:, :], 1.0).then_inc(made, 1)
                pool.wait_ge(made, 1)
                pool.affine_select(out=ident[:, :], in_=ones[:, :], pattern=[[-1, P]], compare_op=ALU.is_equal,
                                   fill=0.0, base=0, channel_multiplier=1).then_inc(made, 1)

            @block.vector
            def _(v):
                v.wait_ge(made, 2)
                v.tensor_copy(ident_r[:, :], ident[:, :])


def build(nc, a, out):
    def dram(name, shape):
        return nc.dram_tensor(name, shape, F32, kind="Internal").ap()
    edge_dram, c_dram = dram("edge_records", (EP * 4,)), dram("edge_counts", (2 * PLANES, NP, NP))
    counts, inv_dram = dram("in_degrees", (PLANES, NP)), dram("inverse_degrees", (R, NP))
    ctot_dram, no_edge_dram = c_dram[plane(R, 0)], dram("no_edge", (NP, NP))
    with ExitStack() as ctx:
        sb = lambda c, name, shape, dt=F32: c.enter_context(nc.sbuf_tensor(name, shape, dt))
        ident, ident_r = sb(ctx, "ident", [P, P]), sb(ctx, "ident_r", [P, P], F32R)
        flag = sb(ctx, "flag", [1, 1], I32)
        pool_loads = [ctx.enter_context(nc.semaphore(f"pool_load{k}")) for k in range(8)]
        identity_phase(nc, ident, ident_r)
        with nc.sbuf_tensor("starts", [1, BLOCKS], I32) as starts:
            edges_phase(nc, a["src"], a["dst"], a["edge_type_8"], edge_dram, starts, flag)
            adjacency_phase(nc, edge_dram, starts, flag, c_dram, counts)
        whole_adjacency_phase(nc, edge_dram, flag, c_dram, counts)
        inverses_phase(nc, counts, inv_dram)
        loops_phase(nc, ident, ctot_dram, no_edge_dram)
        add_low_phase(nc, flag, c_dram, ctot_dram)
        rows_ctx = ExitStack()
        rows = sb(rows_ctx, "rows", [P, NT, D])
        with ExitStack() as parts:
            t_hi, t_lo = (sb(parts, f"x_part{k}", [P, NT, D], F32R) for k in range(2))
            norm_phase(nc, "norm1", rows, ident, tokens=(t_hi, t_lo), load=a["x"])
            rgcn_phase(nc, "rgcn1", t_hi, t_lo, rows, a["L0_gnn_W1"], a["L0_gnn_root1"], c_dram, inv_dram, ident_r, flag,
                       pool_loads[0:4], base=(None, a["L0_gnn_b1"]))
            relu_phase(nc, "relu", rows, t_hi, t_lo)
            rgcn_phase(nc, "rgcn2", t_hi, t_lo, rows, a["L0_gnn_W2"], a["L0_gnn_root2"], c_dram, inv_dram, ident_r, flag,
                       pool_loads[4:8], base=(a["x"], a["L0_gnn_b2"]))
        with ExitStack() as parts:
            f_hi, f_lo = (sb(parts, f"f_part{k}", [P, KB, NP], F32R) for k in range(2))
            norm_phase(nc, "norm2", rows, ident, features=(f_hi, f_lo))
            experts_phase(nc, f_hi, f_lo, rows, *(a[f"L0_ffn_{k}"] for k in ("Wg", "bg", "W1", "b1", "W2", "b2")), ident)
        gat = {name[len("L1_gnn_"):]: v for name, v in a.items() if name.startswith("L1_gnn_")}
        gat["w1_t"], gat["w2_t"] = a["gat_w1_t"], a["gat_w2_t"]
        rows, rows_ctx = gat_layers(nc, rows, rows_ctx, gat, ident, ctot_dram, no_edge_dram)
        attention_layer(nc, rows, rows_ctx, a["w_qkv_t"], a["L1_ffn_b_qkv"], a["w_gate_t"], a["L1_ffn_b_gate"],
                        a["a_t"], a["b_lora_t"], a["w_proj_t"], a["L1_ffn_b_proj"], ident, out)


def kernel(**inputs):
    import numpy as np
    import concourse.bacc as bacc
    from concourse.bass_utils import run_bass_kernel_spmd

    arrays = {name: np.asarray(v) for name, v in inputs.items()}
    arrays["w_qkv_t"] = arrays.pop("L1_ffn_W_qkv").T
    arrays["w_proj_t"] = arrays.pop("L1_ffn_W_proj").T
    arrays["w_gate_t"] = arrays.pop("L1_ffn_W_gate").T
    arrays["a_t"] = arrays.pop("L1_ffn_A").reshape(NE1 * RANK, D).T
    arrays["b_lora_t"] = arrays.pop("L1_ffn_B_lora").transpose(0, 2, 1).reshape(NE1 * RANK, 3 * D)
    arrays["gat_w1_t"], arrays["gat_w2_t"] = arrays["L1_gnn_W1"].T, arrays["L1_gnn_W2"].T
    arrays = {name: np.ascontiguousarray(v) for name, v in arrays.items()}
    nc = bacc.Bacc("TRN2", target_bir_lowering=False, num_devices=1)
    a = {name: nc.dram_tensor(name, v.shape, mybir.dt.from_np(v.dtype), kind="ExternalInput").ap()
         for name, v in arrays.items()}
    out = nc.dram_tensor("out", (N, D), F32, kind="ExternalOutput").ap()
    build(nc, a, out)
    return run_bass_kernel_spmd(nc, [arrays], core_ids=[0]).results[0]["out"]
```
